# Optimizing a Trainium2 kernel written in Bass

```python
import numpy as np
import jax
import jax.numpy as jnp

def _softmax(x, axis=-1):
    return jax.nn.softmax(x, axis=axis)

def _gelu(x):
    return jax.nn.gelu(x, approximate=True)

def _silu(x):
    return jax.nn.silu(x)

def _sigmoid(x):
    return jax.nn.sigmoid(x)

def _layernorm(x, axis=-1, eps=1e-05):
    m = jnp.mean(x, axis=axis, keepdims=True)
    v = jnp.var(x, axis=axis, keepdims=True)
    return (x - m) / jnp.sqrt(v + eps)

def _scatter_add(tgt, idx, src, axis=0):
    return tgt.at[idx].add(src)

def _segment_sum(src, seg, n):
    return jax.ops.segment_sum(src, seg, n)
kernel_name = 'mk_sandwich_d2_jaxref_r8_1e5724'

def setup_inputs(seed: int=0):
    np.random.seed(seed)
    _w = jnp.asarray

    def _L0_attn_setup():
        import jax, jax.numpy as jnp
        import numpy as np
        D_MODEL = 256
        key = jax.random.key(seed)
        kx, kw, kb = jax.random.split(key, 3)
        B, T, D = (4, 512, D_MODEL)
        x = jax.random.normal(kx, (B, T, D), dtype=jnp.float32)
        scale = 1.0 / np.sqrt(D)
        W = jax.random.uniform(kw, (D, 3 * D), dtype=jnp.float32, minval=-scale, maxval=scale)
        b = jax.random.uniform(kb, (3 * D,), dtype=jnp.float32, minval=-scale, maxval=scale)
        return {'x': x, 'W': W, 'b': b}
    _L0_attn_in = _L0_attn_setup()

    def _L0_ffn_setup():
        import jax, jax.numpy as jnp
        import numpy as np
        BLOCK_SIZE = 32
        HIDDEN_SIZE = 256
        MLP_DIM = 2048
        NVFP4_LUT = jnp.array([0.0, 0.5, 1.0, 1.5, 2.0, 3.0, 4.0, 6.0, 0.0, -0.5, -1.0, -1.5, -2.0, -3.0, -4.0, -6.0], dtype=jnp.float32)

        def dequant_nvfp4(W_packed, scales, block=BLOCK_SIZE):
            N = W_packed.shape[0]
            low = W_packed & 15
            high = W_packed >> 4 & 15
            idx = jnp.stack([low, high], axis=-1).reshape(N, -1)
            vals = NVFP4_LUT[idx]
            K = vals.shape[1]
            vals = vals.reshape(N, K // block, block) * scales[:, :, None]
            return vals.reshape(N, K)
        key = jax.random.key(seed)
        ks = jax.random.split(key, 7)
        x = jax.random.normal(ks[0], (4, 32, HIDDEN_SIZE), dtype=jnp.float32)
        gate_W_packed = jax.random.randint(ks[1], (MLP_DIM, HIDDEN_SIZE // 2), 0, 32, dtype=jnp.int32)
        gate_scales = jax.random.uniform(ks[2], (MLP_DIM, HIDDEN_SIZE // BLOCK_SIZE), dtype=jnp.float32) * 0.1 + 0.001
        up_W_packed = jax.random.randint(ks[3], (MLP_DIM, HIDDEN_SIZE // 2), 0, 32, dtype=jnp.int32)
        up_scales = jax.random.uniform(ks[4], (MLP_DIM, HIDDEN_SIZE // BLOCK_SIZE), dtype=jnp.float32) * 0.1 + 0.001
        down_W_packed = jax.random.randint(ks[5], (HIDDEN_SIZE, MLP_DIM // 2), 0, 32, dtype=jnp.int32)
        down_scales = jax.random.uniform(ks[6], (HIDDEN_SIZE, MLP_DIM // BLOCK_SIZE), dtype=jnp.float32) * 0.1 + 0.001
        return {'x': x, 'gate_W_packed': gate_W_packed, 'gate_scales': gate_scales, 'up_W_packed': up_W_packed, 'up_scales': up_scales, 'down_W_packed': down_W_packed, 'down_scales': down_scales}
    _L0_ffn_in = _L0_ffn_setup()

    def _L1_attn_setup():
        import jax, jax.numpy as jnp
        import numpy as np
        import math
        EMB = 256
        HEADS = 16
        HEAD_DIM = EMB // HEADS
        SCALE = math.sqrt(HEAD_DIM)

        def srms_norm(x, eps_min=1e-12):
            d = x.shape[-1]
            xf = x.astype(jnp.float32)
            norm = jnp.linalg.norm(xf * (1.0 / math.sqrt(d)), axis=-1, keepdims=True)
            norm = jnp.maximum(norm, eps_min)
            return (xf / norm).astype(x.dtype)
        key = jax.random.key(seed)
        ks = jax.random.split(key, 6)
        x = jax.random.normal(ks[0], (4, 512, EMB), dtype=jnp.float32)
        std = 1.0 / math.sqrt(EMB)
        Wq = jax.random.normal(ks[1], (EMB, EMB), dtype=jnp.float32) * std
        Wk = jax.random.normal(ks[2], (EMB, EMB), dtype=jnp.float32) * std
        Wv = jax.random.normal(ks[3], (EMB, EMB), dtype=jnp.float32) * std
        Wu = jax.random.normal(ks[4], (EMB, EMB), dtype=jnp.float32) * std
        Wo = jax.random.normal(ks[5], (EMB, EMB), dtype=jnp.float32) * std
        return {'x': x, 'Wq': Wq, 'Wk': Wk, 'Wv': Wv, 'Wu': Wu, 'Wo': Wo}
    _L1_attn_in = _L1_attn_setup()

    def _L1_ffn_setup():
        import jax, jax.numpy as jnp
        import numpy as np
        E, TOP_K, D, H = (8, 2, 256, 176)
        B, S = (2, 256)
        key = jax.random.key(seed)
        ks = jax.random.split(key, 8)
        x = jax.random.normal(ks[0], (B, S, D), dtype=jnp.float32)
        gate_w = jax.random.normal(ks[1], (E, D), dtype=jnp.float32) * (1.0 / np.sqrt(D))
        gate_b = jax.random.normal(ks[2], (E,), dtype=jnp.float32) * 0.01
        bias = jnp.zeros((E,), dtype=jnp.float32)
        w1 = jax.random.normal(ks[3], (E, H, D), dtype=jnp.float32) * (1.0 / np.sqrt(D))
        b1 = jax.random.normal(ks[4], (E, H), dtype=jnp.float32) * 0.01
        w2 = jax.random.normal(ks[5], (E, D, H), dtype=jnp.float32) * (1.0 / np.sqrt(H))
        b2 = jax.random.normal(ks[6], (E, D), dtype=jnp.float32) * 0.01
        return {'x': x, 'gate_w': gate_w, 'gate_b': gate_b, 'bias': bias, 'w1': w1, 'b1': b1, 'w2': w2, 'b2': b2}
    _L1_ffn_in = _L1_ffn_setup()
    _d = {'L0_attn_x': _L0_attn_in['x'], 'L0_attn_W': _L0_attn_in['W'], 'L0_attn_b': _L0_attn_in['b'], 'L0_ffn_gate_W_packed': _L0_ffn_in['gate_W_packed'], 'L0_ffn_gate_scales': _L0_ffn_in['gate_scales'], 'L0_ffn_up_W_packed': _L0_ffn_in['up_W_packed'], 'L0_ffn_up_scales': _L0_ffn_in['up_scales'], 'L0_ffn_down_W_packed': _L0_ffn_in['down_W_packed'], 'L0_ffn_down_scales': _L0_ffn_in['down_scales'], 'L1_attn_Wq': _L1_attn_in['Wq'], 'L1_attn_Wk': _L1_attn_in['Wk'], 'L1_attn_Wv': _L1_attn_in['Wv'], 'L1_attn_Wu': _L1_attn_in['Wu'], 'L1_attn_Wo': _L1_attn_in['Wo'], 'L1_ffn_gate_w': _L1_ffn_in['gate_w'], 'L1_ffn_gate_b': _L1_ffn_in['gate_b'], 'L1_ffn_bias': _L1_ffn_in['bias'], 'L1_ffn_w1': _L1_ffn_in['w1'], 'L1_ffn_b1': _L1_ffn_in['b1'], 'L1_ffn_w2': _L1_ffn_in['w2'], 'L1_ffn_b2': _L1_ffn_in['b2']}
    _x0 = _d['L0_attn_x']
    _d['L0_attn_x'] = jax.random.normal(jax.random.fold_in(jax.random.key(seed), 1), (4, 1024, 256), dtype=_x0.dtype)
    del _x0
    return _d

def reference(L0_attn_x, L0_attn_W, L0_attn_b, L0_ffn_gate_W_packed, L0_ffn_gate_scales, L0_ffn_up_W_packed, L0_ffn_up_scales, L0_ffn_down_W_packed, L0_ffn_down_scales, L1_attn_Wq, L1_attn_Wk, L1_attn_Wv, L1_attn_Wu, L1_attn_Wo, L1_ffn_gate_w, L1_ffn_gate_b, L1_ffn_bias, L1_ffn_w1, L1_ffn_b1, L1_ffn_w2, L1_ffn_b2):

    def _L0_attn_ref(x, W, b):
        import jax, jax.numpy as jnp
        import numpy as np
        D_MODEL = 256
        qkv = x @ W + b
        q, k, v = jnp.split(qkv, 3, axis=-1)
        qn = q / jnp.linalg.norm(q, axis=1, keepdims=True)
        kn = k / jnp.linalg.norm(k, axis=1, keepdims=True)
        kv = jnp.sum(kn * v, axis=1, keepdims=True)
        return qn * kv

    def _L0_ffn_ref(x, gate_W_packed, gate_scales, up_W_packed, up_scales, down_W_packed, down_scales):
        import jax, jax.numpy as jnp
        import numpy as np
        BLOCK_SIZE = 32
        HIDDEN_SIZE = 256
        MLP_DIM = 2048
        NVFP4_LUT = jnp.array([0.0, 0.5, 1.0, 1.5, 2.0, 3.0, 4.0, 6.0, 0.0, -0.5, -1.0, -1.5, -2.0, -3.0, -4.0, -6.0], dtype=jnp.float32)

        def dequant_nvfp4(W_packed, scales, block=BLOCK_SIZE):
            N = W_packed.shape[0]
            low = W_packed & 15
            high = W_packed >> 4 & 15
            idx = jnp.stack([low, high], axis=-1).reshape(N, -1)
            vals = NVFP4_LUT[idx]
            K = vals.shape[1]
            vals = vals.reshape(N, K // block, block) * scales[:, :, None]
            return vals.reshape(N, K)
        B, S, H = x.shape
        xt = x.reshape(B * S, H)
        Wg = dequant_nvfp4(gate_W_packed, gate_scales)
        Wu = dequant_nvfp4(up_W_packed, up_scales)
        Wd = dequant_nvfp4(down_W_packed, down_scales)
        gate = jnp.einsum('th,nh->tn', xt, Wg)
        up = jnp.einsum('th,nh->tn', xt, Wu)
        gelu = jnp.tanh(0.7978845608028654 * (gate + 0.044715 * gate ** 3)) * gate * 0.5 + gate * 0.5
        inter = gelu * up
        out = jnp.einsum('tn,hn->th', inter, Wd)
        return out.reshape(B, S, H)

    def _L1_attn_ref(x, Wq, Wk, Wv, Wu, Wo):
        import jax, jax.numpy as jnp
        import numpy as np
        import math
        EMB = 256
        HEADS = 16
        HEAD_DIM = EMB // HEADS
        SCALE = math.sqrt(HEAD_DIM)

        def srms_norm(x, eps_min=1e-12):
            d = x.shape[-1]
            xf = x.astype(jnp.float32)
            norm = jnp.linalg.norm(xf * (1.0 / math.sqrt(d)), axis=-1, keepdims=True)
            norm = jnp.maximum(norm, eps_min)
            return (xf / norm).astype(x.dtype)
        B, L, D = x.shape
        H, dh = (HEADS, HEAD_DIM)
        q = (x @ Wq).reshape(B, L, H, dh).transpose(0, 2, 1, 3)
        k = (x @ Wk).reshape(B, L, H, dh).transpose(0, 2, 1, 3)
        v = (x @ Wv).reshape(B, L, H, dh).transpose(0, 2, 1, 3)
        u = (x @ Wu).reshape(B, L, H, dh).transpose(0, 2, 1, 3)
        q = jax.nn.relu(q) / SCALE
        k = jax.nn.relu(k) / SCALE
        u = jax.nn.silu(u)
        kv = jnp.einsum('bhlk,bhlv->bhkv', k, v)
        out = jnp.einsum('bhlk,bhkv->bhlv', q, kv)
        out = srms_norm(out) * u
        out = out.transpose(0, 2, 1, 3).reshape(B, L, D)
        return out @ Wo

    def _L1_ffn_ref(x, gate_w, gate_b, bias, w1, b1, w2, b2):
        import jax, jax.numpy as jnp
        import numpy as np
        E, TOP_K, D, H = (8, 2, 256, 176)
        B, S = (2, 256)
        b, s, d = x.shape
        xf = x.reshape(-1, d)
        scores = xf @ gate_w.T + gate_b + bias
        top_scores, top_idx = jax.lax.top_k(scores, TOP_K)
        gates = jax.nn.softmax(top_scores, axis=-1)
        comb = jnp.sum(jax.nn.one_hot(top_idx, E, dtype=gates.dtype) * gates[..., None], axis=1)
        h = jax.nn.silu(jnp.einsum('td,ehd->teh', xf, w1) + b1)
        y = jnp.einsum('teh,edh->ted', h, w2) + b2
        out = jnp.einsum('ted,te->td', y, comb)
        return out.reshape(b, s, d)
    x = L0_attn_x
    x = x + _layernorm(_L0_attn_ref(_layernorm(x, axis=-1), L0_attn_W, L0_attn_b), axis=-1)
    x = x + _layernorm(_L0_ffn_ref(_layernorm(x, axis=-1), L0_ffn_gate_W_packed, L0_ffn_gate_scales, L0_ffn_up_W_packed, L0_ffn_up_scales, L0_ffn_down_W_packed, L0_ffn_down_scales), axis=-1)
    x = x + _layernorm(_L1_attn_ref(_layernorm(x, axis=-1), L1_attn_Wq, L1_attn_Wk, L1_attn_Wv, L1_attn_Wu, L1_attn_Wo), axis=-1)
    x = x + _layernorm(_L1_ffn_ref(_layernorm(x, axis=-1), L1_ffn_gate_w, L1_ffn_gate_b, L1_ffn_bias, L1_ffn_w1, L1_ffn_b1, L1_ffn_w2, L1_ffn_b2), axis=-1)
    return x

_drawn_inputs = setup_inputs


def setup_inputs(seed=0):
    import zlib

    import numpy as np

    out = dict(_drawn_inputs(seed))
    spreads = {'L1_ffn_bias': (0.0, 0.1)}
    factors = {'L1_ffn_b1': 8.0, 'L1_ffn_b2': 7.287}
    for name, (base, spread) in spreads.items():
        noise = np.random.default_rng([zlib.crc32(name.encode()), seed]).standard_normal(out[name].shape)
        drawn = base * np.exp(spread * noise) if base else spread * noise
        out[name] = jnp.asarray(drawn.astype(out[name].dtype))
    for name, factor in factors.items():
        out[name] = (out[name] * factor).astype(out[name].dtype)
    return out
```

```python
from contextlib import ExitStack

import concourse.bass as bass
from concourse import mybir

ALU = mybir.AluOpType
ACT = mybir.ActivationFunctionType
AX_X = mybir.AxisListType.X
F32 = mybir.dt.float32
F32R = mybir.dt.float32r
I32 = mybir.dt.int32
U32 = mybir.dt.uint32
FP8 = mybir.dt.float8e4

P = 128
D = 256
KC = D // P
B = 4
TOK = 4 * 1024
NT = TOK // P
GT = 4
GW = GT * P
NG = NT // GT
ST = NT // B
MLP = 2048
FC = MLP // P
E, EH = 8, 176
MH = E * EH
MC = MH // P
HD = 16
NH = D // HD
EPS = 1e-5
CREDIT = 1
NEWTON = 3
E_BASE = 2.718281828459045
FP8_UNIT = 64.0

FRONT0 = {"A": 0, "B": NG, "C": 2 * NG, "D": 3 * NG}
UPDATE0 = {"B": 0, "C": 2 * NG, "D": 3 * NG}
G0, U0, G1, U1, O0, O1, T0, T1 = range(8)
DQ = FC


def in_attention_update(g):
    return 0 if isinstance(g, int) and g == 0 else g * 2 - 1


def result_update(phase, g, last_g):
    if phase == "D":
        return g + UPDATE0["D"]
    return 2 * NG - 1 if last_g else g * 2 + 2


def build_program(nc, x_in, wqkv, bqkv, packed, scales, wl1, wo, w1, b1, w2, b2, gate_w, gate_b, gate_bias,
                  ident_in, mask_in, sel_in, out):
    with ExitStack() as ctx:
        def place(name, shape, dt, at):
            at = (at + 31) // 32 * 32
            size = 4
            for n in shape[1:]:
                size *= n
            assert at + size <= nc.sbuf_usable_end, (name, at + size)
            return nc.alloc_sbuf_tensor_at(name, shape, dt, offset=at), at + size

        top = nc.sbuf_base
        x, top = place("x", [P, NT, D], F32, top)
        xn, top = place("xn", [P, GT, D], F32, top)
        xh0, top = place("xh0", [P, KC, GW], F32R, top)
        xh1, top = place("xh1", [P, KC, GW], F32R, top)
        xl0, top = place("xl0", [P, KC, GW], F32R, top)
        xl1, top = place("xl1", [P, KC, GW], F32R, top)
        xh, xl = (xh0, xh1), (xl0, xl1)
        ident, top = place("ident", [P, P], F32, top)
        fstats, top = place("fstats", [P, GT, 6], F32, top)
        fmv, top = place("fmv", [P, GT, 2], F32, top)
        fvar, top = place("fvar", [P, GT], F32, top)
        frstd, top = place("frstd", [P, GT], F32, top)
        ustats, top = place("ustats", [P, GT, 6], F32, top)
        umv, top = place("umv", [P, GT, 2], F32, top)
        uvar, top = place("uvar", [P, GT], F32, top)
        urstd, top = place("urstd", [P, GT], F32, top)
        unm, top = place("unm", [P, GT], F32, top)
        neghalf, top = place("neghalf", [P, 64], F32, top)
        colsum, top = place("colsum", [P, NG, 6], F32, top)
        coltot, top = place("coltot", [P, B, 6], F32, top)
        colrn, top = place("colrn", [P, B, 4], F32, top)
        colc, top = place("colc", [P, B, 2], F32, top)
        bq, top = place("bq", [P, 6], F32, top)
        b1s, region_q = place("b1s", [P, MC], F32, top)
        qT, region_w = place("qT", [P, KC, TOK], F32, region_q)
        wch, at = place("wch", [P, KC, 4 * D], F32R, region_q)
        wcl, at = place("wcl", [P, KC, 4 * D], F32R, at)
        woh, at = place("woh", [P, KC, D], F32R, at)
        wol, at = place("wol", [P, KC, D], F32R, at)
        wcraw, at = place("wcraw", [P, KC, 5 * D], F32, at)
        assert at <= region_w
        sel, at = place("sel", [2 * E, MH], F32, region_q)
        selr, at = place("selr", [2 * E, MH], F32R, at)
        gw, at = place("gw", [P, KC, E], F32, at)
        gwh, at = place("gwh", [P, KC, E], F32R, at)
        gwl, at = place("gwl", [P, KC, E], F32R, at)
        gb, at = place("gb", [P, 2, E], F32, at)
        gbs, at = place("gbs", [P, E], F32, at)
        b2s, at = place("b2s", [2 * E, D], F32, at)
        b2h, at = place("b2h", [2 * E, D], F32R, at)
        b2l, at = place("b2l", [2 * E, D], F32R, at)
        score, at = place("score", [P, GT, E], F32, at)
        best, at = place("best", [P, GT, 8], F32, at)
        besti, at = place("besti", [P, GT, 8], U32, at)
        bestf, at = place("bestf", [P, GT, 8], F32, at)
        iota, at = place("iota", [P, E], F32, at)
        gap, at = place("gap", [P, GT], F32, at)
        ebase, at = place("ebase", [P, GT], F32, at)
        second, at = place("second", [P, GT], F32, at)
        denom, at = place("denom", [P, GT], F32, at)
        gate1, at = place("gate1", [P, GT], F32, at)
        gate2, at = place("gate2", [P, GT], F32, at)
        pick1, at = place("pick1", [P, GT, E], F32, at)
        pick2, at = place("pick2", [P, GT, E], F32, at)
        comb, at = place("comb", [P, GT, 2 * E], F32R, at)
        combT0, at = place("combT0", [2 * E, GW], F32R, at)
        combT1, at = place("combT1", [2 * E, GW], F32R, at)
        combT = (combT0, combT1)
        assert at <= region_w
        wah, at = place("wah", [P, KC, 3 * D], F32R, region_w)
        wal, region_f = place("wal", [P, KC, 3 * D], F32R, at)
        hid0, at = place("hid0", [P, GW], F32, region_w)
        hid1, at = place("hid1", [P, GW], F32, at)
        hh0, at = place("hh0", [P, GW], F32R, at)
        hh1, at = place("hh1", [P, GW], F32R, at)
        hl0, at = place("hl0", [P, GW], F32R, at)
        hl1, at = place("hl1", [P, GW], F32R, at)
        assert at <= region_f
        hid, hh, hl = (hid0, hid1), (hh0, hh1), (hl0, hl1)
        wfh, at = place("wfh", [P, DQ, 3, 2, P], F32R, region_f)
        wfl, region_s = place("wfl", [P, DQ, 3, 2, P], F32R, at)
        waraw, _ = place("waraw", [P, KC, 3 * D], F32, region_s - KC * 3 * D * 4)
        qh, at = place("qh", [P, KC, ST * P], F32R, region_f)
        ql, at = place("ql", [P, KC, ST * P], F32R, at)
        us, at = place("us", [P, NT, D], F32, at)
        kvh0, at = place("kvh0", [P, 2 * D], F32R, at)
        kvh1, at = place("kvh1", [P, 2 * D], F32R, at)
        kvl0, at = place("kvl0", [P, 2 * D], F32R, at)
        kvl1, at = place("kvl1", [P, 2 * D], F32R, at)
        kvh, kvl = (kvh0, kvh1), (kvl0, kvl1)
        obuf, at = place("obuf", [P, ST, D], F32, at)
        sq, at = place("sq", [P, ST, D], F32, at)
        oh, at = place("oh", [P, KC, GW], F32R, at)
        ol, at = place("ol", [P, KC, GW], F32R, at)
        state, at = place("state", [P, KC, P], F32, at)
        stateh, at = place("stateh", [P, KC, P], F32R, at)
        statel, at = place("statel", [P, KC, P], F32R, at)
        mask, at = place("mask", [P, P], F32, at)
        hsum, at = place("hsum", [P, ST * NH], F32, at)
        hrstd, at = place("hrstd", [P, ST * NH], F32, at)
        hwork, at = place("hwork", [P, ST * NH], F32, at)
        assert at <= region_s
        w1h, at = place("w1h", [P, KC, MH], F32R, region_f)
        w1l, at = place("w1l", [P, KC, MH], F32R, at)
        w2h, at = place("w2h", [P, MC, D], F32R, at)
        w2l, at = place("w2l", [P, MC, D], F32R, at)
        w1raw, at = place("w1raw", [P, KC, MH], F32, at)
        w2raw, at = place("w2raw", [P, MC, D], F32, at)
        assert at <= region_s
        pk, at = place("pk", [P, 3, P], I32, region_s)
        sc, at = place("sc", [P, 3, P], F32, at)
        code, at = place("code", [P, 3, P], I32, at)
        field, at = place("field", [P, 3, P], I32, at)
        ksb, at = place("ksb", [P, GW], F32, at)
        weight, at = place("weight", [P, 3, 2, P], F32, at)
        rT, at = place("rT", [P, KC, GW], F32, region_s)
        ry, at = place("ry", [P, GT, D], F32, at)

        ps = ctx.enter_context(nc.psum_tensor("ps", [P, 8, GW], F32))
        tok_banks = ps[:, T0:T1 + 1, :].rearrange("p b (t c) -> p (b t) c", t=2)

        names = ("waited consts x_even x_odd wa_raw pk_in sc_in wc_raw wd_raw out_stored "
                 "half_ready wa_hi wa_lo "
                 "f_stats f_mv f_var f_rstd f_xn f_turned f_hi f_lo "
                 "u_turned u_stats u_mv u_var u_rstd u_nm u_normed u_added u_scaled "
                 "proj k_copied k_done v_done q_done "
                 "dq_f dq_code dq_scale dq_w dq_hi dq_lo "
                 "col_tot col_rn col_c0 col_c "
                 "pre_ready up_ready act_done hid_ready hid_hi hid_lo down_done "
                 "acc_copied "
                 "wc_hi wc_lo c_q c_kv c_u c_qhi c_qlo c_kvhi c_kvlo c_ucopied c_state c_masked c_sthi c_stlo "
                 "c_o c_ocopied c_hsum c_hrstd c_scaled c_gated o_turned o_hi o_lo "
                 "wd_hi wd_lo r_consts r_bias r_scores r_scored r_best r_found r_comb_hi r_chain r_gap r_second "
                 "r_comb r_turned r_copied "
                 ).split()
        S = {n: ctx.enter_context(nc.semaphore(n)) for n in names}
        x_loaded = (S["x_even"], S["x_odd"])
        block = ctx.enter_context(nc.Block())

        def apart(eng):
            eng.sem_inc(S["waited"], 1)

        def sequences(eng, first, last, body):
            with eng.Fori(first, last + 1) as b:
                body(b)

        @block.sync
        def _(sp):
            sp.dma_start(ident[:], ident_in).then_inc(S["consts"], 16)
            sp.dma_start(bq[:], bqkv).then_inc(S["consts"], 16)
            sp.dma_start(b1s[:], b1).then_inc(S["consts"], 16)
            sp.dma_start(x[:, 0:GT, :], x_in[0:GT].rearrange("t p c -> p t c")).then_inc(S["x_even"], 16)
            sp.dma_start(waraw[:], wqkv).then_inc(S["wa_raw"], 16)
            sp.dma_start(x[:, GT:2 * GT, :], x_in[GT:2 * GT].rearrange("t p c -> p t c")).then_inc(S["x_odd"], 16)

            def phase_a(b, last_b=False):
                for half in range(2):
                    g = b * 2 + half
                    if not last_b:
                        sp.wait_ge(x_loaded[half], b * 16 + 16)
                        sp.dma_start(x[:, bass.ds(g * GT + 2 * GT, GT), :],
                                     x_in[bass.ds(g * GT + 2 * GT, GT)].rearrange("t p c -> p t c")) \
                            .then_inc(x_loaded[half], 16)
                    for s in range(2):
                        step = g * 2 + s
                        sp.wait_ge(S["dq_code"], CREDIT + step)
                        sp.dma_start(pk[:], packed[bass.ds(step, 1)].rearrange("o p (m c) -> (o p) m c", m=3)) \
                            .then_inc(S["pk_in"], 16)
                        sp.wait_ge(S["dq_w"], CREDIT + step)
                        rows = scales[bass.ds(step * 8, 8)].unsqueeze(1).to_broadcast([8, 16, 3 * P])
                        sp.dma_start(sc[:].rearrange("p m c -> p (m c)"), rows).then_inc(S["sc_in"], 16)

            sequences(sp, 0, B - 2, phase_a)
            phase_a(B - 1, last_b=True)
            sp.wait_ge(S["u_scaled"], NG)
            sp.dma_start(wcraw[:, :, 0:4 * D], wl1).then_inc(S["wc_raw"], 16)
            sp.dma_start(wcraw[:, :, 4 * D:5 * D], wo).then_inc(S["wc_raw"], 16)
            sp.wait_ge(S["down_done"], NG * FC)
            sp.dma_start(mask[:], mask_in).then_inc(S["consts"], 16)
            sp.wait_ge(S["u_turned"], UPDATE0["D"])
            sp.dma_start(w1raw[:], w1).then_inc(S["wd_raw"], 16)
            sp.dma_start(w2raw[:], w2).then_inc(S["wd_raw"], 16)
            sp.dma_start(sel[:], sel_in).then_inc(S["wd_raw"], 16)
            sp.dma_start(gw[:], gate_w).then_inc(S["wd_raw"], 16)
            sp.dma_start(gb[:, 0, :], gate_b.unsqueeze(0).to_broadcast([P, E])).then_inc(S["wd_raw"], 16)
            sp.dma_start(gb[:, 1, :], gate_bias.unsqueeze(0).to_broadcast([P, E])).then_inc(S["wd_raw"], 16)
            sp.dma_start(b2s[0:E, :], b2).then_inc(S["wd_raw"], 16)
            sp.dma_start(b2s[E:2 * E, :], b2).then_inc(S["wd_raw"], 16)

            def store(b):
                for half in range(2):
                    g = b * 2 + half
                    sp.wait_ge(S["u_added"], g + (UPDATE0["D"] + 1))
                    sp.dma_start(out[bass.ds(g * GT, GT)].rearrange("t p c -> p t c"),
                                 x[:, bass.ds(g * GT, GT), :]).then_inc(S["out_stored"], 16)

            sequences(sp, 0, B - 1, store)
            sp.wait_ge(S["out_stored"], 16 * NG)

        @block.tensor
        def _(pe):
            def product(dst, terms, start=True, stop=True, group_check=True):
                n = len(terms)
                for k, (ah, al, bh, bl) in enumerate(terms):
                    pe.matmul(dst, ah, bl, start=start and k == 0, stop=False, skip_group_check=not group_check)
                    pe.matmul(dst, ah, bh, start=False, stop=False, skip_group_check=not group_check)
                    last = pe.matmul(dst, al, bh, start=False, stop=stop and k == n - 1,
                                     skip_group_check=not group_check)
                return last

            def turn_banks_free(updates, fronts, outputs=0):
                if not (isinstance(updates, int) and updates == 0):
                    pe.wait_ge(S["u_normed"], updates)
                if not (isinstance(fronts, int) and fronts == 0):
                    pe.wait_ge(S["f_lo"], fronts * 2)
                if not (isinstance(outputs, int) and outputs == 0):
                    pe.wait_ge(S["o_lo"], CREDIT + outputs * 2)

            def front(F, updates, outputs=0):
                turn_banks_free(updates, F, outputs)
                pe.wait_ge(S["f_xn"], F + 1)
                for k in range(KC):
                    for t in range(GT):
                        last = pe.transpose(ps[:, T0 + k, t * P:(t + 1) * P], xn[:, t, k * P:(k + 1) * P], ident[:])
                last.then_inc(S["f_turned"], 1)

            def update_turn(fronts, updates):
                for t in range(GT):
                    for k in range(KC):
                        last = pe.transpose(tok_banks[:, t, k * P:(k + 1) * P], rT[:, k, t * P:(t + 1) * P], ident[:])
                last.then_inc(S["u_turned"], 1)

            def front_ready(F):
                pe.wait_ge(S["f_hi"], F * 2 + 2)
                pe.wait_ge(S["f_lo"], F * 2 + 2)

            pe.wait_ge(S["consts"], 48)
            front(0, 0)
            pe.wait_ge(S["wa_hi"], 1)
            pe.wait_ge(S["wa_lo"], 1)

            def phase_a(b, last_b=False):
                for half in range(2):
                    g = b * 2 + half
                    front_ready(g)
                    order = ((2, 0, "k_done"), (4, 1, "v_done"), (3, 2, "k_done"), (5, 3, "v_done"),
                             (0, 4, "q_done"), (1, 5, "q_done"))
                    for n, (m, bank, reader) in enumerate(order):
                        if n in (0, 4):
                            if n == 0:
                                pe.wait_ge(S["k_done"], CREDIT + g * 2)
                                pe.wait_ge(S["v_done"], CREDIT + g * 2)
                            else:
                                pe.wait_ge(S["q_done"], CREDIT + g * 2)
                        cols = slice(m * P, (m + 1) * P)
                        product(ps[:, bank, :], [(wah[:, k, cols], wal[:, k, cols], xh[half][:, k, :], xl[half][:, k, :])
                                                 for k in range(KC)]).then_inc(S["proj"], 1)
                        if n == 3 and not (last_b and half == 1):
                            front(g + 1, 0)

            sequences(pe, 0, B - 2, phase_a)
            phase_a(B - 1, last_b=True)

            def hidden_layer(phase, chunks, pre, down, slot_work):
                n0 = 0 if phase == "B" else NG * FC
                def pre_chunk(half, c):
                    pre(half, c, (half * chunks + c) % 2 * 2)

                def down_chunk(g, half, c):
                    n = g * chunks + (c + n0)
                    pe.wait_ge(S["hid_hi"], n + 1)
                    pe.wait_ge(S["hid_lo"], n + 1)
                    if c == 0:
                        pe.wait_ge(S["acc_copied"], g * 2 + (0 if phase == "B" else 2 * NG))
                    down(half, c, (half * chunks + c) % 2).then_inc(S["down_done"], 1)

                def start_group(g, half, first=False):
                    if first:
                        pre_chunk(half, 0)
                        pre_chunk(half, 1)
                    down_chunk(g, half, 0)
                    pre_chunk(half, 2)
                    down_chunk(g, half, 1)

                def body(b, last_b=False):
                    for half in range(2):
                        g = b * 2 + half
                        last_g = last_b and half == 1
                        for c in range(2, chunks):
                            if c + 1 < chunks:
                                pre_chunk(half, c + 1)
                            elif not last_g:
                                front_ready(g + (FRONT0[phase] + 1))
                                pre_chunk(1 - half, 0)
                            down_chunk(g, half, c)
                            slot_work(g, half, c, last_g)
                        if not last_g:
                            pre_chunk(1 - half, 1)
                            start_group(g + 1, 1 - half)
                        upd = result_update(phase, g, last_g)
                        fronts = g + (FRONT0[phase] + 2)
                        turn_banks_free(upd, fronts - 1 if phase == "D" and last_g else fronts)
                        pe.wait_ge(S["acc_copied"], g * 2 + (2 if phase == "B" else 2 * NG + 2))
                        update_turn(fronts, upd)

                return start_group, body

            def mlp_pre(half, c, bank):
                for m, dst, done in ((0, bank, "pre_ready"), (1, bank + 1, "up_ready")):
                    product(ps[:, dst, :], [(wfh[:, c, m, k, :], wfl[:, c, m, k, :], xh[half][:, k, :], xl[half][:, k, :])
                                            for k in range(KC)]).then_inc(S[done], 1)

            def mlp_down(half, c, slot):
                for m in range(KC):
                    step = c // 2 * 2 + m
                    last = product(ps[:, O0 + m, :], [(wfh[:, step, 2, c % 2, :], wfl[:, step, 2, c % 2, :],
                                                       hh[slot][:], hl[slot][:])], start=c == 0, stop=c == FC - 1)
                return last

            def attention_turn(g):
                n = in_attention_update(g)
                turn_banks_free(n, g + FRONT0["B"])
                pe.wait_ge(S["u_scaled"], g + 1)
                update_turn(g + FRONT0["B"], n)

            def mlp_slot(g, half, c, last_g):
                if c == 4 and not last_g:
                    attention_turn(g + 1)
                if c == 10:
                    front(g + (FRONT0["B"] + 1), 2 * NG - 1 if last_g else g * 2 + 2)

            attention_turn(0)
            front(FRONT0["B"], 1)
            front_ready(FRONT0["B"])
            pe.wait_ge(S["dq_hi"], DQ)
            pe.wait_ge(S["dq_lo"], CREDIT + DQ)
            start, body = hidden_layer("B", FC, mlp_pre, mlp_down, mlp_slot)
            start(0, 0, first=True)
            sequences(pe, 0, B - 2, body)
            body(B - 1, last_b=True)

            def project(b, g, half, updates, outputs, finish=None):
                F = g + FRONT0["C"]
                front_ready(F)
                pe.wait_ge(S["c_ucopied"], g * GT)
                for m in range(KC):
                    cols = slice(m * P, (m + 1) * P)
                    product(ps[:, m, :], [(wch[:, k, cols], wcl[:, k, cols], xh[half][:, k, :], xl[half][:, k, :])
                                          for k in range(KC)]).then_inc(S["c_q"], 1)
                front(F + 1, updates, outputs)

                def kv_u(t):
                    tk = slice(t * P, (t + 1) * P)
                    product(ps[:, 2 + t % 2, :], [(xh[half][:, k, tk], xl[half][:, k, tk], wch[:, k, D:3 * D],
                                                   wcl[:, k, D:3 * D]) for k in range(KC)]).then_inc(S["c_kv"], 1)
                    if t < 2:
                        pe.wait_ge(S["c_qlo"], g * KC + (t + 1))
                    else:
                        pe.wait_ge(S["c_ucopied"], g * GT + (t - 1))
                    product(ps[:, t % 2, 0:D], [(xh[half][:, k, tk], xl[half][:, k, tk], wch[:, k, 3 * D:4 * D],
                                                 wcl[:, k, 3 * D:4 * D]) for k in range(KC)]).then_inc(S["c_u"], 1)

                def accumulate(t):
                    pe.wait_ge(S["c_kvlo"], g * GT + (t + 1))
                    if half == 0 and t == 0:
                        pe.wait_ge(S["c_ocopied"], b * ST)
                    first, final = half == 0 and t == 0, half == 1 and t == GT - 1
                    for m in range(KC):
                        kc, vc = slice(m * P, (m + 1) * P), slice(D + m * P, D + (m + 1) * P)
                        last = product(ps[:, O0, m * P:(m + 1) * P],
                                       [(kvh[t % 2][:, kc], kvl[t % 2][:, kc], kvh[t % 2][:, vc], kvl[t % 2][:, vc])],
                                       start=first and m == 0, stop=final and m == KC - 1, group_check=False)
                    if final:
                        last.then_inc(S["c_state"], 1)

                kv_u(0)
                kv_u(1)
                accumulate(0)
                kv_u(2)
                accumulate(1)
                kv_u(3)
                accumulate(2)
                if finish is not None:
                    output_turn(*finish)
                accumulate(3)
                if finish is not None:
                    output_product(*finish)

            def attend(b):
                pe.wait_ge(S["c_stlo"], b + 1)
                for t in range(ST):
                    pe.wait_ge(S["c_ocopied"], b * ST + max(t - 1, 0))
                    for m in range(KC):
                        tk = slice(t * P, (t + 1) * P)
                        last = product(ps[:, O1 - t % 2, m * P:(m + 1) * P],
                                       [(qh[:, m, tk], ql[:, m, tk], stateh[:, m, :], statel[:, m, :])])
                    last.then_inc(S["c_o"], 1)

            def output_turn(g, fronts):
                turn_banks_free(g + UPDATE0["C"], fronts, g)
                pe.wait_ge(S["c_gated"], g + 1)
                half = g % 2 if isinstance(g, int) else finish_half[0]
                for k in range(KC):
                    for t in range(GT):
                        last = pe.transpose(ps[:, T0 + k, t * P:(t + 1) * P],
                                            obuf[:, half * GT + t, k * P:(k + 1) * P], ident[:])
                last.then_inc(S["o_turned"], 1)

            def output_product(g, fronts):
                pe.wait_ge(S["o_hi"], g * 2 + 2)
                pe.wait_ge(S["o_lo"], CREDIT + g * 2 + 2)
                for t in range(GT):
                    tk = slice(t * P, (t + 1) * P)
                    last = product(tok_banks[:, t, :], [(oh[:, k, tk], ol[:, k, tk], woh[:, k, :], wol[:, k, :])
                                                        for k in range(KC)])
                last.then_inc(S["u_turned"], 1)

            finish_half = [0]
            pe.wait_ge(S["wc_hi"], 2)
            pe.wait_ge(S["wc_lo"], 2)
            project(0, 0, 0, 2 * NG, 0)
            project(0, 1, 1, 2 * NG, 0)
            attend(0)

            def phase_c(b):
                for half in range(2):
                    g = b * 2 + half
                    finish_half[0] = half
                    project(b, g, half, g + (UPDATE0["C"] - 2), g - 2, finish=(g - 2, g + (FRONT0["C"] + 2)))
                attend(b)

            sequences(pe, 1, B - 1, phase_c)
            for g in (NG - 2, NG - 1):
                output_turn(g, FRONT0["D"] + 1)
                output_product(g, FRONT0["D"] + 1)

            def router(F, half, updates):
                turn_banks_free(updates, F + 1, NG)
                front_ready(F)
                for t in range(GT):
                    tk = slice(t * P, (t + 1) * P)
                    last = product(ps[:, T0, t * E:(t + 1) * E], [(xh[half][:, k, tk], xl[half][:, k, tk], gwh[:, k, :],
                                                                   gwl[:, k, :]) for k in range(KC)])
                last.then_inc(S["r_scores"], 1)

            def router_turn(g):
                pe.wait_ge(S["r_comb"], g + 1)
                for t in range(GT):
                    last = pe.transpose(ps[0:2 * E, T1, t * P:(t + 1) * P], comb[:, t, :].bitcast(F32), ident[:])
                last.then_inc(S["r_turned"], 1)

            def expert_pre(half, c, bank):
                cols = slice(c * P, (c + 1) * P)
                product(ps[:, bank, :], [(w1h[:, k, cols], w1l[:, k, cols], xh[half][:, k, :], xl[half][:, k, :])
                                         for k in range(KC)]).then_inc(S["pre_ready"], 1)
                pe.matmul(ps[:, bank + 1, :], selr[:, cols], combT[half][:], start=True, stop=True) \
                    .then_inc(S["up_ready"], 1)

            def expert_down(half, c, slot):
                for m in range(KC):
                    cols = slice(m * P, (m + 1) * P)
                    if c == 0:
                        pe.matmul(ps[:, O0 + m, :], b2l[:, cols], combT[half][:], start=True, stop=False)
                        pe.matmul(ps[:, O0 + m, :], b2h[:, cols], combT[half][:], start=False, stop=False)
                    last = product(ps[:, O0 + m, :], [(w2h[:, c, cols], w2l[:, c, cols], hh[slot][:], hl[slot][:])],
                                   start=False, stop=c == MC - 1)
                return last

            def expert_slot(g, half, c, last_g):
                if last_g:
                    return
                if c == 3:
                    front(g + (FRONT0["D"] + 1), g + UPDATE0["D"], NG)
                if c == 5:
                    router(g + (FRONT0["D"] + 1), 1 - half, g + UPDATE0["D"])
                if c == 8:
                    router_turn(g + 1)
                if c == MC - 2:
                    pe.wait_ge(S["r_copied"], g + 2)

            pe.wait_ge(S["wd_hi"], 5)
            pe.wait_ge(S["wd_lo"], 4)
            router(FRONT0["D"], 0, UPDATE0["D"])
            router_turn(0)
            pe.wait_ge(S["r_copied"], 1)
            start, body = hidden_layer("D", MC, expert_pre, expert_down, expert_slot)
            start(0, 0, first=True)
            sequences(pe, 0, B - 2, body)
            body(B - 1, last_b=True)

        @block.scalar
        def _(act):
            def front(F, half):
                act.wait_ge(S["f_turned"], F + 1)
                for k in range(KC):
                    act.activation(xh[half][:, k, :], ps[:, T0 + k, :], ACT.Copy).then_inc(S["f_hi"], 1)

            def update(n):
                act.wait_ge(S["u_rstd"], n + 1)
                act.wait_ge(S["u_nm"], n + 1)
                act.wait_ge(S["u_added"], n)
                for t in range(GT):
                    last = act.activation(ry[:, t, :], tok_banks[:, t, :], ACT.Identity,
                                          bias=unm[:, t:t + 1], scale=urstd[:, t:t + 1])
                last.then_inc(S["u_normed"], 1)

            act.sem_inc(S["k_done"], CREDIT)
            act.sem_inc(S["q_done"], CREDIT)
            act.preload_act_table(ACT.Copy)
            act.wait_ge(S["wa_raw"], 16)
            act.activation(wah[:], waraw[:], ACT.Copy).then_inc(S["wa_hi"], 1)
            act.wait_ge(S["consts"], 48)
            front(0, 0)

            def phase_a(b, last_b=False):
                for half in range(2):
                    g = b * 2 + half

                    def dequant_hi(s):
                        step = g * 2 + s
                        act.wait_ge(S["dq_w"], CREDIT + step + 1)
                        act.activation(wfh[:, bass.ds(step, 1)].rearrange("p o m n c -> p (o m n c)"),
                                       weight[:].rearrange("p m n c -> p (m n c)"), ACT.Copy) \
                            .then_inc(S["dq_hi"], 1)

                    for m, n in ((0, 1), (1, 3)):
                        act.wait_ge(S["proj"], g * 6 + n)
                        act.wait_ge(S["v_done"], CREDIT + g * 2 + m)
                        act.activation(ksb[:], ps[:, 2 * m, :], ACT.Identity, bias=bq[:, 2 + m:3 + m]) \
                            .then_inc(S["k_copied"], 1)
                        act.activation(ps[:, 2 * m, :], ps[:, 2 * m, :], ACT.Square, bias=bq[:, 2 + m:3 + m],
                                       accum_out=colsum[:, bass.ds(g, 1), m]).then_inc(S["k_done"], 1)
                        if m == 0:
                            dequant_hi(0)
                    if not (last_b and half == 1):
                        front(g + 1, 1 - half)
                    for m in range(KC):
                        act.wait_ge(S["proj"], g * 6 + (5 + m))
                        act.activation(qT[:, m, bass.ds(g * GW, GW)], ps[:, 4 + m, :], ACT.Identity,
                                       bias=bq[:, m:m + 1])
                        act.activation(ps[:, 4 + m, :], ps[:, 4 + m, :], ACT.Square, bias=bq[:, m:m + 1],
                                       accum_out=colsum[:, bass.ds(g, 1), 2 + m]).then_inc(S["q_done"], 1)
                        if m == 0:
                            dequant_hi(1)

            sequences(act, 0, B - 2, phase_a)
            phase_a(B - 1, last_b=True)

            def copy_acc(g, phase, n):
                act.wait_ge(S["down_done"], g * FC + FC if phase == "B" else g * MC + (NG * FC + MC))
                act.wait_ge(S["u_turned"], n)
                for m in range(KC):
                    act.activation(rT[:, m, :], ps[:, O0 + m, :], ACT.Copy).then_inc(S["acc_copied"], 1)

            def hidden_layer(phase, chunks, func, bias, slot_work):
                n0 = 0 if phase == "B" else NG * FC

                def chunk(g, half, c):
                    n = g * chunks + (c + n0)
                    par = (half * chunks + c) % 2
                    act.wait_ge(S["pre_ready"], n + 1)
                    act.activation(hid[par][:], ps[:, par * 2, :], func, bias=bias(c)).then_inc(S["act_done"], 1)
                    act.wait_ge(S["hid_ready"], n + 1)
                    act.activation(hh[par][:], hid[par][:], ACT.Copy).then_inc(S["hid_hi"], 1)

                def body(b, last_b=False):
                    for half in range(2):
                        g = b * 2 + half
                        last_g = last_b and half == 1
                        for c in range(3, chunks):
                            chunk(g, half, c)
                            slot_work(g, half, c, last_g)
                        if not last_g:
                            chunk(g + 1, 1 - half, 0)
                        n = result_update(phase, g, last_g)
                        copy_acc(g, phase, n)
                        if not last_g:
                            chunk(g + 1, 1 - half, 1)
                            chunk(g + 1, 1 - half, 2)
                        update(n)

                for c in range(3):
                    chunk(0, 0, c)
                sequences(act, 0, B - 2, body)
                body(B - 1, last_b=True)

            def mlp_slot(g, half, c, last_g):
                if c == 7 and not last_g:
                    update(in_attention_update(g + 1))
                if c == 11:
                    front(g + (FRONT0["B"] + 1), 1 - half)
                if last_g and c == 13:
                    act.wait_ge(S["wc_raw"], 32)
                    act.activation(wch[:], wcraw[:, :, 0:4 * D], ACT.Copy).then_inc(S["wc_hi"], 1)
                    act.activation(woh[:], wcraw[:, :, 4 * D:5 * D], ACT.Copy).then_inc(S["wc_hi"], 1)

            update(0)
            front(FRONT0["B"], 0)
            act.preload_act_table(ACT.Gelu_apprx_tanh)
            hidden_layer("B", FC, ACT.Gelu_apprx_tanh, lambda c: 0.0, mlp_slot)

            act.preload_act_table(ACT.Silu)

            def project(b, g, half, finish=None):
                for m in range(KC):
                    act.wait_ge(S["c_q"], g * KC + (m + 1))
                    act.activation(qh[:, m, half * GW:(half + 1) * GW], ps[:, m, :], ACT.Relu).then_inc(S["c_qhi"], 1)
                front(g + (FRONT0["C"] + 1), 1 - half)
                for t in range(GT):
                    act.wait_ge(S["c_kv"], g * GT + (t + 1))
                    act.activation(kvh[t % 2][:, 0:D], ps[:, 2 + t % 2, 0:D], ACT.Relu)
                    act.activation(kvh[t % 2][:, D:2 * D], ps[:, 2 + t % 2, D:2 * D], ACT.Copy) \
                        .then_inc(S["c_kvhi"], 1)
                    act.wait_ge(S["c_u"], g * GT + (t + 1))
                    act.activation(us[:, bass.ds(g * GT + t, 1), :].rearrange("p o c -> p (o c)"), ps[:, t % 2, 0:D],
                                   ACT.Silu) \
                        .then_inc(S["c_ucopied"], 1)
                if finish is not None:
                    output(finish)

            def output(g):
                act.wait_ge(S["o_turned"], g + 1)
                for k in range(KC):
                    act.activation(oh[:, k, :], ps[:, T0 + k, :], ACT.Copy).then_inc(S["o_hi"], 1)
                update(g + UPDATE0["C"])

            def attend(b):
                for t in range(ST):
                    act.wait_ge(S["c_o"], b * ST + (t + 1))
                    act.activation(obuf[:, t, :], ps[:, O1 - t % 2, 0:D], ACT.Copy)
                    act.activation(sq[:, t, :], ps[:, O1 - t % 2, 0:D], ACT.Square).then_inc(S["c_ocopied"], 1)

            project(0, 0, 0)
            project(0, 1, 1)
            attend(0)

            def phase_c(b):
                for half in range(2):
                    g = b * 2 + half
                    project(b, g, half, finish=g - 2)
                attend(b)

            sequences(act, 1, B - 1, phase_c)
            output(NG - 2)
            output(NG - 1)

            def gates(g, half):
                act.wait_ge(S["r_turned"], g + 1)
                act.activation(combT[half][:], ps[0:2 * E, T1, :], ACT.Copy).then_inc(S["r_copied"], 1)

            def expert_slot(g, half, c, last_g):
                if last_g:
                    return
                if c == 4:
                    front(g + (FRONT0["D"] + 1), 1 - half)
                if c == 9:
                    gates(g + 1, 1 - half)

            act.wait_ge(S["wd_raw"], 128)
            for hi, raw in ((gwh, gw), (selr, sel), (b2h, b2s), (w1h, w1raw), (w2h, w2raw)):
                act.activation(hi[:], raw[:], ACT.Copy).then_inc(S["wd_hi"], 1)
            gates(0, 0)
            hidden_layer("D", MC, ACT.Silu, lambda c: b1s[:, c:c + 1], expert_slot)

        @block.vector
        def _(dve):
            dve.memset(neghalf[:], -0.5).then_inc(S["half_ready"], 1)
            dve.sem_inc(S["dq_code"], CREDIT)
            dve.sem_inc(S["v_done"], CREDIT)
            dve.sem_inc(S["o_lo"], CREDIT)

            def front_stats(F, g, updates):
                dve.wait_ge(S["u_added"], updates)
                apart(dve)
                for t in range(GT):
                    last = dve.bn_stats(fstats[:, t, :], x[:, bass.ds(g * GT + t, 1), :].rearrange("p o c -> p (o c)"))
                last.then_inc(S["f_stats"], 1)
                dve.wait_ge(S["f_stats"], F + 1)
                apart(dve)
                for t in range(GT):
                    last = dve.bn_aggr(fmv[:, t, :], fstats[:, t, :])
                last.then_inc(S["f_mv"], 1)

            def front_norm(F, g):
                dve.wait_ge(S["f_rstd"], F + 1)
                dve.wait_ge(S["f_turned"], F)
                for t in range(GT):
                    last = dve.tensor_scalar(xn[:, t, :], x[:, bass.ds(g * GT + t, 1), :].rearrange("p o c -> p (o c)"),
                                             fmv[:, t, 0:1], frstd[:, t:t + 1], ALU.subtract, ALU.mult)
                last.then_inc(S["f_xn"], 1)

            def front_lo(F, half):
                for k in range(KC):
                    dve.wait_ge(S["f_hi"], F * 2 + (k + 1))
                    dve.tensor_tensor(xl[half][:, k, :], ps[:, T0 + k, :], xh[half][:, k, :].bitcast(F32),
                                      ALU.subtract).then_inc(S["f_lo"], 1)

            def update_stats(n):
                dve.wait_ge(S["u_turned"], n + 1)
                apart(dve)
                for t in range(GT):
                    last = dve.bn_stats(ustats[:, t, :], tok_banks[:, t, :])
                last.then_inc(S["u_stats"], 1)
                dve.wait_ge(S["u_stats"], n + 1)
                apart(dve)
                for t in range(GT):
                    last = dve.bn_aggr(umv[:, t, :], ustats[:, t, :])
                last.then_inc(S["u_mv"], 1)

            def update_offset(n):
                dve.wait_ge(S["u_rstd"], n + 1)
                dve.scalar_tensor_tensor(unm[:], umv[:, :, 0], -1.0, urstd[:], ALU.mult, ALU.mult) \
                    .then_inc(S["u_nm"], 1)

            def update_add(n, g):
                dve.wait_ge(S["u_normed"], n + 1)
                xg = x[:, bass.ds(g * GT, GT), :]
                dve.tensor_tensor(xg, xg, ry[:], ALU.add).then_inc(S["u_added"], 1)

            dve.wait_ge(S["x_even"], 16)
            front_stats(0, 0, 0)
            front_norm(0, 0)
            dve.wait_ge(S["wa_hi"], 1)
            dve.tensor_tensor(wal[:], waraw[:], wah[:].bitcast(F32), ALU.subtract).then_inc(S["wa_lo"], 1)
            dve.wait_ge(S["consts"], 48)
            front_lo(0, 0)

            def phase_a(b, last_b=False):
                for half in range(2):
                    g = b * 2 + half

                    def codes(s):
                        step = g * 2 + s
                        f0 = step * 6
                        dve.wait_ge(S["sc_in"], step * 16 + 16)
                        dve.tensor_scalar(sc[:], sc[:], FP8_UNIT, None, ALU.mult).then_inc(S["dq_scale"], 1)
                        dve.wait_ge(S["pk_in"], step * 16 + 16)
                        dve.wait_ge(S["dq_w"], CREDIT + step)
                        dve.tensor_scalar(code[:], pk[:], 0x07, 2, ALU.bitwise_and, ALU.logical_shift_left) \
                            .then_inc(S["dq_f"], 1)
                        for n, (bitmask, shift) in enumerate(((0x08, 4), (0x70, 6), (0x80, 8))):
                            dve.wait_ge(S["dq_f"], f0 + (2 * n + 1))
                            dve.tensor_scalar(field[:], pk[:], bitmask, shift, ALU.bitwise_and,
                                              ALU.logical_shift_left).then_inc(S["dq_f"], 1)
                            dve.wait_ge(S["dq_f"], f0 + (2 * n + 2))
                            dve.tensor_tensor(code[:], code[:], field[:], ALU.bitwise_or) \
                                .then_inc(S["dq_f" if n < 2 else "dq_code"], 1)

                    front_next = not (last_b and half == 1)
                    if front_next:
                        gn = g + 1
                        dve.wait_ge(x_loaded[1 - half], (b + half) * 16 + 16)
                        front_stats(gn, gn, 0)
                    codes(0)
                    dve.wait_ge(S["proj"], g * 6 + 2)
                    dve.wait_ge(S["k_copied"], g * 2 + 1)

                    def v_sum(m):
                        dve.scalar_tensor_tensor(ps[:, 1 + 2 * m, :], ps[:, 1 + 2 * m, :], bq[:, 4 + m:5 + m], ksb[:],
                                                 ALU.add, ALU.mult, accum_out=colsum[:, bass.ds(g, 1), 4 + m]) \
                            .then_inc(S["v_done"], 1)

                    v_sum(0)
                    if front_next:
                        front_norm(gn, gn)
                    dve.wait_ge(S["proj"], g * 6 + 4)
                    dve.wait_ge(S["k_copied"], g * 2 + 2)
                    v_sum(1)
                    if front_next:
                        front_lo(gn, 1 - half)
                    codes(1)

            sequences(dve, 0, B - 2, phase_a)
            phase_a(B - 1, last_b=True)

            dve.wait_ge(S["k_done"], CREDIT + 2 * NG)
            dve.wait_ge(S["q_done"], CREDIT + 2 * NG)
            dve.wait_ge(S["v_done"], CREDIT + 2 * NG)
            sums = colsum[:].rearrange("p (b h) s -> p b h s", h=2)
            dve.tensor_tensor(coltot[:], sums[:, :, 0, :], sums[:, :, 1, :], ALU.add).then_inc(S["col_tot"], 1)
            dve.wait_ge(S["col_tot"], 1)
            dve.wait_ge(S["col_rn"], 1)
            dve.tensor_tensor(colc[:], coltot[:, :, 4:6], colrn[:, :, 0:2], ALU.mult).then_inc(S["col_c0"], 1)
            dve.wait_ge(S["col_c0"], 1)
            dve.tensor_tensor(colc[:], colc[:], colrn[:, :, 2:4], ALU.mult).then_inc(S["col_c"], 1)
            dve.wait_ge(S["col_c"], 1)

            def scale(g, seq, n):
                dve.wait_ge(S["u_turned"], n)
                for m in range(KC):
                    last = dve.tensor_scalar(rT[:, m, :], qT[:, m, bass.ds(g * GW, GW)],
                                             colc[:, bass.ds(seq, 1), m], None, ALU.mult)
                last.then_inc(S["u_scaled"], 1)

            def hidden_layer(phase, chunks, slot_work):
                n0 = 0 if phase == "B" else NG * FC

                def chunk(g, half, c):
                    n = g * chunks + (c + n0)
                    par = (half * chunks + c) % 2
                    dve.wait_ge(S["act_done"], n + 1)
                    dve.wait_ge(S["up_ready"], n + 1)
                    dve.tensor_tensor(hid[par][:], hid[par][:], ps[:, par * 2 + 1, :], ALU.mult) \
                        .then_inc(S["hid_ready"], 1)
                    dve.wait_ge(S["hid_hi"], n + 1)
                    dve.tensor_tensor(hl[par][:], hid[par][:], hh[par][:].bitcast(F32), ALU.subtract) \
                        .then_inc(S["hid_lo"], 1)

                def body(b, last_b=False):
                    for half in range(2):
                        g = b * 2 + half
                        last_g = last_b and half == 1
                        for c in range(3, chunks):
                            chunk(g, half, c)
                            slot_work(b, g, half, c, last_g)
                        if not last_g:
                            for c in range(3):
                                chunk(g + 1, 1 - half, c)
                        n = result_update(phase, g, last_g)
                        update_stats(n)
                        update_offset(n)
                        update_add(n, g)

                for c in range(3):
                    chunk(0, 0, c)
                sequences(dve, 0, B - 2, body)
                body(B - 1, last_b=True)

            def mlp_slot(b, g, half, c, last_g):
                n = g * 2 + 1
                if not last_g:
                    if c == 3:
                        scale(g + 1, b + half, n)
                    if c == 5:
                        update_stats(n)
                    if c == 6:
                        update_offset(n)
                    if c == 8:
                        update_add(n, g + 1)
                if c == 8:
                    if last_g:
                        front_stats(FRONT0["C"], 0, 2 * NG - 1)
                    else:
                        front_stats(g + (FRONT0["B"] + 1), g + 1, g * 2 + 2)
                if c == 9:
                    front_norm(g + (FRONT0["B"] + 1), 0 if last_g else g + 1)
                if c == 11:
                    front_lo(g + (FRONT0["B"] + 1), 1 - half)
                if last_g and c == 14:
                    dve.wait_ge(S["wc_hi"], 2)
                    dve.tensor_tensor(wcl[:], wcraw[:, :, 0:4 * D], wch[:].bitcast(F32), ALU.subtract) \
                        .then_inc(S["wc_lo"], 1)
                    dve.tensor_tensor(wol[:], wcraw[:, :, 4 * D:5 * D], woh[:].bitcast(F32), ALU.subtract) \
                        .then_inc(S["wc_lo"], 1)

            scale(0, 0, 0)
            update_stats(0)
            update_offset(0)
            update_add(0, 0)
            front_stats(FRONT0["B"], 0, 1)
            front_norm(FRONT0["B"], 0)
            front_lo(FRONT0["B"], 0)
            hidden_layer("B", FC, mlp_slot)

            def project(b, g, half, updates, finish=None):
                F = g + (FRONT0["C"] + 1)
                gx = g + 1
                if isinstance(g, int) and g == NG - 1:
                    gx = 0
                front_stats(F, gx, updates)
                for m in range(KC):
                    dve.wait_ge(S["c_qhi"], g * KC + (m + 1))
                    dve.scalar_tensor_tensor(ql[:, m, half * GW:(half + 1) * GW], ps[:, m, :], 0.0,
                                             qh[:, m, half * GW:(half + 1) * GW].bitcast(F32), ALU.max, ALU.subtract) \
                        .then_inc(S["c_qlo"], 1)
                front_norm(F, gx)
                if finish is not None:
                    gate(finish, half)
                front_lo(F, 1 - half)
                for t in range(GT):
                    dve.wait_ge(S["c_kvhi"], g * GT + (t + 1))
                    dve.scalar_tensor_tensor(kvl[t % 2][:, 0:D], ps[:, 2 + t % 2, 0:D], 0.0,
                                             kvh[t % 2][:, 0:D].bitcast(F32), ALU.max, ALU.subtract)
                    dve.tensor_tensor(kvl[t % 2][:, D:2 * D], ps[:, 2 + t % 2, D:2 * D],
                                      kvh[t % 2][:, D:2 * D].bitcast(F32), ALU.subtract).then_inc(S["c_kvlo"], 1)
                if finish is not None:
                    output(finish)

            def gate(g, half):
                o = obuf[:, half * GT:(half + 1) * GT, :]
                heads = o.rearrange("p t (h d) -> p (t h) d", d=HD)
                rstd = hrstd[:, half * GT * NH:(half + 1) * GT * NH].unsqueeze(2).to_broadcast([P, GT * NH, HD])
                dve.tensor_tensor(heads, heads, rstd, ALU.mult).then_inc(S["c_scaled"], 1)
                dve.wait_ge(S["c_scaled"], g + 1)
                dve.tensor_tensor(o, o, us[:, bass.ds(g * GT, GT), :], ALU.mult).then_inc(S["c_gated"], 1)

            def output(g):
                for k in range(KC):
                    dve.wait_ge(S["o_hi"], g * 2 + (k + 1))
                    dve.tensor_tensor(ol[:, k, :], ps[:, T0 + k, :], oh[:, k, :].bitcast(F32), ALU.subtract) \
                        .then_inc(S["o_lo"], 1)
                update_stats(g + UPDATE0["C"])
                update_offset(g + UPDATE0["C"])
                update_add(g + UPDATE0["C"], g)

            def attend(b):
                dve.wait_ge(S["c_state"], b + 1)
                for m in range(KC):
                    last = dve.scalar_tensor_tensor(state[:, m, :], ps[:, O0, m * P:(m + 1) * P], 1.0 / HD, mask[:],
                                                    ALU.mult, ALU.mult)
                last.then_inc(S["c_masked"], 1)
                dve.wait_ge(S["c_masked"], b + 1)
                dve.tensor_copy(stateh[:], state[:]).then_inc(S["c_sthi"], 1)
                dve.wait_ge(S["c_sthi"], b + 1)
                dve.tensor_tensor(statel[:], state[:], stateh[:].bitcast(F32), ALU.subtract).then_inc(S["c_stlo"], 1)
                for half in range(2):
                    dve.wait_ge(S["c_ocopied"], b * ST + (half + 1) * GT)
                    dve.tensor_reduce(hsum[:, half * GT * NH:(half + 1) * GT * NH],
                                      sq[:, half * GT:(half + 1) * GT, :].rearrange("p t (h d) -> p (t h) d", d=HD),
                                      AX_X, ALU.add).then_inc(S["c_hsum"], 1)
                links = 3 + 3 * NEWTON
                k = [0]

                def link(ins):
                    k[0] += 1
                    ins.then_inc(S["c_hrstd"], 1)
                    dve.wait_ge(S["c_hrstd"], b * links + k[0])

                dve.wait_ge(S["c_hsum"], b * 2 + 2)
                link(dve.tensor_scalar(hsum[:], hsum[:], 1.0 / HD, 1e-24, ALU.mult, ALU.max))
                guess = hrstd[:].bitcast(I32)
                link(dve.tensor_scalar(guess, hsum[:].bitcast(I32), 1, None, ALU.logical_shift_right))
                link(dve.tensor_scalar(guess, guess, -1.0, float(0x5F3759DF), ALU.mult, ALU.add))
                for _ in range(NEWTON):
                    link(dve.tensor_tensor(hwork[:], hrstd[:], hrstd[:], ALU.mult))
                    link(dve.scalar_tensor_tensor(hwork[:], hwork[:], -0.5, hsum[:], ALU.mult, ALU.mult))
                    link(dve.scalar_tensor_tensor(hrstd[:], hwork[:], 1.5, hrstd[:], ALU.add, ALU.mult))
                assert k[0] == links

            dve.wait_ge(S["consts"], 64)
            project(0, 0, 0, 2 * NG)
            project(0, 1, 1, 2 * NG)
            attend(0)

            def phase_c(b):
                for half in range(2):
                    g = b * 2 + half
                    project(b, g, half, g + (UPDATE0["C"] - 2), finish=g - 2)
                attend(b)

            sequences(dve, 1, B - 2, phase_c)
            phase_c(B - 1)
            for half in range(2):
                gate(NG - 2 + half, half)
                output(NG - 2 + half)

            RC = 9

            def route(g):
                k = [0]

                def link(ins):
                    k[0] += 1
                    ins.then_inc(S["r_chain"], 1)
                    dve.wait_ge(S["r_chain"], g * RC + k[0])

                dve.wait_ge(S["r_scores"], g + 1)
                dve.tensor_tensor(score[:], ps[:, T0, 0:GT * E].rearrange("p (t e) -> p t e", e=E),
                                  gbs[:].unsqueeze(1).to_broadcast([P, GT, E]), ALU.add).then_inc(S["r_scored"], 1)
                dve.wait_ge(S["r_scored"], g + 1)
                apart(dve)
                for t in range(GT):
                    last = dve.max(best[:, t, :], score[:, t, :])
                last.then_inc(S["r_best"], 1)
                dve.wait_ge(S["r_best"], g + 1)
                apart(dve)
                for t in range(GT):
                    last = dve.max_index(besti[:, t, :], best[:, t, :], score[:, t, :])
                last.then_inc(S["r_found"], 1)
                dve.tensor_tensor(gap[:], best[:, :, 1], best[:, :, 0], ALU.subtract).then_inc(S["r_gap"], 1)
                dve.wait_ge(S["r_found"], g + 1)
                link(dve.tensor_copy(bestf[:], besti[:]))
                rows = iota[:].unsqueeze(1).to_broadcast([P, GT, E])
                link(dve.tensor_tensor(pick1[:], rows, bestf[:, :, 0:1].to_broadcast([P, GT, E]), ALU.is_equal))
                link(dve.tensor_tensor(pick2[:], rows, bestf[:, :, 1:2].to_broadcast([P, GT, E]), ALU.is_equal))
                dve.wait_ge(S["r_second"], g + 1)
                link(dve.tensor_scalar(denom[:], second[:], 1.0, None, ALU.add))
                link(dve.reciprocal(gate1[:], denom[:]))
                link(dve.tensor_tensor(gate2[:], gate1[:], second[:], ALU.mult))
                link(dve.tensor_tensor(pick1[:], pick1[:], gate1[:].unsqueeze(2).to_broadcast([P, GT, E]), ALU.mult))
                link(dve.tensor_tensor(pick2[:], pick2[:], gate2[:].unsqueeze(2).to_broadcast([P, GT, E]), ALU.mult))
                link(dve.tensor_tensor(pick1[:], pick1[:], pick2[:], ALU.add))
                assert k[0] == RC
                dve.tensor_copy(comb[:, :, 0:E], pick1[:]).then_inc(S["r_comb_hi"], 1)
                dve.wait_ge(S["r_comb_hi"], g + 1)
                dve.tensor_tensor(comb[:, :, E:2 * E], pick1[:], comb[:, :, 0:E].bitcast(F32), ALU.subtract) \
                    .then_inc(S["r_comb"], 1)

            dve.wait_ge(S["wd_raw"], 128)
            dve.tensor_tensor(gbs[:], gb[:, 0, :], gb[:, 1, :], ALU.add).then_inc(S["r_bias"], 1)
            dve.wait_ge(S["wd_hi"], 5)
            for lo, raw, hi in ((gwl, gw, gwh), (b2l, b2s, b2h), (w1l, w1raw, w1h), (w2l, w2raw, w2h)):
                dve.tensor_tensor(lo[:], raw[:], hi[:].bitcast(F32), ALU.subtract).then_inc(S["wd_lo"], 1)
            dve.wait_ge(S["r_bias"], 1)
            dve.wait_ge(S["r_consts"], E + 1)
            route(0)

            def d_slot(b, g, half, c, last_g):
                if last_g:
                    return
                if c == 3:
                    front_stats(g + (FRONT0["D"] + 1), g + 1, UPDATE0["D"])
                    front_norm(g + (FRONT0["D"] + 1), g + 1)
                if c == 4:
                    front_lo(g + (FRONT0["D"] + 1), 1 - half)
                if c == 6:
                    route(g + 1)

            hidden_layer("D", MC, d_slot)

        @block.gpsimd
        def _(pool):
            pool.sem_inc(S["dq_w"], CREDIT)
            pool.sem_inc(S["dq_lo"], CREDIT)
            pool.wait_ge(S["half_ready"], 1)

            def front(F):
                pool.wait_ge(S["f_mv"], F + 1)
                pool.wait_ge(S["f_xn"], F)
                apart(pool)
                pool.tensor_scalar(fvar[:], fmv[:, :, 1], EPS, None, ALU.add).then_inc(S["f_var"], 1)
                pool.wait_ge(S["f_var"], F + 1)
                pool.tensor_tensor(frstd[:], fvar[:], neghalf[:, 0:GT], ALU.pow).then_inc(S["f_rstd"], 1)

            def update(n):
                pool.wait_ge(S["u_mv"], n + 1)
                pool.wait_ge(S["u_normed"], n)
                apart(pool)
                pool.tensor_scalar(uvar[:], umv[:, :, 1], EPS, None, ALU.add).then_inc(S["u_var"], 1)
                pool.wait_ge(S["u_var"], n + 1)
                pool.tensor_tensor(urstd[:], uvar[:], neghalf[:, 0:GT], ALU.pow).then_inc(S["u_rstd"], 1)

            front(0)

            def phase_a(b, last_b=False):
                for half in range(2):
                    g = b * 2 + half
                    if not (last_b and half == 1):
                        front(g + 1)
                    for s in range(2):
                        step = g * 2 + s
                        pool.wait_ge(S["dq_code"], CREDIT + step + 1)
                        pool.wait_ge(S["dq_scale"], step + 1)
                        pool.wait_ge(S["dq_lo"], CREDIT + step)
                        apart(pool)
                        low = code[:].bitcast(FP8).rearrange("p m (c e) -> p m e c", e=4)
                        for nib in range(2):
                            last = pool.tensor_tensor(weight[:, :, nib, :], low[:, :, nib, :], sc[:], ALU.mult)
                        last.then_inc(S["dq_w"], 1)
                        pool.wait_ge(S["dq_hi"], step + 1)
                        pool.tensor_tensor(wfl[:, bass.ds(step, 1)].rearrange("p o m n c -> p (o m n c)"),
                                           weight[:].rearrange("p m n c -> p (m n c)"),
                                           wfh[:, bass.ds(step, 1)].bitcast(F32).rearrange("p o m n c -> p (o m n c)"),
                                           ALU.subtract).then_inc(S["dq_lo"], 1)

            sequences(pool, 0, B - 2, phase_a)
            phase_a(B - 1, last_b=True)
            pool.wait_ge(S["col_tot"], 1)
            pool.tensor_tensor(colrn[:], coltot[:, :, 0:4], neghalf[:, 0:4 * B].rearrange("p (b s) -> p b s", b=B),
                               ALU.pow).then_inc(S["col_rn"], 1)

            update(0)
            front(FRONT0["B"])

            def phase_b(b, last_b=False):
                for half in range(2):
                    g = b * 2 + half
                    last_g = last_b and half == 1
                    if not last_g:
                        update(g * 2 + 1)
                    front(g + (FRONT0["B"] + 1))
                    update(2 * NG - 1 if last_g else g * 2 + 2)

            sequences(pool, 0, B - 2, phase_b)
            phase_b(B - 1, last_b=True)

            front(FRONT0["C"] + 1)
            front(FRONT0["C"] + 2)

            def phase_c(b):
                for half in range(2):
                    g = b * 2 + half
                    front(g + (FRONT0["C"] + 1))
                    update(g + (UPDATE0["C"] - 2))

            sequences(pool, 1, B - 1, phase_c)
            update(UPDATE0["C"] + NG - 2)
            update(UPDATE0["C"] + NG - 1)

            def second_gate(g):
                pool.wait_ge(S["r_gap"], g + 1)
                pool.tensor_tensor(second[:], ebase[:], gap[:], ALU.pow).then_inc(S["r_second"], 1)

            pool.wait_ge(S["u_turned"], UPDATE0["D"])
            for e in range(E):
                pool.memset(iota[:, e:e + 1], float(e)).then_inc(S["r_consts"], 1)
            pool.memset(ebase[:], E_BASE).then_inc(S["r_consts"], 1)
            pool.wait_ge(S["r_consts"], E + 1)
            second_gate(0)

            def phase_d(b, last_b=False):
                for half in range(2):
                    g = b * 2 + half
                    if not (last_b and half == 1):
                        front(g + (FRONT0["D"] + 1))
                        second_gate(g + 1)
                    update(g + UPDATE0["D"])

            sequences(pool, 0, B - 2, phase_d)
            phase_d(B - 1, last_b=True)


def kernel(L0_attn_x, L0_attn_W, L0_attn_b, L0_ffn_gate_W_packed, L0_ffn_gate_scales, L0_ffn_up_W_packed,
           L0_ffn_up_scales, L0_ffn_down_W_packed, L0_ffn_down_scales, L1_attn_Wq, L1_attn_Wk, L1_attn_Wv, L1_attn_Wu,
           L1_attn_Wo, L1_ffn_gate_w, L1_ffn_gate_b, L1_ffn_bias, L1_ffn_w1, L1_ffn_b1, L1_ffn_w2, L1_ffn_b2):
    import numpy as np
    import concourse.bacc as bacc
    from concourse.bass_utils import run_bass_kernel_spmd

    a = np.asarray

    def in_rows(w):
        return a(w).reshape(P, KC, -1)

    def pack_in(w, t):
        return a(w).reshape(FC // 2, P, 2, t).transpose(0, 2, 3, 1).reshape(FC, t, P)

    def pack_down(w, t):
        return a(w).reshape(P, KC, FC // 2, t).transpose(2, 1, 3, 0).reshape(FC, t, P)

    packed = np.stack([pack_in(L0_ffn_gate_W_packed, P), pack_in(L0_ffn_up_W_packed, P),
                       pack_down(L0_ffn_down_W_packed, P)], axis=2).reshape(FC, P, 3 * P)
    scales = np.stack([pack_in(L0_ffn_gate_scales, 8), pack_in(L0_ffn_up_scales, 8),
                       pack_down(L0_ffn_down_scales, 8)], axis=2).reshape(FC * 8, 3 * P)
    arrays = {
        "x_in": a(L0_attn_x).reshape(NT, P, P, KC).transpose(0, 1, 3, 2).reshape(NT, P, D),
        "wqkv": a(L0_attn_W).reshape(P, KC, 3, P, KC).transpose(0, 1, 2, 4, 3).reshape(P, KC, 3 * D),
        "bqkv": a(L0_attn_b).reshape(3, P, KC).transpose(1, 0, 2).reshape(P, 6),
        "packed": packed,
        "scales": scales,
        "wl1": np.concatenate([in_rows(w) for w in (L1_attn_Wq, L1_attn_Wk, L1_attn_Wv, L1_attn_Wu)], axis=2),
        "wo": a(L1_attn_Wo).reshape(KC, P, P, KC).transpose(1, 0, 3, 2).reshape(P, KC, D),
        "w1": a(L1_ffn_w1).reshape(MH, P, KC).transpose(1, 2, 0),
        "b1": a(L1_ffn_b1).reshape(MC, P).T,
        "w2": a(L1_ffn_w2).transpose(0, 2, 1).reshape(MC, P, P, KC).transpose(1, 0, 3, 2).reshape(P, MC, D),
        "b2": a(L1_ffn_b2).reshape(E, P, KC).transpose(0, 2, 1).reshape(E, D),
        "gate_w": a(L1_ffn_gate_w).reshape(E, P, KC).transpose(1, 2, 0),
        "gate_b": a(L1_ffn_gate_b),
        "gate_bias": a(L1_ffn_bias),
        "ident_in": np.eye(P, dtype=np.float32),
        "mask_in": np.kron(np.eye(P // HD), np.ones((HD, HD))).astype(np.float32),
        "sel_in": np.tile(np.repeat(np.eye(E), EH, axis=1), (2, 1)).astype(np.float32),
    }
    nc = bacc.Bacc("TRN2", target_bir_lowering=False, num_devices=1)
    arrays = {n: np.ascontiguousarray(v) for n, v in arrays.items()}
    args = [nc.dram_tensor(n, v.shape, mybir.dt.from_np(v.dtype), kind="ExternalInput").ap() for n, v in arrays.items()]
    out = nc.dram_tensor("out", (NT, P, D), F32, kind="ExternalOutput").ap()
    build_program(nc, *args, out)
    r = run_bass_kernel_spmd(nc, [arrays], core_ids=[0])
    got = r.results[0]["out"]
    return got.reshape(B, TOK // B, KC, P).transpose(0, 1, 3, 2).reshape(B, TOK // B, D)
```

```python
from contextlib import ExitStack

import concourse.bass as bass
from concourse import mybir

ALU = mybir.AluOpType
ACT = mybir.ActivationFunctionType
AX_X = mybir.AxisListType.X
F32 = mybir.dt.float32
F32R = mybir.dt.float32r
I32 = mybir.dt.int32
U32 = mybir.dt.uint32
FP8 = mybir.dt.float8e4

P = 128
D = 256
KC = D // P
B = 4
TOK = 4 * 1024
NT = TOK // P
GT = 4
GW = GT * P
NG = NT // GT
ST = NT // B
MLP = 2048
FC = MLP // P
E, EH = 8, 176
MH = E * EH
MC = MH // P
HD = 16
NH = D // HD
EPS = 1e-5
CREDIT = 1
NEWTON = 3
E_BASE = 2.718281828459045
FP8_UNIT = 64.0

FRONT0 = {"A": 0, "B": NG, "C": 2 * NG, "D": 3 * NG}
UPDATE0 = {"B": 0, "C": 2 * NG, "D": 3 * NG}
G0, U0, G1, U1, O0, O1, T0, T1 = range(8)
DQ = FC
LEAD = {"B": 5, "D": 9}


def in_attention_update(g):
    return 0 if isinstance(g, int) and g == 0 else g * 2 - 1


def result_update(phase, g, last_g):
    if phase == "D":
        return g + UPDATE0["D"]
    return 2 * NG - 1 if last_g else g * 2 + 2


def build_program(nc, x_in, wqkv, bqkv, packed, scales, wl1, wo, w1, b1, w2, b2, gate_w, gate_b, gate_bias,
                  ident_in, mask_in, sel_in, out):
    with ExitStack() as ctx:
        def place(name, shape, dt, at):
            at = (at + 31) // 32 * 32
            size = 4
            for n in shape[1:]:
                size *= n
            assert at + size <= nc.sbuf_usable_end, (name, at + size)
            return nc.alloc_sbuf_tensor_at(name, shape, dt, offset=at), at + size

        top = nc.sbuf_base
        x, top = place("x", [P, NT, D], F32, top)
        xn, top = place("xn", [P, GT, D], F32, top)
        xh0, top = place("xh0", [P, KC, GW], F32R, top)
        xh1, top = place("xh1", [P, KC, GW], F32R, top)
        xl0, top = place("xl0", [P, KC, GW], F32R, top)
        xl1, top = place("xl1", [P, KC, GW], F32R, top)
        xh, xl = (xh0, xh1), (xl0, xl1)
        rT_first, _ = place("rT_first", [P, KC, GW], F32, top - 2 * KC * GW * 4)
        ry_first, _ = place("ry_first", [P, GT, D], F32, top - 4 * KC * GW * 4)
        ident, top = place("ident", [P, P], F32, top)
        fstats, top = place("fstats", [P, GT, 6], F32, top)
        fmv, top = place("fmv", [P, GT, 2], F32, top)
        fvar, top = place("fvar", [P, GT], F32, top)
        frstd, top = place("frstd", [P, GT], F32, top)
        ustats, top = place("ustats", [P, GT, 6], F32, top)
        umv, top = place("umv", [P, GT, 2], F32, top)
        uvar, top = place("uvar", [P, GT], F32, top)
        urstd, top = place("urstd", [P, GT], F32, top)
        unm, top = place("unm", [P, GT], F32, top)
        neghalf, top = place("neghalf", [P, 64], F32, top)
        colsum, top = place("colsum", [P, NG, 6], F32, top)
        coltot, top = place("coltot", [P, B, 6], F32, top)
        colrn, top = place("colrn", [P, B, 4], F32, top)
        colkv, top = place("colkv", [P, B, 2], F32, top)
        colc, top = place("colc", [P, NG, 2], F32, top)
        bq, top = place("bq", [P, 6], F32, top)
        b1s, region_q = place("b1s", [P, MC], F32, top)
        qT, region_w = place("qT", [P, KC, TOK], F32, region_q)
        wch, at = place("wch", [P, KC, 4 * D], F32R, region_q)
        wcl, at = place("wcl", [P, KC, 4 * D], F32R, at)
        woh, at = place("woh", [P, KC, D], F32R, at)
        wol, at = place("wol", [P, KC, D], F32R, at)
        wcraw, at = place("wcraw", [P, KC, 5 * D], F32, region_w - KC * 5 * D * 4)
        assert at <= region_w
        sel, at = place("sel", [2 * E, MH], F32, region_q)
        selr, at = place("selr", [2 * E, MH], F32R, at)
        assert at <= region_q + 2 * KC * 4 * D * 4
        gw, at = place("gw", [P, KC, E], F32, region_w - KC * 5 * D * 4)
        gwh, at = place("gwh", [P, KC, E], F32R, at)
        gwl, at = place("gwl", [P, KC, E], F32R, at)
        gb, at = place("gb", [P, 2, E], F32, at)
        gbs, at = place("gbs", [P, E], F32, at)
        b2s, at = place("b2s", [2 * E, D], F32, at)
        b2h, at = place("b2h", [2 * E, D], F32R, at)
        b2l, at = place("b2l", [2 * E, D], F32R, at)
        score, at = place("score", [P, GT, E], F32, at)
        best, at = place("best", [P, GT, 8], F32, at)
        besti, at = place("besti", [P, GT, 8], U32, at)
        bestf, at = place("bestf", [P, GT, 8], F32, at)
        iota, at = place("iota", [P, E], F32, at)
        gap, at = place("gap", [P, GT], F32, at)
        ebase, at = place("ebase", [P, GT], F32, at)
        second, at = place("second", [P, GT], F32, at)
        denom, at = place("denom", [P, GT], F32, at)
        gate1, at = place("gate1", [P, GT], F32, at)
        gate2, at = place("gate2", [P, GT], F32, at)
        pick1, at = place("pick1", [P, GT, E], F32, at)
        pick2, at = place("pick2", [P, GT, E], F32, at)
        comb, at = place("comb", [P, GT, 2 * E], F32R, at)
        combT0, at = place("combT0", [2 * E, GW], F32R, at)
        combT1, at = place("combT1", [2 * E, GW], F32R, at)
        combT = (combT0, combT1)
        assert at <= region_w
        wah, at = place("wah", [P, KC, 3 * D], F32R, region_w)
        wal, region_f = place("wal", [P, KC, 3 * D], F32R, at)
        hid0, at = place("hid0", [P, GW], F32, region_w)
        hid1, at = place("hid1", [P, GW], F32, at)
        hh0, at = place("hh0", [P, GW], F32R, at)
        hh1, at = place("hh1", [P, GW], F32R, at)
        hl0, at = place("hl0", [P, GW], F32R, at)
        hl1, at = place("hl1", [P, GW], F32R, at)
        assert at <= region_f
        hid, hh, hl = (hid0, hid1), (hh0, hh1), (hl0, hl1)
        wfh, at = place("wfh", [P, DQ, 3, 2, P], F32R, region_f)
        wfl, region_s = place("wfl", [P, DQ, 3, 2, P], F32R, at)
        waraw, _ = place("waraw", [P, KC, 3 * D], F32, region_s - KC * 3 * D * 4)
        qh, at = place("qh", [P, KC, ST * P], F32R, region_f)
        ql, at = place("ql", [P, KC, ST * P], F32R, at)
        kvh0, at = place("kvh0", [P, 2 * D], F32R, at)
        kvh1, at = place("kvh1", [P, 2 * D], F32R, at)
        kvl0, at = place("kvl0", [P, 2 * D], F32R, at)
        kvl1, at = place("kvl1", [P, 2 * D], F32R, at)
        kvh, kvl = (kvh0, kvh1), (kvl0, kvl1)
        us, at = place("us", [P, NT, D], F32, at)
        obuf, at = place("obuf", [P, ST, D], F32, at)
        sq, at = place("sq", [P, GT, D], F32, at)
        oh, at = place("oh", [P, KC, GW], F32R, at)
        ol, at = place("ol", [P, KC, GW], F32R, at)
        state, at = place("state", [P, KC, P], F32, at)
        stateh, at = place("stateh", [P, KC, P], F32R, at)
        statel, at = place("statel", [P, KC, P], F32R, at)
        mask, at = place("mask", [P, P], F32, at)
        hsum, at = place("hsum", [P, ST * NH], F32, at)
        hrstd, at = place("hrstd", [P, ST * NH], F32, at)
        hwork, at = place("hwork", [P, ST * NH], F32, at)
        w1raw_at = region_s - KC * MH * 4
        assert at <= w1raw_at
        w1raw, _ = place("w1raw", [P, KC, MH], F32, w1raw_at)
        w2raw, _ = place("w2raw", [P, MC, D], F32, region_w)
        w1h, at = place("w1h", [P, KC, MH], F32R, region_f)
        w1l, at = place("w1l", [P, KC, MH], F32R, at)
        w2h, at = place("w2h", [P, MC, D], F32R, at)
        w2l, at = place("w2l", [P, MC, D], F32R, at)
        assert at <= w1raw_at
        pk0, at = place("pk0", [P, 3, P], I32, region_s)
        pk1, at = place("pk1", [P, 3, P], I32, at)
        sc0, at = place("sc0", [P, 3, P], F32, at)
        sc1, at = place("sc1", [P, 3, P], F32, at)
        pk, sc = (pk0, pk1), (sc0, sc1)
        code, at = place("code", [P, 3, P], I32, at)
        field, at = place("field", [P, 3, P], I32, at)
        ksb, at = place("ksb", [P, GW], F32, at)
        weight, at = place("weight", [P, 3, 2, P], F32, at)
        rT, at = place("rT", [P, KC, GW], F32, region_s)
        ry, at = place("ry", [P, GT, D], F32, at)

        ps = ctx.enter_context(nc.psum_tensor("ps", [P, 8, GW], F32))
        def token_major(bank):
            return ps[:, bank:bank + 2, :].rearrange("p b (t c) -> p (b t) c", t=2)

        tok_banks = token_major(T0)

        names = ("w1_hi w1_lo w2_hi w2_lo sel_hi rt_hi rt_lo sel_raw u_neg "
                 "waited consts x_even x_odd wa_raw pk_even pk_odd sc_even sc_odd wc_raw wd_raw out_stored "
                 "half_ready wa_hi wa_lo "
                 "f_stats f_mv f_var f_rstd f_xn f_turned f_hi f_lo "
                 "u_turned u_stats u_mv u_var u_rstd u_nm u_normed u_added u_scaled "
                 "proj k_copied k_done v_done q_done "
                 "dq_f dq_code dq_w dq_hi dq_lo "
                 "col_tot col_rn col_c0 col_c "
                 "pre_ready up_ready act_done hid_ready hid_hi hid_lo down_done "
                 "acc_copied "
                 "wc_hi wc_lo c_q c_kv c_u c_qhi c_qlo c_kvhi c_kvlo c_ucopied c_state c_masked c_sthi c_stlo "
                 "c_o c_ocopied c_hsum c_hrstd c_scaled c_gated o_turned o_hi o_lo "
                 "r_consts r_bias r_scores r_scored r_best r_found r_comb_hi r_chain r_gap r_second "
                 "r_comb r_turned r_copied "
                 ).split()
        S = {n: ctx.enter_context(nc.semaphore(n)) for n in names}
        x_loaded = (S["x_even"], S["x_odd"])
        pk_loaded = (S["pk_even"], S["pk_odd"])
        sc_loaded = (S["sc_even"], S["sc_odd"])
        block = ctx.enter_context(nc.Block())

        def apart(eng):
            eng.sem_inc(S["waited"], 1)

        def sequences(eng, first, last, body):
            with eng.Fori(first, last + 1) as b:
                body(b)

        def run_groups(eng, lead, chunks, begin, chunk, slot_work):
            begin()
            for c in range(lead):
                chunk(0, 0, c, 2)
                slot_work(0, 0, c, 2, None)

            def body(b, last_b=False):
                for half in range(2):
                    g = b * 2 + half
                    left = 1 - half if last_b else 2
                    for c in range(lead, chunks):
                        chunk(g, half, c, left)
                        slot_work(g, half, c, left, None)
                    if left > 0:
                        for c in range(lead):
                            chunk(g + 1, 1 - half, c, left - 1)
                            slot_work(g + 1, 1 - half, c, left - 1, g)

            sequences(eng, 0, B - 2, body)
            body(B - 1, last_b=True)

        @block.sync
        def _(sp):
            def load_step(step, s):
                sp.dma_start(pk[s][:], packed[bass.ds(step, 1)].rearrange("o p (m c) -> (o p) m c", m=3)) \
                    .then_inc(pk_loaded[s], 16)
                rows = scales[bass.ds(step * 8, 8)].unsqueeze(1).to_broadcast([8, 16, 3 * P])
                sp.dma_start(sc[s][:].rearrange("p m c -> p (m c)"), rows).then_inc(sc_loaded[s], 16)

            sp.dma_start(x[:, 0:GT, :], x_in[0:GT].rearrange("t p c -> p t c")).then_inc(S["x_even"], 16)
            sp.dma_start(waraw[:], wqkv).then_inc(S["wa_raw"], 16)
            sp.dma_start(ident[:], ident_in).then_inc(S["consts"], 16)
            sp.dma_start(bq[:], bqkv).then_inc(S["consts"], 16)
            sp.dma_start(b1s[:], b1).then_inc(S["consts"], 16)
            sp.dma_start(x[:, GT:2 * GT, :], x_in[GT:2 * GT].rearrange("t p c -> p t c")).then_inc(S["x_odd"], 16)
            for s in range(2):
                load_step(s, s)

            def phase_a(b, last_b=False):
                for half in range(2):
                    g = b * 2 + half
                    if not last_b:
                        sp.wait_ge(x_loaded[half], b * 16 + 16)
                        sp.dma_start(x[:, bass.ds(g * GT + 2 * GT, GT), :],
                                     x_in[bass.ds(g * GT + 2 * GT, GT)].rearrange("t p c -> p t c")) \
                            .then_inc(x_loaded[half], 16)
                    if not (last_b and half == 1):
                        for s in range(2):
                            step = g * 2 + s
                            sp.wait_ge(S["dq_w"], step + (CREDIT + 1))
                            apart(sp)
                            load_step(step + 2, s)

            sequences(sp, 0, B - 2, phase_a)
            phase_a(B - 1, last_b=True)
            sp.wait_ge(S["u_scaled"], NG)
            sp.dma_start(wcraw[:, :, 0:4 * D], wl1).then_inc(S["wc_raw"], 16)
            sp.dma_start(wcraw[:, :, 4 * D:5 * D], wo).then_inc(S["wc_raw"], 16)
            sp.wait_ge(S["down_done"], NG * FC)
            sp.dma_start(mask[:], mask_in).then_inc(S["consts"], 16)
            sp.dma_start(w1raw[:], w1).then_inc(S["wd_raw"], 16)
            sp.dma_start(w2raw[:], w2).then_inc(S["wd_raw"], 16)
            sp.wait_ge(S["wc_lo"], 2)
            sp.dma_start(gw[:], gate_w).then_inc(S["wd_raw"], 16)
            sp.dma_start(gb[:, 0, :], gate_b.unsqueeze(0).to_broadcast([P, E])).then_inc(S["wd_raw"], 16)
            sp.dma_start(gb[:, 1, :], gate_bias.unsqueeze(0).to_broadcast([P, E])).then_inc(S["wd_raw"], 16)
            sp.dma_start(b2s[0:E, :], b2).then_inc(S["wd_raw"], 16)
            sp.dma_start(b2s[E:2 * E, :], b2).then_inc(S["wd_raw"], 16)
            sp.wait_ge(S["c_q"], NG * KC)
            sp.dma_start(sel[:], sel_in).then_inc(S["sel_raw"], 16)

            def store(b):
                for half in range(2):
                    g = b * 2 + half
                    sp.wait_ge(S["u_added"], g + (UPDATE0["D"] + 1))
                    sp.dma_start(out[bass.ds(g * GT, GT)].rearrange("t p c -> p t c"),
                                 x[:, bass.ds(g * GT, GT), :]).then_inc(S["out_stored"], 16)

            sequences(sp, 0, B - 1, store)
            sp.wait_ge(S["out_stored"], 16 * NG)

        @block.tensor
        def _(pe):
            def product(dst, terms, start=True, stop=True, group_check=True):
                n = len(terms)
                for k, (ah, al, bh, bl) in enumerate(terms):
                    pe.matmul(dst, ah, bl, start=start and k == 0, stop=False, skip_group_check=not group_check)
                    pe.matmul(dst, ah, bh, start=False, stop=False, skip_group_check=not group_check)
                    last = pe.matmul(dst, al, bh, start=False, stop=stop and k == n - 1,
                                     skip_group_check=not group_check)
                return last

            def front(F, updates):
                if not (isinstance(updates, int) and updates == 0):
                    pe.wait_ge(S["u_normed"], updates)
                if not (isinstance(F, int) and F == 0):
                    pe.wait_ge(S["f_lo"], F * 2)
                pe.wait_ge(S["f_xn"], F + 1)
                for k in range(KC):
                    for t in range(GT):
                        last = pe.transpose(ps[:, T0 + k, t * P:(t + 1) * P], xn[:, t, k * P:(k + 1) * P], ident[:])
                last.then_inc(S["f_turned"], 1)

            def update_turn(updates, fronts, src=rT):
                if not (isinstance(updates, int) and updates == 0):
                    pe.wait_ge(S["u_normed"], updates)
                pe.wait_ge(S["f_lo"], fronts * 2)
                for t in range(GT):
                    for k in range(KC):
                        last = pe.transpose(tok_banks[:, t, k * P:(k + 1) * P], src[:, k, t * P:(t + 1) * P], ident[:])
                last.then_inc(S["u_turned"], 1)

            def front_ready(F):
                pe.wait_ge(S["f_hi"], F * 2 + 2)
                pe.wait_ge(S["f_lo"], F * 2 + 2)

            def attention_turn(g, src=rT):
                pe.wait_ge(S["u_scaled"], g + 1)
                update_turn(in_attention_update(g), g + FRONT0["B"], src)

            pe.wait_ge(S["consts"], 48)
            front(0, 0)
            pe.wait_ge(S["wa_hi"], 1)
            pe.wait_ge(S["wa_lo"], 1)

            def phase_a(b, last_b=False):
                for half in range(2):
                    g = b * 2 + half
                    front_ready(g)
                    order = ((2, 0, "k_done"), (4, 1, "v_done"), (3, 2, "k_done"), (5, 3, "v_done"),
                             (0, 4, "q_done"), (1, 5, "q_done"))
                    for n, (m, bank, reader) in enumerate(order):
                        if n in (0, 4):
                            if n == 0:
                                pe.wait_ge(S["k_done"], CREDIT + g * 2)
                                pe.wait_ge(S["v_done"], CREDIT + g * 2)
                            else:
                                pe.wait_ge(S["q_done"], CREDIT + g * 2)
                        cols = slice(m * P, (m + 1) * P)
                        product(ps[:, bank, :], [(wah[:, k, cols], wal[:, k, cols], xh[half][:, k, :], xl[half][:, k, :])
                                                 for k in range(KC)]).then_inc(S["proj"], 1)
                        if n == 1 and last_b and half == 1:
                            attention_turn(0, rT_first)
                        if n == 3 and not (last_b and half == 1):
                            front(g + 1, 0)

            sequences(pe, 0, B - 2, phase_a)
            phase_a(B - 1, last_b=True)

            def hidden_layer(phase, chunks, pre, down, slot_work):
                n0 = 0 if phase == "B" else NG * FC

                def pre_chunk(half, c):
                    pre(half, c, (half * chunks + c) % 2 * 2)

                def chunk(g, half, c, left):
                    n = g * chunks + (c + n0)
                    pe.wait_ge(S["hid_ready"], n + 1)
                    if c + 2 < chunks:
                        pre_chunk(half, c + 2)
                    elif left > 0:
                        if c + 2 == chunks:
                            front_ready(g + (FRONT0[phase] + 1))
                            if phase == "D":
                                pe.wait_ge(S["r_copied"], g + 2)
                        pre_chunk(1 - half, c + 2 - chunks)
                    pe.wait_ge(S["hid_hi"], n + 1)
                    pe.wait_ge(S["hid_lo"], n + 1)
                    if c == 0:
                        pe.wait_ge(S["acc_copied"], g * 2 + (0 if phase == "B" else 2 * NG))
                    down(half, c, (half * chunks + c) % 2).then_inc(S["down_done"], 1)

                def begin():
                    pre_chunk(0, 0)
                    pre_chunk(0, 1)

                return begin, chunk, slot_work

            def result_turn(phase, g, last_g=False):
                pe.wait_ge(S["acc_copied"], g * 2 + (2 if phase == "B" else 2 * NG + 2))
                fronts = g + (FRONT0[phase] + (2 if phase == "B" else 3))
                update_turn(result_update(phase, g, last_g), FRONT0["D"] + NG if phase == "D" and last_g else fronts)

            def mlp_pre(half, c, bank):
                for m, dst, done in ((0, bank, "pre_ready"), (1, bank + 1, "up_ready")):
                    product(ps[:, dst, :], [(wfh[:, c, m, k, :], wfl[:, c, m, k, :], xh[half][:, k, :], xl[half][:, k, :])
                                            for k in range(KC)]).then_inc(S[done], 1)

            def mlp_down(half, c, slot):
                for m in range(KC):
                    step = c // 2 * 2 + m
                    last = product(ps[:, O0 + m, :], [(wfh[:, step, 2, c % 2, :], wfl[:, step, 2, c % 2, :],
                                                       hh[slot][:], hl[slot][:])], start=c == 0, stop=c == FC - 1)
                return last

            def mlp_slot(g, half, c, left, prev):
                if c == 1 and prev is not None:
                    result_turn("B", prev)
                if c == 5 and left > 0:
                    attention_turn(g + 1)
                if c == 10:
                    front(g + (FRONT0["B"] + 1), g * 2 + 2 if left > 0 else 2 * NG - 1)

            front(FRONT0["B"], 1)
            front_ready(FRONT0["B"])
            pe.wait_ge(S["dq_hi"], DQ)
            pe.wait_ge(S["dq_lo"], CREDIT + DQ)
            run_groups(pe, LEAD["B"], FC, *hidden_layer("B", FC, mlp_pre, mlp_down, mlp_slot))

            def kv_u(g, half, t):
                tk = slice(t * P, (t + 1) * P)
                product(ps[:, 2 + t % 2, :], [(xh[half][:, k, tk], xl[half][:, k, tk], wch[:, k, D:3 * D],
                                               wcl[:, k, D:3 * D]) for k in range(KC)]).then_inc(S["c_kv"], 1)
                if t >= 2:
                    pe.wait_ge(S["c_ucopied"], g * GT + (t - 1))
                elif not (isinstance(g, int) and g == 0):
                    pe.wait_ge(S["c_qlo"], g * KC + (t + 1 - KC))
                product(ps[:, t % 2, 0:D], [(xh[half][:, k, tk], xl[half][:, k, tk], wch[:, k, 3 * D:4 * D],
                                             wcl[:, k, 3 * D:4 * D]) for k in range(KC)]).then_inc(S["c_u"], 1)

            def q_projection(g, half):
                for m in range(KC):
                    pe.wait_ge(S["c_ucopied"], g * GT + (m + 3))
                    cols = slice(m * P, (m + 1) * P)
                    product(ps[:, m, :], [(wch[:, k, cols], wcl[:, k, cols], xh[half][:, k, :], xl[half][:, k, :])
                                          for k in range(KC)]).then_inc(S["c_q"], 1)

            def accumulate(b, g, half, t):
                pe.wait_ge(S["c_kvlo"], g * GT + (t + 1))
                first, final = half == 0 and t == 0, half == 1 and t == GT - 1
                if first and not (isinstance(b, int) and b == 0):
                    pe.wait_ge(S["c_masked"], b)
                for m in range(KC):
                    kc, vc = slice(m * P, (m + 1) * P), slice(D + m * P, D + (m + 1) * P)
                    last = product(ps[:, O0, m * P:(m + 1) * P],
                                   [(kvh[t % 2][:, kc], kvl[t % 2][:, kc], kvh[t % 2][:, vc], kvl[t % 2][:, vc])],
                                   start=first and m == 0, stop=final and m == KC - 1, group_check=False)
                if final:
                    last.then_inc(S["c_state"], 1)

            def attend(b, pair):
                pe.wait_ge(S["c_stlo"], b + 1)
                if not (isinstance(b, int) and b == 0 and pair == 0):
                    pe.wait_ge(S["c_ocopied"], b * (ST // 2) + pair)
                for t in (pair * 2, pair * 2 + 1):
                    for m in range(KC):
                        tk = slice(t * P, (t + 1) * P)
                        last = product(ps[:, O1, t % 2 * D + m * P:t % 2 * D + (m + 1) * P],
                                       [(qh[:, m, tk], ql[:, m, tk], stateh[:, m, :], statel[:, m, :])],
                                       group_check=False)
                last.then_inc(S["c_o"], 1)

            def output_turn(h, half, bank=T0):
                pe.wait_ge(S["c_gated"], h + 1)
                for k in range(KC):
                    for t in range(GT):
                        last = pe.transpose(ps[:, bank + k, t * P:(t + 1) * P],
                                            obuf[:, half * GT + t, k * P:(k + 1) * P], ident[:])
                last.then_inc(S["o_turned"], 1)

            def output_product(h, bank=T0):
                pe.wait_ge(S["o_hi"], h * 2 + 2)
                pe.wait_ge(S["o_lo"], CREDIT + h * 2 + 2)
                for t in range(GT):
                    tk = slice(t * P, (t + 1) * P)
                    last = product(token_major(bank)[:, t, :], [(oh[:, k, tk], ol[:, k, tk], woh[:, k, :], wol[:, k, :])
                                                                for k in range(KC)])
                last.then_inc(S["u_turned"], 1)

            def step(b, g, half, seq=None, h=None):
                first = isinstance(g, int) and g == 0
                front_ready(g + FRONT0["C"])
                kv_u(g, half, 0)
                if first:
                    result_turn("B", NG - 1, True)
                kv_u(g, half, 1)
                accumulate(b, g, half, 0)
                if seq is not None:
                    attend(seq, 0)
                if not first:
                    front(g + (FRONT0["C"] + 1), g + (UPDATE0["C"] - 3) if h is not None else UPDATE0["C"])
                kv_u(g, half, 2)
                accumulate(b, g, half, 1)
                if seq is not None:
                    attend(seq, 1)
                if h is not None:
                    pe.wait_ge(S["f_lo"], g * 2 + (FRONT0["C"] * 2 + 4))
                    output_turn(h, 1 - half)
                kv_u(g, half, 3)
                if first:
                    front(FRONT0["C"] + 1, UPDATE0["C"])
                accumulate(b, g, half, 2)
                if seq is not None:
                    attend(seq, 2)
                if h is not None:
                    output_product(h)
                if seq is not None:
                    attend(seq, 3)
                accumulate(b, g, half, 3)
                q_projection(g, half)

            pe.wait_ge(S["wc_hi"], 2)
            pe.wait_ge(S["wc_lo"], 2)
            step(0, 0, 0)
            step(0, 1, 1)
            step(1, 2, 0, seq=0)

            def phase_c(b):
                step(b, b * 2 + 1, 1, h=b * 2 - 2)
                step(b + 1, b * 2 + 2, 0, seq=b, h=b * 2 - 1)

            sequences(pe, 1, B - 2, phase_c)
            step(B - 1, NG - 1, 1, h=NG - 4)

            def router(F, half, bank=T0):
                front_ready(F)
                for t in range(GT):
                    tk = slice(t * P, (t + 1) * P)
                    last = product(ps[:, bank, t * E:(t + 1) * E], [(xh[half][:, k, tk], xl[half][:, k, tk],
                                                                     gwh[:, k, :], gwl[:, k, :]) for k in range(KC)])
                last.then_inc(S["r_scores"], 1)

            def router_turn(g, bank=T1):
                pe.wait_ge(S["r_comb"], g + 1)
                for t in range(GT):
                    last = pe.transpose(ps[0:2 * E, bank, t * P:(t + 1) * P], comb[:, t, :].bitcast(F32), ident[:])
                last.then_inc(S["r_turned"], 1)

            attend(B - 1, 0)
            attend(B - 1, 1)
            pe.wait_ge(S["c_ucopied"], NG * GT)
            pe.wait_ge(S["c_qlo"], NG * KC)
            output_turn(NG - 3, 1, G0)
            attend(B - 1, 2)
            attend(B - 1, 3)
            output_product(NG - 3, G0)
            pe.wait_ge(S["rt_hi"], 2)
            pe.wait_ge(S["rt_lo"], 2)
            router(FRONT0["D"], 0, O0)
            front(FRONT0["D"] + 1, UPDATE0["D"] - 3)
            output_turn(NG - 2, 0, G1)
            output_product(NG - 2, G1)
            pe.wait_ge(S["f_lo"], FRONT0["D"] * 2 + 4)
            output_turn(NG - 1, 1)
            pe.wait_ge(S["c_ocopied"], NT // 2)
            router_turn(0, O1)
            output_product(NG - 1)

            def expert_pre(half, c, bank):
                cols = slice(c * P, (c + 1) * P)
                product(ps[:, bank, :], [(w1h[:, k, cols], w1l[:, k, cols], xh[half][:, k, :], xl[half][:, k, :])
                                         for k in range(KC)]).then_inc(S["pre_ready"], 1)
                pe.matmul(ps[:, bank + 1, :], selr[:, cols], combT[half][:], start=True, stop=True) \
                    .then_inc(S["up_ready"], 1)

            def expert_down(half, c, slot):
                for m in range(KC):
                    cols = slice(m * P, (m + 1) * P)
                    if c == 0:
                        pe.matmul(ps[:, O0 + m, :], b2l[:, cols], combT[half][:], start=True, stop=False)
                        pe.matmul(ps[:, O0 + m, :], b2h[:, cols], combT[half][:], start=False, stop=False)
                    last = product(ps[:, O0 + m, :], [(w2h[:, c, cols], w2l[:, c, cols], hh[slot][:], hl[slot][:])],
                                   start=False, stop=c == MC - 1)
                return last

            def expert_slot(g, half, c, left, prev):
                if c == 0 and left > 0 and prev is not None:
                    front(g + (FRONT0["D"] + 1), g + (UPDATE0["D"] - 1))
                if c == 2 and left > 0:
                    if prev is None:
                        pe.wait_ge(S["u_normed"], UPDATE0["D"])
                    router(g + (FRONT0["D"] + 1), 1 - half)
                if c == 4 and left > 0:
                    router_turn(g + 1)
                if c == 5 and prev is not None:
                    if left > 0:
                        pe.wait_ge(S["r_copied"], g + 2)
                    result_turn("D", prev, left == 0)

            pe.wait_ge(S["u_normed"], UPDATE0["D"] - 1)
            pe.wait_ge(S["w1_hi"], 1)
            pe.wait_ge(S["w1_lo"], 1)
            pe.wait_ge(S["w2_hi"], 1)
            pe.wait_ge(S["w2_lo"], 1)
            pe.wait_ge(S["sel_hi"], 1)
            pe.wait_ge(S["r_copied"], 1)
            run_groups(pe, LEAD["D"], MC, *hidden_layer("D", MC, expert_pre, expert_down, expert_slot))
            result_turn("D", NG - 1, True)

        @block.scalar
        def _(act):
            def front(F, half):
                act.wait_ge(S["f_turned"], F + 1)
                for k in range(KC):
                    act.activation(xh[half][:, k, :], ps[:, T0 + k, :], ACT.Copy).then_inc(S["f_hi"], 1)

            def update(n, bank=T0, dst=ry):
                act.wait_ge(S["u_rstd"], n + 1)
                act.wait_ge(S["u_nm"], n + 1)
                act.wait_ge(S["u_added"], n)
                for t in range(GT):
                    last = act.activation(dst[:, t, :], token_major(bank)[:, t, :], ACT.Identity,
                                          bias=unm[:, t:t + 1], scale=urstd[:, t:t + 1])
                last.then_inc(S["u_normed"], 1)

            act.sem_inc(S["k_done"], CREDIT)
            act.sem_inc(S["q_done"], CREDIT)
            act.preload_act_table(ACT.Copy)
            act.wait_ge(S["wa_raw"], 16)
            act.activation(wah[:], waraw[:], ACT.Copy).then_inc(S["wa_hi"], 1)
            act.wait_ge(S["consts"], 48)
            front(0, 0)

            def phase_a(b, last_b=False):
                for half in range(2):
                    g = b * 2 + half

                    def dequant_hi(s):
                        step = g * 2 + s
                        act.wait_ge(S["dq_w"], CREDIT + step + 1)
                        act.activation(wfh[:, bass.ds(step, 1)].rearrange("p o m n c -> p (o m n c)"),
                                       weight[:].rearrange("p m n c -> p (m n c)"), ACT.Copy) \
                            .then_inc(S["dq_hi"], 1)

                    for m, n in ((0, 1), (1, 3)):
                        act.wait_ge(S["proj"], g * 6 + n)
                        act.wait_ge(S["v_done"], CREDIT + g * 2 + m)
                        act.activation(ksb[:], ps[:, 2 * m, :], ACT.Identity, bias=bq[:, 2 + m:3 + m]) \
                            .then_inc(S["k_copied"], 1)
                        act.activation(ps[:, 2 * m, :], ps[:, 2 * m, :], ACT.Square, bias=bq[:, 2 + m:3 + m],
                                       accum_out=colsum[:, bass.ds(g, 1), m]).then_inc(S["k_done"], 1)
                        if m == 0:
                            dequant_hi(0)
                    if not (last_b and half == 1):
                        front(g + 1, 1 - half)
                    else:
                        update(0, dst=ry_first)
                    for m in range(KC):
                        act.wait_ge(S["proj"], g * 6 + (5 + m))
                        act.activation(qT[:, m, bass.ds(g * GW, GW)], ps[:, 4 + m, :], ACT.Identity,
                                       bias=bq[:, m:m + 1])
                        act.activation(ps[:, 4 + m, :], ps[:, 4 + m, :], ACT.Square, bias=bq[:, m:m + 1],
                                       accum_out=colsum[:, bass.ds(g, 1), 2 + m]).then_inc(S["q_done"], 1)
                        if m == 0:
                            dequant_hi(1)

            sequences(act, 0, B - 2, phase_a)
            phase_a(B - 1, last_b=True)

            def copy_acc(g, phase, n):
                scale = FP8_UNIT * FP8_UNIT if phase == "B" else 1.0
                act.wait_ge(S["down_done"], g * FC + FC if phase == "B" else g * MC + (NG * FC + MC))
                act.wait_ge(S["u_turned"], n)
                for m in range(KC):
                    act.activation(rT[:, m, :], ps[:, O0 + m, :], ACT.Copy, scale=scale).then_inc(S["acc_copied"], 1)

            def hidden_layer(phase, chunks, func, bias, scale, slot_work):
                n0 = 0 if phase == "B" else NG * FC

                def chunk(g, half, c, left):
                    n = g * chunks + (c + n0)
                    par = (half * chunks + c) % 2
                    act.wait_ge(S["pre_ready"], n + 1)
                    act.activation(hid[par][:], ps[:, par * 2, :], func, bias=bias(c), scale=scale).then_inc(S["act_done"], 1)
                    act.wait_ge(S["hid_ready"], n + 1)
                    if not (isinstance(n, int) and n < 2):
                        act.wait_ge(S["down_done"], n - 1)
                    act.activation(hh[par][:], hid[par][:], ACT.Copy).then_inc(S["hid_hi"], 1)

                return (lambda: None), chunk, slot_work

            def mlp_slot(g, half, c, left, prev):
                if c == 0 and prev is not None:
                    copy_acc(prev, "B", prev * 2 + 2)
                if c == 4 and prev is not None:
                    update(prev * 2 + 2)
                if c == 8 and left > 0:
                    update(in_attention_update(g + 1))
                if c == 12:
                    front(g + (FRONT0["B"] + 1), 1 - half)
                if c == 14 and left == 0:
                    act.wait_ge(S["wc_raw"], 32)
                    act.activation(wch[:], wcraw[:, :, 0:4 * D], ACT.Copy).then_inc(S["wc_hi"], 1)
                    act.activation(woh[:], wcraw[:, :, 4 * D:5 * D], ACT.Copy).then_inc(S["wc_hi"], 1)

            front(FRONT0["B"], 0)
            act.preload_act_table(ACT.Gelu_apprx_tanh)
            run_groups(act, LEAD["B"], FC, *hidden_layer("B", FC, ACT.Gelu_apprx_tanh, lambda c: 0.0, FP8_UNIT, mlp_slot))
            copy_acc(NG - 1, "B", 2 * NG - 1)

            act.preload_act_table(ACT.Silu)

            def kv_u(g, t):
                act.wait_ge(S["c_kv"], g * GT + (t + 1))
                act.activation(kvh[t % 2][:, 0:D], ps[:, 2 + t % 2, 0:D], ACT.Relu)
                act.activation(kvh[t % 2][:, D:2 * D], ps[:, 2 + t % 2, D:2 * D], ACT.Copy).then_inc(S["c_kvhi"], 1)
                act.wait_ge(S["c_u"], g * GT + (t + 1))
                act.activation(us[:, bass.ds(g * GT + t, 1), :].rearrange("p o c -> p (o c)"), ps[:, t % 2, 0:D],
                               ACT.Silu).then_inc(S["c_ucopied"], 1)

            def q_hi(g, half):
                for m in range(KC):
                    act.wait_ge(S["c_q"], g * KC + (m + 1))
                    act.activation(qh[:, m, half * GW:(half + 1) * GW], ps[:, m, :], ACT.Relu).then_inc(S["c_qhi"], 1)

            def output_hi(h, bank=T0):
                act.wait_ge(S["o_turned"], h + 1)
                for k in range(KC):
                    act.activation(oh[:, k, :], ps[:, bank + k, :], ACT.Copy).then_inc(S["o_hi"], 1)

            def attend(b, pair):
                act.wait_ge(S["c_o"], b * (ST // 2) + (pair + 1))
                o = ps[:, O1, :].rearrange("p (t c) -> p t c", t=2)
                act.activation(obuf[:, pair * 2:pair * 2 + 2, :], o, ACT.Copy)
                if pair >= 2:
                    act.wait_ge(S["c_hsum"], b * 2 + 1)
                elif not (isinstance(b, int) and b == 0):
                    act.wait_ge(S["c_hsum"], b * 2)
                act.activation(sq[:, pair % 2 * 2:pair % 2 * 2 + 2, :], o, ACT.Square).then_inc(S["c_ocopied"], 1)

            def step(g, half, seq=None, h=None):
                first = isinstance(g, int) and g == 0
                kv_u(g, 0)
                kv_u(g, 1)
                if seq is not None:
                    attend(seq, 0)
                if first:
                    update(2 * NG - 1)
                else:
                    front(g + (FRONT0["C"] + 1), 1 - half)
                kv_u(g, 2)
                if seq is not None:
                    attend(seq, 1)
                if h is not None:
                    output_hi(h)
                kv_u(g, 3)
                if first:
                    front(FRONT0["C"] + 1, 1)
                if seq is not None:
                    attend(seq, 2)
                    attend(seq, 3)
                q_hi(g, half)
                if h is not None:
                    update(h + UPDATE0["C"])

            step(0, 0)
            step(1, 1)
            step(2, 0, seq=0)

            def phase_c(b):
                step(b * 2 + 1, 1, h=b * 2 - 2)
                step(b * 2 + 2, 0, seq=b, h=b * 2 - 1)

            sequences(act, 1, B - 2, phase_c)
            step(NG - 1, 1, h=NG - 4)

            def gates(g, half, bank=T1):
                act.wait_ge(S["r_turned"], g + 1)
                act.activation(combT[half][:], ps[0:2 * E, bank, :], ACT.Copy).then_inc(S["r_copied"], 1)

            def expert_slot(g, half, c, left, prev):
                if c == 0 and prev is not None:
                    copy_acc(prev, "D", prev + UPDATE0["D"])
                if c == 2 and left > 0 and prev is not None:
                    front(g + (FRONT0["D"] + 1), 1 - half)
                if c == 6 and left > 0:
                    gates(g + 1, 1 - half)
                if c == 8 and prev is not None:
                    update(prev + UPDATE0["D"])

            act.wait_ge(S["wd_raw"], 112)
            for hi, raw in ((gwh, gw), (b2h, b2s)):
                act.activation(hi[:], raw[:], ACT.Copy).then_inc(S["rt_hi"], 1)
            attend(B - 1, 0)
            attend(B - 1, 1)
            output_hi(NG - 3, G0)
            attend(B - 1, 2)
            attend(B - 1, 3)
            act.activation(w1h[:], w1raw[:], ACT.Copy).then_inc(S["w1_hi"], 1)
            update(NG - 3 + UPDATE0["C"], G0)
            front(FRONT0["D"] + 1, 1)
            output_hi(NG - 2, G1)
            act.wait_ge(S["c_gated"], NG - 2)
            act.activation(w2h[:], w2raw[:], ACT.Copy).then_inc(S["w2_hi"], 1)
            output_hi(NG - 1)
            gates(0, 0, O1)
            update(NG - 2 + UPDATE0["C"], G1)
            act.wait_ge(S["sel_raw"], 16)
            act.activation(selr[:], sel[:], ACT.Copy).then_inc(S["sel_hi"], 1)
            update(NG - 1 + UPDATE0["C"])
            run_groups(act, LEAD["D"], MC, *hidden_layer("D", MC, ACT.Silu, lambda c: b1s[:, c:c + 1], 1.0, expert_slot))
            copy_acc(NG - 1, "D", NG - 1 + UPDATE0["D"])
            update(NG - 1 + UPDATE0["D"])

        @block.vector
        def _(dve):
            dve.memset(neghalf[:], -0.5).then_inc(S["half_ready"], 1)
            dve.sem_inc(S["v_done"], CREDIT)
            dve.sem_inc(S["o_lo"], CREDIT)

            def front_stats(F, g, updates):
                dve.wait_ge(S["u_added"], updates)
                apart(dve)
                for t in range(GT):
                    last = dve.bn_stats(fstats[:, t, :], x[:, bass.ds(g * GT + t, 1), :].rearrange("p o c -> p (o c)"))
                last.then_inc(S["f_stats"], 1)
                dve.wait_ge(S["f_stats"], F + 1)
                apart(dve)
                for t in range(GT):
                    last = dve.bn_aggr(fmv[:, t, :], fstats[:, t, :])
                last.then_inc(S["f_mv"], 1)

            def front_norm(F, g):
                dve.wait_ge(S["f_rstd"], F + 1)
                dve.wait_ge(S["f_turned"], F)
                for t in range(GT):
                    last = dve.tensor_scalar(xn[:, t, :], x[:, bass.ds(g * GT + t, 1), :].rearrange("p o c -> p (o c)"),
                                             fmv[:, t, 0:1], frstd[:, t:t + 1], ALU.subtract, ALU.mult)
                last.then_inc(S["f_xn"], 1)

            def front_lo(F, half):
                for k in range(KC):
                    dve.wait_ge(S["f_hi"], F * 2 + (k + 1))
                    dve.tensor_tensor(xl[half][:, k, :], ps[:, T0 + k, :], xh[half][:, k, :].bitcast(F32),
                                      ALU.subtract).then_inc(S["f_lo"], 1)

            def update_stats(n, bank=T0):
                dve.wait_ge(S["u_turned"], n + 1)
                apart(dve)
                for t in range(GT):
                    last = dve.bn_stats(ustats[:, t, :], token_major(bank)[:, t, :])
                last.then_inc(S["u_stats"], 1)
                dve.wait_ge(S["u_stats"], n + 1)
                if not (isinstance(n, int) and n == 0):
                    dve.wait_ge(S["u_nm"], n)
                apart(dve)
                for t in range(GT):
                    last = dve.bn_aggr(umv[:, t, :], ustats[:, t, :])
                last.then_inc(S["u_mv"], 1)

            def scale(g, n, dst=rT):
                dve.wait_ge(S["u_turned"], n)
                for m in range(KC):
                    last = dve.tensor_scalar(dst[:, m, :], qT[:, m, bass.ds(g * GW, GW)],
                                             colc[:, bass.ds(g, 1), m], None, ALU.mult)
                last.then_inc(S["u_scaled"], 1)

            def column_totals(b0, b1):
                dve.wait_ge(S["k_done"], CREDIT + 4 * b1)
                dve.wait_ge(S["q_done"], CREDIT + 4 * b1)
                dve.wait_ge(S["v_done"], CREDIT + 4 * b1)
                sums = colsum[:].rearrange("p (b h) s -> p b h s", h=2)[:, b0:b1]
                dve.tensor_tensor(coltot[:, b0:b1], sums[:, :, 0, :], sums[:, :, 1, :], ALU.add).then_inc(S["col_tot"], 1)

            def column_factors(b0, b1, done):
                dve.wait_ge(S["col_tot"], done)
                dve.wait_ge(S["col_rn"], done)
                dve.tensor_tensor(colkv[:, b0:b1], coltot[:, b0:b1, 4:6], colrn[:, b0:b1, 0:2], ALU.mult) \
                    .then_inc(S["col_c0"], 1)
                dve.wait_ge(S["col_c0"], done)
                factor = colc[:].rearrange("p (b h) c -> p b h c", h=2)[:, b0:b1]
                for half in range(2):
                    dve.tensor_tensor(factor[:, :, half, :], colkv[:, b0:b1], colrn[:, b0:b1, 2:4], ALU.mult) \
                        .then_inc(S["col_c"], 1)
                dve.wait_ge(S["col_c"], done * 2)

            dve.wait_ge(S["x_even"], 16)
            front_stats(0, 0, 0)
            front_norm(0, 0)
            dve.wait_ge(S["wa_hi"], 1)
            dve.tensor_tensor(wal[:], waraw[:], wah[:].bitcast(F32), ALU.subtract).then_inc(S["wa_lo"], 1)
            dve.wait_ge(S["consts"], 48)
            front_lo(0, 0)

            def phase_a(b, last_b=False):
                for half in range(2):
                    g = b * 2 + half

                    def codes(s):
                        step = g * 2 + s
                        f0 = step * 4
                        dve.wait_ge(pk_loaded[s], g * 16 + 16)
                        dve.tensor_scalar(field[:], pk[s][:], 0xF0, 4, ALU.bitwise_and, ALU.logical_shift_left) \
                            .then_inc(S["dq_f"], 1)
                        dve.wait_ge(S["dq_f"], f0 + 1)
                        dve.wait_ge(S["dq_w"], CREDIT + step)
                        dve.scalar_tensor_tensor(code[:], pk[s][:], 0x0F, field[:], ALU.bitwise_and, ALU.bitwise_or) \
                            .then_inc(S["dq_f"], 1)
                        dve.wait_ge(S["dq_f"], f0 + 2)
                        dve.tensor_scalar(field[:], code[:], 0x707, 2, ALU.bitwise_and, ALU.logical_shift_left) \
                            .then_inc(S["dq_f"], 1)
                        dve.tensor_scalar(code[:], code[:], 0x808, 4, ALU.bitwise_and, ALU.logical_shift_left) \
                            .then_inc(S["dq_f"], 1)
                        dve.wait_ge(S["dq_f"], f0 + 4)
                        dve.tensor_tensor(code[:], code[:], field[:], ALU.bitwise_or).then_inc(S["dq_code"], 1)

                    front_next = not (last_b and half == 1)
                    if front_next:
                        gn = g + 1
                        dve.wait_ge(x_loaded[1 - half], (b + half) * 16 + 16)
                        front_stats(gn, gn, 0)
                    codes(0)
                    dve.wait_ge(S["proj"], g * 6 + 2)
                    dve.wait_ge(S["k_copied"], g * 2 + 1)

                    def v_sum(m):
                        dve.scalar_tensor_tensor(ps[:, 1 + 2 * m, :], ps[:, 1 + 2 * m, :], bq[:, 4 + m:5 + m], ksb[:],
                                                 ALU.add, ALU.mult, accum_out=colsum[:, bass.ds(g, 1), 4 + m]) \
                            .then_inc(S["v_done"], 1)

                    v_sum(0)
                    if front_next:
                        front_norm(gn, gn)
                    dve.wait_ge(S["proj"], g * 6 + 4)
                    dve.wait_ge(S["k_copied"], g * 2 + 2)
                    v_sum(1)
                    if front_next:
                        front_lo(gn, 1 - half)
                    else:
                        update_stats(0)
                    codes(1)
                    if last_b and half == 0:
                        column_totals(0, 1)
                        column_factors(0, 1, 1)
                        dve.wait_ge(S["proj"], 42)
                        scale(0, 0, rT_first)

            sequences(dve, 0, B - 2, phase_a)
            phase_a(B - 1, last_b=True)

            column_totals(1, B)
            def hidden_layer(phase, chunks, slot_work):
                n0 = 0 if phase == "B" else NG * FC

                def chunk(g, half, c, left):
                    n = g * chunks + (c + n0)
                    par = (half * chunks + c) % 2
                    dve.wait_ge(S["act_done"], n + 1)
                    dve.wait_ge(S["up_ready"], n + 1)
                    dve.tensor_tensor(hid[par][:], hid[par][:], ps[:, par * 2 + 1, :], ALU.mult) \
                        .then_inc(S["hid_ready"], 1)
                    dve.wait_ge(S["hid_hi"], n + 1)
                    dve.tensor_tensor(hl[par][:], hid[par][:], hh[par][:].bitcast(F32), ALU.subtract) \
                        .then_inc(S["hid_lo"], 1)

                return (lambda: None), chunk, slot_work

            def mlp_slot(g, half, c, left, prev):
                if c == 2 and prev is None:
                    column_factors(1, B, 2)
                if c == 3 and prev is not None:
                    update_stats(prev * 2 + 2)
                if left > 0:
                    n = g * 2 + 1
                    if c == 5:
                        scale(g + 1, n)
                    if c == 7:
                        update_stats(n)
                if c == 9:
                    if left > 0:
                        front_stats(g + (FRONT0["B"] + 1), g + 1, g * 2 + 2)
                    else:
                        front_stats(FRONT0["C"], 0, 2 * NG - 1)
                if c == 10:
                    front_norm(g + (FRONT0["B"] + 1), g + 1 if left > 0 else 0)
                if c == 12:
                    front_lo(g + (FRONT0["B"] + 1), 1 - half)
                if c == 13 and left == 0:
                    front_stats(FRONT0["C"] + 1, 1, 2 * NG - 1)
                if c == 14 and left == 0:
                    front_norm(FRONT0["C"] + 1, 1)
                if c == 15 and left == 0:
                    dve.wait_ge(S["wc_hi"], 2)
                    dve.tensor_tensor(wcl[:], wcraw[:, :, 0:4 * D], wch[:].bitcast(F32), ALU.subtract) \
                        .then_inc(S["wc_lo"], 1)
                    dve.tensor_tensor(wol[:], wcraw[:, :, 4 * D:5 * D], woh[:].bitcast(F32), ALU.subtract) \
                        .then_inc(S["wc_lo"], 1)

            front_stats(FRONT0["B"], 0, 1)
            front_norm(FRONT0["B"], 0)
            front_lo(FRONT0["B"], 0)
            run_groups(dve, LEAD["B"], FC, *hidden_layer("B", FC, mlp_slot))

            def kv_lo(g, t):
                dve.wait_ge(S["c_kvhi"], g * GT + (t + 1))
                dve.scalar_tensor_tensor(kvl[t % 2][:, 0:D], ps[:, 2 + t % 2, 0:D], 0.0,
                                         kvh[t % 2][:, 0:D].bitcast(F32), ALU.max, ALU.subtract)
                dve.tensor_tensor(kvl[t % 2][:, D:2 * D], ps[:, 2 + t % 2, D:2 * D],
                                  kvh[t % 2][:, D:2 * D].bitcast(F32), ALU.subtract).then_inc(S["c_kvlo"], 1)

            def q_lo(g, half):
                for m in range(KC):
                    dve.wait_ge(S["c_qhi"], g * KC + (m + 1))
                    dve.scalar_tensor_tensor(ql[:, m, half * GW:(half + 1) * GW], ps[:, m, :], 0.0,
                                             qh[:, m, half * GW:(half + 1) * GW].bitcast(F32), ALU.max, ALU.subtract) \
                        .then_inc(S["c_qlo"], 1)

            def gate(h, half):
                heads = obuf[:, half * GT:(half + 1) * GT, :].rearrange("p t (h d) -> p (t h) d", d=HD)
                rstd = hrstd[:, half * GT * NH:(half + 1) * GT * NH].unsqueeze(2).to_broadcast([P, GT * NH, HD])
                dve.tensor_tensor(heads, heads, rstd, ALU.mult).then_inc(S["c_scaled"], 1)

            def output_lo(h, bank=T0):
                for k in range(KC):
                    dve.wait_ge(S["o_hi"], h * 2 + (k + 1))
                    dve.tensor_tensor(ol[:, k, :], ps[:, bank + k, :], oh[:, k, :].bitcast(F32), ALU.subtract) \
                        .then_inc(S["o_lo"], 1)

            def mask_state(b):
                dve.wait_ge(S["c_state"], b + 1)
                for m in range(KC):
                    last = dve.scalar_tensor_tensor(state[:, m, :], ps[:, O0, m * P:(m + 1) * P], 1.0 / HD, mask[:],
                                                    ALU.mult, ALU.mult)
                last.then_inc(S["c_masked"], 1)
                dve.wait_ge(S["c_masked"], b + 1)
                dve.tensor_copy(stateh[:], state[:]).then_inc(S["c_sthi"], 1)
                dve.wait_ge(S["c_sthi"], b + 1)
                dve.tensor_tensor(statel[:], state[:], stateh[:].bitcast(F32), ALU.subtract).then_inc(S["c_stlo"], 1)

            def head_sums(b, half):
                dve.wait_ge(S["c_ocopied"], b * (ST // 2) + (half * 2 + 2))
                dve.tensor_reduce(hsum[:, half * GT * NH:(half + 1) * GT * NH],
                                  sq[:].rearrange("p t (h d) -> p (t h) d", d=HD),
                                  AX_X, ALU.add).then_inc(S["c_hsum"], 1)

            def head_rstd(b):
                links = 3 + 3 * NEWTON
                k = [0]

                def link(ins):
                    k[0] += 1
                    ins.then_inc(S["c_hrstd"], 1)
                    dve.wait_ge(S["c_hrstd"], b * links + k[0])

                dve.wait_ge(S["c_hsum"], b * 2 + 2)
                link(dve.tensor_scalar(hsum[:], hsum[:], 1.0 / HD, 1e-24, ALU.mult, ALU.max))
                guess = hrstd[:].bitcast(I32)
                link(dve.tensor_scalar(guess, hsum[:].bitcast(I32), 1, None, ALU.logical_shift_right))
                link(dve.tensor_scalar(guess, guess, -1.0, float(0x5F3759DF), ALU.mult, ALU.add))
                for _ in range(NEWTON):
                    link(dve.tensor_tensor(hwork[:], hrstd[:], hrstd[:], ALU.mult))
                    link(dve.scalar_tensor_tensor(hwork[:], hwork[:], -0.5, hsum[:], ALU.mult, ALU.mult))
                    link(dve.scalar_tensor_tensor(hrstd[:], hwork[:], 1.5, hrstd[:], ALU.add, ALU.mult))
                assert k[0] == links

            def step(g, half, seq=None, h=None):
                first = isinstance(g, int) and g == 0
                F = g + (FRONT0["C"] + 1)
                gx = 0 if isinstance(g, int) and g == NG - 1 else g + 1
                if not first:
                    front_stats(F, gx, UPDATE0["C"] + 1 if isinstance(g, int) and g == NG - 1 else UPDATE0["C"])
                if seq is not None and half == 0:
                    mask_state(seq)
                kv_lo(g, 0)
                if first:
                    update_stats(2 * NG - 1)
                if seq is not None and half == 1:
                    head_rstd(seq)
                if not first:
                    front_norm(F, gx)
                if h is not None:
                    gate(h, 1 - half)
                kv_lo(g, 1)
                if not first:
                    front_lo(F, 1 - half)
                kv_lo(g, 2)
                if h is not None:
                    output_lo(h)
                kv_lo(g, 3)
                if first:
                    front_lo(F, 1)
                if seq is not None and half == 0:
                    head_sums(seq, 0)
                if h is not None:
                    update_stats(h + UPDATE0["C"])
                q_lo(g, half)
                if seq is not None and half == 0:
                    head_sums(seq, 1)

            dve.wait_ge(S["consts"], 64)
            step(0, 0)
            step(1, 1)
            step(2, 0, seq=0)

            def phase_c(b):
                step(b * 2 + 1, 1, seq=b - 1, h=b * 2 - 2)
                step(b * 2 + 2, 0, seq=b, h=b * 2 - 1)

            sequences(dve, 1, B - 2, phase_c)
            step(NG - 1, 1, seq=B - 2, h=NG - 4)

            RC = 9

            def linker(g, k):
                def link(ins):
                    k[0] += 1
                    ins.then_inc(S["r_chain"], 1)
                    dve.wait_ge(S["r_chain"], g * RC + k[0])
                return link

            def pick(g, bank=T0):
                link = linker(g, [0])
                dve.wait_ge(S["r_scores"], g + 1)
                dve.tensor_tensor(score[:], ps[:, bank, 0:GT * E].rearrange("p (t e) -> p t e", e=E),
                                  gbs[:].unsqueeze(1).to_broadcast([P, GT, E]), ALU.add).then_inc(S["r_scored"], 1)
                dve.wait_ge(S["r_scored"], g + 1)
                apart(dve)
                for t in range(GT):
                    last = dve.max(best[:, t, :], score[:, t, :])
                last.then_inc(S["r_best"], 1)
                dve.wait_ge(S["r_best"], g + 1)
                apart(dve)
                for t in range(GT):
                    last = dve.max_index(besti[:, t, :], best[:, t, :], score[:, t, :])
                last.then_inc(S["r_found"], 1)
                dve.tensor_tensor(gap[:], best[:, :, 1], best[:, :, 0], ALU.subtract).then_inc(S["r_gap"], 1)
                dve.wait_ge(S["r_found"], g + 1)
                link(dve.tensor_copy(bestf[:], besti[:]))
                rows = iota[:].unsqueeze(1).to_broadcast([P, GT, E])
                link(dve.tensor_tensor(pick1[:], rows, bestf[:, :, 0:1].to_broadcast([P, GT, E]), ALU.is_equal))
                link(dve.tensor_tensor(pick2[:], rows, bestf[:, :, 1:2].to_broadcast([P, GT, E]), ALU.is_equal))

            def combine(g):
                k = [3]
                link = linker(g, k)
                dve.wait_ge(S["r_second"], g + 1)
                link(dve.tensor_scalar(denom[:], second[:], 1.0, None, ALU.add))
                link(dve.reciprocal(gate1[:], denom[:]))
                link(dve.tensor_tensor(gate2[:], gate1[:], second[:], ALU.mult))
                link(dve.tensor_tensor(pick1[:], pick1[:], gate1[:].unsqueeze(2).to_broadcast([P, GT, E]), ALU.mult))
                link(dve.tensor_tensor(pick2[:], pick2[:], gate2[:].unsqueeze(2).to_broadcast([P, GT, E]), ALU.mult))
                link(dve.tensor_tensor(pick1[:], pick1[:], pick2[:], ALU.add))
                assert k[0] == RC
                dve.tensor_copy(comb[:, :, 0:E], pick1[:]).then_inc(S["r_comb_hi"], 1)
                dve.wait_ge(S["r_comb_hi"], g + 1)
                dve.tensor_tensor(comb[:, :, E:2 * E], pick1[:], comb[:, :, 0:E].bitcast(F32), ALU.subtract) \
                    .then_inc(S["r_comb"], 1)

            dve.wait_ge(S["rt_hi"], 2)
            for lo, raw, hi in ((gwl, gw, gwh), (b2l, b2s, b2h)):
                dve.tensor_tensor(lo[:], raw[:], hi[:].bitcast(F32), ALU.subtract).then_inc(S["rt_lo"], 1)
            dve.tensor_tensor(gbs[:], gb[:, 0, :], gb[:, 1, :], ALU.add).then_inc(S["r_bias"], 1)
            mask_state(B - 1)
            gate(NG - 3, 1)
            front_stats(FRONT0["D"] + 1, 1, UPDATE0["C"] + 2)
            output_lo(NG - 3, G0)
            head_sums(B - 1, 0)
            front_norm(FRONT0["D"] + 1, 1)
            update_stats(NG - 3 + UPDATE0["C"], G0)
            head_sums(B - 1, 1)
            head_rstd(B - 1)
            gate(NG - 2, 0)
            gate(NG - 1, 1)
            dve.wait_ge(S["r_bias"], 1)
            dve.wait_ge(S["r_consts"], E + 1)
            pick(0, O0)
            front_lo(FRONT0["D"] + 1, 1)
            combine(0)
            output_lo(NG - 2, G1)
            dve.wait_ge(S["w1_hi"], 1)
            dve.tensor_tensor(w1l[:], w1raw[:], w1h[:].bitcast(F32), ALU.subtract).then_inc(S["w1_lo"], 1)
            update_stats(NG - 2 + UPDATE0["C"], G1)
            dve.wait_ge(S["w2_hi"], 1)
            dve.tensor_tensor(w2l[:], w2raw[:], w2h[:].bitcast(F32), ALU.subtract).then_inc(S["w2_lo"], 1)
            output_lo(NG - 1)
            update_stats(NG - 1 + UPDATE0["C"])

            def expert_slot(g, half, c, left, prev):
                if c == 2 and left > 0 and prev is not None:
                    front_lo(g + (FRONT0["D"] + 1), 1 - half)
                if c == 4 and left > 0:
                    pick(g + 1)
                if c == 5 and left > 0:
                    combine(g + 1)
                if c == 7 and prev is not None:
                    update_stats(prev + UPDATE0["D"])
                if c == 9 and left > 1:
                    front_stats(g + (FRONT0["D"] + 2), g + 2, g + (UPDATE0["C"] + 3))
                if c == 10 and left > 1:
                    front_norm(g + (FRONT0["D"] + 2), g + 2)

            run_groups(dve, LEAD["D"], MC, *hidden_layer("D", MC, expert_slot))
            update_stats(NG - 1 + UPDATE0["D"])

        @block.gpsimd
        def _(pool):
            pool.sem_inc(S["dq_w"], CREDIT)
            pool.sem_inc(S["dq_lo"], CREDIT)
            pool.wait_ge(S["half_ready"], 1)

            def front(F):
                pool.wait_ge(S["f_mv"], F + 1)
                pool.wait_ge(S["f_xn"], F)
                apart(pool)
                pool.tensor_scalar(fvar[:], fmv[:, :, 1], EPS, None, ALU.add).then_inc(S["f_var"], 1)
                pool.wait_ge(S["f_var"], F + 1)
                pool.tensor_tensor(frstd[:], fvar[:], neghalf[:, 0:GT], ALU.pow).then_inc(S["f_rstd"], 1)

            def update(n, g, result=ry):
                pool.wait_ge(S["u_mv"], n + 1)
                apart(pool)
                pool.tensor_scalar(uvar[:], umv[:, :, 1], EPS, None, ALU.add).then_inc(S["u_var"], 1)
                pool.tensor_scalar(unm[:], umv[:, :, 0], -1.0, None, ALU.mult).then_inc(S["u_neg"], 1)
                pool.wait_ge(S["u_var"], n + 1)
                pool.tensor_tensor(urstd[:], uvar[:], neghalf[:, 0:GT], ALU.pow).then_inc(S["u_rstd"], 1)
                pool.wait_ge(S["u_neg"], n + 1)
                pool.wait_ge(S["u_rstd"], n + 1)
                pool.tensor_tensor(unm[:], unm[:], urstd[:], ALU.mult).then_inc(S["u_nm"], 1)
                pool.wait_ge(S["u_normed"], n + 1)
                apart(pool)
                xg = x[:, bass.ds(g * GT, GT), :]
                pool.tensor_tensor(xg, xg, result[:], ALU.add).then_inc(S["u_added"], 1)

            def column_rn(b0, b1, done):
                pool.wait_ge(S["col_tot"], done)
                pool.tensor_tensor(colrn[:, b0:b1], coltot[:, b0:b1, 0:4],
                                   neghalf[:, 0:4 * (b1 - b0)].rearrange("p (b s) -> p b s", s=4),
                                   ALU.pow).then_inc(S["col_rn"], 1)

            front(0)

            def phase_a(b, last_b=False):
                for half in range(2):
                    g = b * 2 + half
                    if not (last_b and half == 1):
                        front(g + 1)
                    for s in range(2):
                        if last_b and half == 1 and s == 1:
                            update(0, 0, ry_first)
                        step = g * 2 + s
                        pool.wait_ge(S["dq_code"], step + 1)
                        pool.wait_ge(sc_loaded[s], g * 16 + 16)
                        pool.wait_ge(S["dq_lo"], CREDIT + step)
                        apart(pool)
                        low = code[:].bitcast(FP8).rearrange("p m (c e) -> p m e c", e=4)
                        for nib in range(2):
                            last = pool.tensor_tensor(weight[:, :, nib, :], low[:, :, nib, :], sc[s][:], ALU.mult)
                        last.then_inc(S["dq_w"], 1)
                        pool.wait_ge(S["dq_hi"], step + 1)
                        pool.tensor_tensor(wfl[:, bass.ds(step, 1)].rearrange("p o m n c -> p (o m n c)"),
                                           weight[:].rearrange("p m n c -> p (m n c)"),
                                           wfh[:, bass.ds(step, 1)].bitcast(F32).rearrange("p o m n c -> p (o m n c)"),
                                           ALU.subtract).then_inc(S["dq_lo"], 1)
                    if last_b and half == 0:
                        column_rn(0, 1, 1)

            sequences(pool, 0, B - 2, phase_a)
            phase_a(B - 1, last_b=True)
            front(FRONT0["B"])
            column_rn(1, B, 2)

            def phase_b(b, last_b=False):
                for half in range(2):
                    g = b * 2 + half
                    last_g = last_b and half == 1
                    if not last_g:
                        update(g * 2 + 1, g + 1)
                    front(g + (FRONT0["B"] + 1))
                    if last_g:
                        front(FRONT0["C"] + 1)
                    update(2 * NG - 1 if last_g else g * 2 + 2, g)

            sequences(pool, 0, B - 2, phase_b)
            phase_b(B - 1, last_b=True)

            pool.wait_ge(S["wc_lo"], 2)
            for e in range(E):
                pool.memset(iota[:, e:e + 1], float(e)).then_inc(S["r_consts"], 1)
            pool.memset(ebase[:], E_BASE).then_inc(S["r_consts"], 1)

            def gate(h, half):
                o = obuf[:, half * GT:(half + 1) * GT, :]
                pool.wait_ge(S["c_scaled"], h + 1)
                apart(pool)
                pool.tensor_tensor(o, o, us[:, bass.ds(h * GT, GT), :], ALU.mult).then_inc(S["c_gated"], 1)

            def step(g, h, half):
                front(g + (FRONT0["C"] + 1))
                gate(h, half)
                update(h + UPDATE0["C"], h)

            front(FRONT0["C"] + 2)
            front(FRONT0["C"] + 3)

            def phase_c(b):
                step(b * 2 + 1, b * 2 - 2, 0)
                step(b * 2 + 2, b * 2 - 1, 1)

            sequences(pool, 1, B - 2, phase_c)
            step(NG - 1, NG - 4, 0)

            def second_gate(g):
                pool.wait_ge(S["r_gap"], g + 1)
                pool.tensor_tensor(second[:], ebase[:], gap[:], ALU.pow).then_inc(S["r_second"], 1)

            pool.wait_ge(S["r_consts"], E + 1)
            gate(NG - 3, 1)
            front(FRONT0["D"] + 1)
            update(UPDATE0["C"] + NG - 3, NG - 3)
            gate(NG - 2, 0)
            second_gate(0)
            gate(NG - 1, 1)
            update(UPDATE0["C"] + NG - 2, NG - 2)
            update(UPDATE0["C"] + NG - 1, NG - 1)
            second_gate(1)

            def phase_d(b, last_b=False):
                for half in range(2):
                    g = b * 2 + half
                    if not last_b:
                        front(g + (FRONT0["D"] + 2))
                        second_gate(g + 2)
                    update(g + UPDATE0["D"], g)

            sequences(pool, 0, B - 2, phase_d)
            phase_d(B - 1, last_b=True)


def kernel(L0_attn_x, L0_attn_W, L0_attn_b, L0_ffn_gate_W_packed, L0_ffn_gate_scales, L0_ffn_up_W_packed,
           L0_ffn_up_scales, L0_ffn_down_W_packed, L0_ffn_down_scales, L1_attn_Wq, L1_attn_Wk, L1_attn_Wv, L1_attn_Wu,
           L1_attn_Wo, L1_ffn_gate_w, L1_ffn_gate_b, L1_ffn_bias, L1_ffn_w1, L1_ffn_b1, L1_ffn_w2, L1_ffn_b2):
    import numpy as np
    import concourse.bacc as bacc
    from concourse.bass_utils import run_bass_kernel_spmd

    a = np.asarray

    def in_rows(w):
        return a(w).reshape(P, KC, -1)

    def pack_in(w, t):
        return a(w).reshape(FC // 2, P, 2, t).transpose(0, 2, 3, 1).reshape(FC, t, P)

    def pack_down(w, t):
        return a(w).reshape(P, KC, FC // 2, t).transpose(2, 1, 3, 0).reshape(FC, t, P)

    packed = np.stack([pack_in(L0_ffn_gate_W_packed, P), pack_in(L0_ffn_up_W_packed, P),
                       pack_down(L0_ffn_down_W_packed, P)], axis=2).reshape(FC, P, 3 * P)
    scales = np.stack([pack_in(L0_ffn_gate_scales, 8), pack_in(L0_ffn_up_scales, 8),
                       pack_down(L0_ffn_down_scales, 8)], axis=2).reshape(FC * 8, 3 * P)
    arrays = {
        "x_in": a(L0_attn_x).reshape(NT, P, P, KC).transpose(0, 1, 3, 2).reshape(NT, P, D),
        "wqkv": a(L0_attn_W).reshape(P, KC, 3, P, KC).transpose(0, 1, 2, 4, 3).reshape(P, KC, 3 * D),
        "bqkv": a(L0_attn_b).reshape(3, P, KC).transpose(1, 0, 2).reshape(P, 6),
        "packed": packed,
        "scales": scales,
        "wl1": np.concatenate([in_rows(w) for w in (L1_attn_Wq, L1_attn_Wk, L1_attn_Wv, L1_attn_Wu)], axis=2),
        "wo": a(L1_attn_Wo).reshape(KC, P, P, KC).transpose(1, 0, 3, 2).reshape(P, KC, D),
        "w1": a(L1_ffn_w1).reshape(MH, P, KC).transpose(1, 2, 0),
        "b1": a(L1_ffn_b1).reshape(MC, P).T,
        "w2": a(L1_ffn_w2).transpose(0, 2, 1).reshape(MC, P, P, KC).transpose(1, 0, 3, 2).reshape(P, MC, D),
        "b2": a(L1_ffn_b2).reshape(E, P, KC).transpose(0, 2, 1).reshape(E, D),
        "gate_w": a(L1_ffn_gate_w).reshape(E, P, KC).transpose(1, 2, 0),
        "gate_b": a(L1_ffn_gate_b),
        "gate_bias": a(L1_ffn_bias),
        "ident_in": np.eye(P, dtype=np.float32),
        "mask_in": np.kron(np.eye(P // HD), np.ones((HD, HD))).astype(np.float32),
        "sel_in": np.tile(np.repeat(np.eye(E), EH, axis=1), (2, 1)).astype(np.float32),
    }
    nc = bacc.Bacc("TRN2", target_bir_lowering=False, num_devices=1)
    arrays = {n: np.ascontiguousarray(v) for n, v in arrays.items()}
    args = [nc.dram_tensor(n, v.shape, mybir.dt.from_np(v.dtype), kind="ExternalInput").ap() for n, v in arrays.items()]
    out = nc.dram_tensor("out", (NT, P, D), F32, kind="ExternalOutput").ap()
    build_program(nc, *args, out)
    r = run_bass_kernel_spmd(nc, [arrays], core_ids=[0])
    got = r.results[0]["out"]
    return got.reshape(B, TOK // B, KC, P).transpose(0, 1, 3, 2).reshape(B, TOK // B, D)
```

```python
from contextlib import ExitStack

import concourse.bass as bass
from concourse import mybir

ALU = mybir.AluOpType
ACT = mybir.ActivationFunctionType
AX_X = mybir.AxisListType.X
F32 = mybir.dt.float32
F32R = mybir.dt.float32r
I32 = mybir.dt.int32
U32 = mybir.dt.uint32
FP8 = mybir.dt.float8e4

P = 128
D = 256
KC = D // P
B = 4
TOK = 4 * 1024
NT = TOK // P
GT = 4
GW = GT * P
NG = NT // GT
ST = NT // B
MLP = 2048
FC = MLP // P
E, EH = 8, 176
MH = E * EH
MC = MH // P
HD = 16
NH = D // HD
EPS = 1e-5
CREDIT = 1
NEWTON = 3
HEAD_OPS = 3 + 3 * NEWTON
assert HEAD_OPS == 12
E_BASE = 2.718281828459045
FP8_UNIT = 64.0

FRONT0 = {"A": 0, "B": NG, "C": 2 * NG, "D": 3 * NG}
UPDATE0 = {"B": 0, "C": 2 * NG, "D": 3 * NG}
G0, U0, G1, U1, O0, O1, T0, T1 = range(8)
DQ = FC
LEAD = {"B": 5, "D": 9}


def in_attention_update(g):
    return 0 if isinstance(g, int) and g == 0 else g * 2 - 1


def result_update(phase, g, last_g):
    if phase == "D":
        return g + UPDATE0["D"]
    return 2 * NG - 1 if last_g else g * 2 + 2


def build_program(nc, x_in, wqkv, bqkv, packed, scales, wl1, wo, w1, b1, w2, b2, gate_w, gate_b, gate_bias,
                  ident_in, mask_in, sel_in, out):
    with ExitStack() as ctx:
        def place(name, shape, dt, at):
            at = (at + 31) // 32 * 32
            size = 4
            for n in shape[1:]:
                size *= n
            assert at + size <= nc.sbuf_usable_end, (name, at + size)
            return nc.alloc_sbuf_tensor_at(name, shape, dt, offset=at), at + size

        top = nc.sbuf_base
        x, top = place("x", [P, NT, D], F32, top)
        xn, top = place("xn", [P, GT, D], F32, top)
        xh0, top = place("xh0", [P, KC, GW], F32R, top)
        xh1, top = place("xh1", [P, KC, GW], F32R, top)
        xl0, top = place("xl0", [P, KC, GW], F32R, top)
        xl1, top = place("xl1", [P, KC, GW], F32R, top)
        xh, xl = (xh0, xh1), (xl0, xl1)
        ident, top = place("ident", [P, P], F32, top)
        fstats, top = place("fstats", [P, GT, 6], F32, top)
        fmv, top = place("fmv", [P, GT, 2], F32, top)
        fvar, top = place("fvar", [P, GT], F32, top)
        frstd, top = place("frstd", [P, GT], F32, top)
        ustats, top = place("ustats", [P, GT, 6], F32, top)
        umv, top = place("umv", [P, GT, 2], F32, top)
        uvar, top = place("uvar", [P, GT], F32, top)
        urstd, top = place("urstd", [P, GT], F32, top)
        unm, top = place("unm", [P, GT], F32, top)
        neghalf, top = place("neghalf", [P, 64], F32, top)
        colsum, top = place("colsum", [P, NG, 6], F32, top)
        coltot, top = place("coltot", [P, B, 6], F32, top)
        colrn, top = place("colrn", [P, B, 4], F32, top)
        colkv, top = place("colkv", [P, B, 2], F32, top)
        colc, top = place("colc", [P, NG, 2], F32, top)
        bq, top = place("bq", [P, 6], F32, top)
        b1s, region_q = place("b1s", [P, MC], F32, top)
        qT, region_w = place("qT", [P, KC, TOK], F32, region_q)
        wch, at = place("wch", [P, KC, 4 * D], F32R, region_q)
        wcl, at = place("wcl", [P, KC, 4 * D], F32R, at)
        woh, at = place("woh", [P, KC, D], F32R, at)
        wol, at = place("wol", [P, KC, D], F32R, at)
        wcraw, at = place("wcraw", [P, KC, 5 * D], F32, region_w - KC * 5 * D * 4)
        assert at <= region_w
        sel, at = place("sel", [2 * E, MH], F32, region_q)
        selr, at = place("selr", [2 * E, MH], F32R, at)
        assert at <= region_q + 2 * KC * 4 * D * 4
        gw, at = place("gw", [P, KC, E], F32, region_w - KC * 5 * D * 4)
        gws, at = place("gws", [P, KC, 2, E], F32R, at)
        gwh, gwl = gws[:, :, 0, :], gws[:, :, 1, :]
        gb, at = place("gb", [P, 2, E], F32, at)
        gbs, at = place("gbs", [P, E], F32, at)
        b2s, at = place("b2s", [2 * E, D], F32, at)
        b2h, at = place("b2h", [2 * E, D], F32R, at)
        b2l, at = place("b2l", [2 * E, D], F32R, at)
        score, at = place("score", [P, GT, E], F32, at)
        best, at = place("best", [P, GT, 8], F32, at)
        besti, at = place("besti", [P, GT, 8], U32, at)
        bestf, at = place("bestf", [P, GT, 8], F32, at)
        iota, at = place("iota", [P, E], F32, at)
        gap, at = place("gap", [P, GT], F32, at)
        ebase, at = place("ebase", [P, GT], F32, at)
        second, at = place("second", [P, GT], F32, at)
        denom, at = place("denom", [P, GT], F32, at)
        gate1, at = place("gate1", [P, GT], F32, at)
        gate2, at = place("gate2", [P, GT], F32, at)
        pick1, at = place("pick1", [P, GT, E], F32, at)
        pick2, at = place("pick2", [P, GT, E], F32, at)
        comb, at = place("comb", [P, GT, 2 * E], F32R, at)
        combT0, at = place("combT0", [2 * E, GW], F32R, at)
        combT1, at = place("combT1", [2 * E, GW], F32R, at)
        combT = (combT0, combT1)
        assert at <= region_w
        wah, at = place("wah", [P, KC, 3 * D], F32R, region_w)
        wal, region_f = place("wal", [P, KC, 3 * D], F32R, at)
        hid0, at = place("hid0", [P, GW], F32, region_w)
        hid1, at = place("hid1", [P, GW], F32, at)
        hh0, at = place("hh0", [P, GW], F32R, at)
        hh1, at = place("hh1", [P, GW], F32R, at)
        hl0, at = place("hl0", [P, GW], F32R, at)
        hl1, at = place("hl1", [P, GW], F32R, at)
        assert at <= region_f
        hid, hh, hl = (hid0, hid1), (hh0, hh1), (hl0, hl1)
        wfh, at = place("wfh", [P, DQ, 3, 2, P], F32R, region_f)
        wfl, region_s = place("wfl", [P, DQ, 3, 2, P], F32R, at)
        last_steps = 2 * 3 * 2 * P * 4
        rT_first, _ = place("rT_first", [P, KC, GW], F32, region_f + DQ * 3 * 2 * P * 4 - last_steps)
        ry_first, _ = place("ry_first", [P, GT, D], F32, region_s - last_steps)
        waraw, _ = place("waraw", [P, KC, 3 * D], F32, region_s - KC * 3 * D * 4)
        qh, at = place("qh", [P, KC, ST * P], F32R, region_f)
        ql, at = place("ql", [P, KC, ST * P], F32R, at)
        kv0, at = place("kv0", [P, 2, 2 * D], F32R, at)
        kv1, at = place("kv1", [P, 2, 2 * D], F32R, at)
        kvs = (kv0, kv1)
        kvh, kvl = [t[:, 0, :] for t in kvs], [t[:, 1, :] for t in kvs]
        us, at = place("us", [P, NT, D], F32, at)
        obuf, at = place("obuf", [P, ST, D], F32, at)
        sq, at = place("sq", [P, GT, D], F32, at)
        oh, at = place("oh", [P, KC, GW], F32R, at)
        ol, at = place("ol", [P, KC, GW], F32R, at)
        state, at = place("state", [P, KC, P], F32, at)
        state_lo, at = place("state_lo", [P, KC, P], F32, at)
        stateh, at = place("stateh", [P, KC, P], F32R, at)
        statel, at = place("statel", [P, KC, P], F32R, at)
        mask, at = place("mask", [P, P], F32, at)
        hsum, at = place("hsum", [P, ST * NH], F32, at)
        hrstd, at = place("hrstd", [P, ST * NH], F32, at)
        hwork, at = place("hwork", [P, ST * NH], F32, at)
        w1raw_at = region_s - KC * MH * 4
        assert at <= w1raw_at
        w1raw, _ = place("w1raw", [P, KC, MH], F32, w1raw_at)
        w2raw, _ = place("w2raw", [P, MC, D], F32, region_w)
        w1h, at = place("w1h", [P, KC, MH], F32R, region_f)
        w1l, at = place("w1l", [P, KC, MH], F32R, at)
        w2h, at = place("w2h", [P, MC, D], F32R, at)
        w2l, at = place("w2l", [P, MC, D], F32R, at)
        assert at <= w1raw_at
        pk0, at = place("pk0", [P, 3, P], I32, region_s)
        pk1, at = place("pk1", [P, 3, P], I32, at)
        sc0, at = place("sc0", [P, 3, P], F32, at)
        sc1, at = place("sc1", [P, 3, P], F32, at)
        pk, sc = (pk0, pk1), (sc0, sc1)
        code, at = place("code", [P, 3, P], I32, at)
        field, at = place("field", [P, 3, P], I32, at)
        ksb, at = place("ksb", [P, GW], F32, at)
        weight, at = place("weight", [P, 3, 2, P], F32, at)
        rT, at = place("rT", [P, KC, GW], F32, region_s)
        ry, at = place("ry", [P, GT, D], F32, at)

        ps = ctx.enter_context(nc.psum_tensor("ps", [P, 8, GW], F32))
        def token_major(bank):
            return ps[:, bank:bank + 2, :].rearrange("p b (t c) -> p (b t) c", t=2)

        tok_banks = token_major(T0)

        names = ("waited consts x_even x_odd wa_raw pk_even pk_odd sc_even sc_odd wc_raw wd_raw sel_raw out_stored "
                 "half_ready wa_hi wa_lo "
                 "f_stats f_mv f_var f_rstd f_xn f_turned f_hi f_lo "
                 "u_turned u_stats u_mv u_var u_neg u_rstd u_nm u_normed u_added u_scaled end_normed end_added "
                 "proj k_copied k_done v_done q_done dq_f dq_code dq_w dq_hi dq_lo "
                 "col_tot col_rn col_c0 col_c "
                 "pre_ready up_ready act_done hid_ready hid_hi hid_lo down_done acc_copied "
                 "wc_hi wc_lo c_q c_kv c_u c_qhi c_qlo c_kvhi c_kvlo c_ucopied c_state c_masked c_sthi c_stlo "
                 "c_o c_ocopied c_hsum c_hrstd c_scaled c_gated o_turned o_hi o_lo "
                 "w1_hi w1_lo w2_hi w2_lo sel_hi rt_hi rt_lo r_consts r_bias r_scores r_scored r_best r_found "
                 "r_comb_hi r_chain r_gap r_second r_comb r_turned r_copied"
                 ).split()
        S = {n: ctx.enter_context(nc.semaphore(n)) for n in names}
        x_loaded = (S["x_even"], S["x_odd"])
        pk_loaded = (S["pk_even"], S["pk_odd"])
        sc_loaded = (S["sc_even"], S["sc_odd"])
        block = ctx.enter_context(nc.Block())

        def apart(eng):
            eng.sem_inc(S["waited"], 1)

        def sequences(eng, first, last, body):
            with eng.Fori(first, last + 1) as b:
                body(b)

        def run_groups(eng, lead, chunks, begin, chunk, slot_work):
            begin()
            for c in range(lead):
                chunk(0, 0, c, 2)
                slot_work(0, 0, c, 2, None)

            def body(b, last_b=False):
                for half in range(2):
                    g = b * 2 + half
                    left = 1 - half if last_b else 2
                    for c in range(lead, chunks):
                        chunk(g, half, c, left)
                        slot_work(g, half, c, left, None)
                    if left > 0:
                        for c in range(lead):
                            chunk(g + 1, 1 - half, c, left - 1)
                            slot_work(g + 1, 1 - half, c, left - 1, g)

            sequences(eng, 0, B - 2, body)
            body(B - 1, last_b=True)

        @block.sync
        def _(sp):
            def load_step(step, s):
                sp.dma_start(pk[s][:], packed[bass.ds(step, 1)].rearrange("o p (m c) -> (o p) m c", m=3)) \
                    .then_inc(pk_loaded[s], 16)
                rows = scales[bass.ds(step * 8, 8)].unsqueeze(1).to_broadcast([8, 16, 3 * P])
                sp.dma_start(sc[s][:].rearrange("p m c -> p (m c)"), rows).then_inc(sc_loaded[s], 16)

            sp.dma_start(x[:, 0:GT, :], x_in[0:GT].rearrange("t p c -> p t c")).then_inc(S["x_even"], 16)
            sp.dma_start(waraw[:], wqkv).then_inc(S["wa_raw"], 16)
            sp.dma_start(ident[:], ident_in).then_inc(S["consts"], 16)
            sp.dma_start(bq[:], bqkv).then_inc(S["consts"], 16)
            sp.dma_start(b1s[:], b1).then_inc(S["consts"], 16)
            sp.dma_start(x[:, GT:2 * GT, :], x_in[GT:2 * GT].rearrange("t p c -> p t c")).then_inc(S["x_odd"], 16)
            for s in range(2):
                load_step(s, s)

            def phase_a(b, last_b=False):
                for half in range(2):
                    g = b * 2 + half
                    if not last_b:
                        sp.wait_ge(x_loaded[half], b * 16 + 16)
                        sp.dma_start(x[:, bass.ds(g * GT + 2 * GT, GT), :],
                                     x_in[bass.ds(g * GT + 2 * GT, GT)].rearrange("t p c -> p t c")) \
                            .then_inc(x_loaded[half], 16)
                    if not (last_b and half == 1):
                        for s in range(2):
                            step = g * 2 + s
                            sp.wait_ge(S["dq_w"], step + (CREDIT + 1))
                            apart(sp)
                            load_step(step + 2, s)

            sequences(sp, 0, B - 2, phase_a)
            phase_a(B - 1, last_b=True)
            sp.wait_ge(S["u_scaled"], NG)
            sp.dma_start(wcraw[:, :, 0:4 * D], wl1).then_inc(S["wc_raw"], 16)
            sp.dma_start(wcraw[:, :, 4 * D:5 * D], wo).then_inc(S["wc_raw"], 16)
            sp.wait_ge(S["down_done"], NG * FC)
            sp.dma_start(mask[:], mask_in).then_inc(S["consts"], 16)
            sp.dma_start(w1raw[:], w1).then_inc(S["wd_raw"], 16)
            sp.dma_start(w2raw[:], w2).then_inc(S["wd_raw"], 16)
            sp.wait_ge(S["wc_lo"], 2)
            sp.dma_start(gw[:], gate_w).then_inc(S["wd_raw"], 16)
            sp.dma_start(gb[:, 0, :], gate_b.unsqueeze(0).to_broadcast([P, E])).then_inc(S["wd_raw"], 16)
            sp.dma_start(gb[:, 1, :], gate_bias.unsqueeze(0).to_broadcast([P, E])).then_inc(S["wd_raw"], 16)
            sp.dma_start(b2s[0:E, :], b2).then_inc(S["wd_raw"], 16)
            sp.dma_start(b2s[E:2 * E, :], b2).then_inc(S["wd_raw"], 16)
            sp.wait_ge(S["c_q"], NG * KC)
            sp.dma_start(sel[:], sel_in).then_inc(S["sel_raw"], 16)

            def store(b, last_b=False):
                for half in range(1 if last_b else 2):
                    g = b * 2 + half
                    sp.wait_ge(S["u_added"], g + (UPDATE0["D"] + 1))
                    sp.dma_start(out[bass.ds(g * GT, GT)].rearrange("t p c -> p t c"),
                                 x[:, bass.ds(g * GT, GT), :]).then_inc(S["out_stored"], 16)

            sequences(sp, 0, B - 2, store)
            store(B - 1, last_b=True)
            for t in range(0, GT, 2):
                sp.wait_ge(S["end_added"], t + 2)
                sp.dma_start(out[NT - GT + t:NT - GT + t + 2].rearrange("t p c -> p t c"),
                             x[:, NT - GT + t:NT - GT + t + 2, :]).then_inc(S["out_stored"], 16)
            sp.wait_ge(S["out_stored"], 16 * (NG + 1))

        @block.tensor
        def _(pe):
            def product(dst, terms, start=True, stop=True, group_check=True):
                n = len(terms)
                for k, (ah, al, bh, bl) in enumerate(terms):
                    pe.matmul(dst, ah, bl, start=start and k == 0, stop=False, skip_group_check=not group_check)
                    pe.matmul(dst, ah, bh, start=False, stop=False, skip_group_check=not group_check)
                    last = pe.matmul(dst, al, bh, start=False, stop=stop and k == n - 1,
                                     skip_group_check=not group_check)
                return last

            def front(F, updates):
                if not (isinstance(updates, int) and updates == 0):
                    pe.wait_ge(S["u_normed"], updates)
                if not (isinstance(F, int) and F == 0):
                    pe.wait_ge(S["f_lo"], F * 2)
                pe.wait_ge(S["f_xn"], F + 1)
                for k in range(KC):
                    for t in range(GT):
                        last = pe.transpose(ps[:, T0 + k, t * P:(t + 1) * P], xn[:, t, k * P:(k + 1) * P], ident[:])
                last.then_inc(S["f_turned"], 1)

            def update_turn(updates, fronts, src=rT):
                if not (isinstance(updates, int) and updates == 0):
                    pe.wait_ge(S["u_normed"], updates)
                pe.wait_ge(S["f_lo"], fronts * 2)
                for t in range(GT):
                    for k in range(KC):
                        last = pe.transpose(tok_banks[:, t, k * P:(k + 1) * P], src[:, k, t * P:(t + 1) * P], ident[:])
                last.then_inc(S["u_turned"], 1)

            def front_ready(F):
                pe.wait_ge(S["f_hi"], F * 2 + 2)
                pe.wait_ge(S["f_lo"], F * 2 + 2)

            def attention_turn(g, src=rT):
                pe.wait_ge(S["u_scaled"], g + 1)
                update_turn(in_attention_update(g), NG - 1 if isinstance(g, int) and g == 0 else g + FRONT0["B"], src)

            pe.wait_ge(S["consts"], 48)
            front(0, 0)
            pe.wait_ge(S["wa_hi"], 1)
            pe.wait_ge(S["wa_lo"], 1)

            def phase_a(b, last_b=False):
                for half in range(2):
                    g = b * 2 + half
                    front_ready(g)
                    order = ((2, 0, "k_done"), (4, 1, "v_done"), (3, 2, "k_done"), (5, 3, "v_done"),
                             (0, 4, "q_done"), (1, 5, "q_done"))
                    for n, (m, bank, reader) in enumerate(order):
                        if n in (0, 4):
                            if n == 0:
                                pe.wait_ge(S["k_done"], CREDIT + g * 2)
                                pe.wait_ge(S["v_done"], CREDIT + g * 2)
                            else:
                                pe.wait_ge(S["q_done"], CREDIT + g * 2)
                        cols = slice(m * P, (m + 1) * P)
                        product(ps[:, bank, :], [(wah[:, k, cols], wal[:, k, cols], xh[half][:, k, :], xl[half][:, k, :])
                                                 for k in range(KC)]).then_inc(S["proj"], 1)
                        if n == 3 and not (last_b and half == 0):
                            front(g + 1, 1 if last_b else 0)
                        if last_b and half == 0:
                            if n == 3:
                                attention_turn(0, rT_first)
                            if n == 5:
                                front(g + 1, 1)

            sequences(pe, 0, B - 2, phase_a)
            phase_a(B - 1, last_b=True)

            def hidden_layer(phase, chunks, pre, down, slot_work):
                n0 = 0 if phase == "B" else NG * FC

                def pre_chunk(half, c, first=False):
                    if phase == "D" and first:
                        pe.wait_ge(S["w1_lo"], c + 1)
                    pre(half, c, (half * chunks + c) % 2 * 2)

                def chunk(g, half, c, left):
                    n = g * chunks + (c + n0)
                    pe.wait_ge(S["hid_ready"], n + 1)
                    if c + 2 < chunks:
                        pre_chunk(half, c + 2, isinstance(g, int) and g == 0)
                    elif left > 0:
                        if c + 2 == chunks:
                            front_ready(g + (FRONT0[phase] + 1))
                            if phase == "D":
                                pe.wait_ge(S["r_copied"], g + 2)
                        pre_chunk(1 - half, c + 2 - chunks)
                    pe.wait_ge(S["hid_hi"], n + 1)
                    pe.wait_ge(S["hid_lo"], n + 1)
                    if c == 0:
                        pe.wait_ge(S["acc_copied"], g * 2 + (0 if phase == "B" else 2 * NG))
                    down(half, c, (half * chunks + c) % 2).then_inc(S["down_done"], 1)

                def begin():
                    pre_chunk(0, 0, True)
                    if phase == "D":
                        pe.wait_ge(S["u_normed"], UPDATE0["D"] - 1)
                    pre_chunk(0, 1, True)

                return begin, chunk, slot_work

            def result_turn(phase, g, last_g=False):
                pe.wait_ge(S["acc_copied"], g * 2 + (2 if phase == "B" else 2 * NG + 2))
                fronts = g + (FRONT0[phase] + (2 if phase == "B" else 3))
                update_turn(result_update(phase, g, last_g), FRONT0["D"] + NG if phase == "D" and last_g else fronts)

            def mlp_pre(half, c, bank):
                for m, dst, done in ((0, bank, "pre_ready"), (1, bank + 1, "up_ready")):
                    product(ps[:, dst, :], [(wfh[:, c, m, k, :], wfl[:, c, m, k, :],
                                             xh[half][:, k, :], xl[half][:, k, :]) for k in range(KC)]) \
                        .then_inc(S[done], 1)

            def mlp_down(half, c, slot):
                for m in range(KC):
                    step = c // 2 * 2 + m
                    last = product(ps[:, O0 + m, :], [(wfh[:, step, 2, c % 2, :], wfl[:, step, 2, c % 2, :],
                                                       hh[slot][:], hl[slot][:])], start=c == 0, stop=c == FC - 1)
                return last

            def mlp_slot(g, half, c, left, prev):
                if c == 3 and prev is None:
                    pe.wait_ge(S["dq_lo"], CREDIT + DQ)
                if c == 1 and prev is not None:
                    result_turn("B", prev)
                if c == 5 and left > 0:
                    attention_turn(g + 1)
                if c == 10:
                    front(g + (FRONT0["B"] + 1), g * 2 + 2 if left > 0 else 2 * NG - 1)

            front_ready(FRONT0["B"])
            pe.wait_ge(S["dq_lo"], CREDIT + DQ - 2)
            run_groups(pe, LEAD["B"], FC, *hidden_layer("B", FC, mlp_pre, mlp_down, mlp_slot))

            def kv_u(g, half, t):
                tk = slice(t * P, (t + 1) * P)
                product(ps[:, 2 + t % 2, :], [(xh[half][:, k, tk], xl[half][:, k, tk], wch[:, k, D:3 * D],
                                               wcl[:, k, D:3 * D]) for k in range(KC)]).then_inc(S["c_kv"], 1)
                if t >= 2:
                    pe.wait_ge(S["c_ucopied"], g * GT + (t - 1))
                elif not (isinstance(g, int) and g == 0):
                    pe.wait_ge(S["c_qlo"], g * KC + (t + 1 - KC))
                product(ps[:, t % 2, 0:D], [(xh[half][:, k, tk], xl[half][:, k, tk], wch[:, k, 3 * D:4 * D],
                                             wcl[:, k, 3 * D:4 * D]) for k in range(KC)]).then_inc(S["c_u"], 1)

            def q_projection(g, half):
                for m in range(KC):
                    pe.wait_ge(S["c_ucopied"], g * GT + (m + 3))
                    cols = slice(m * P, (m + 1) * P)
                    product(ps[:, m, :], [(wch[:, k, cols], wcl[:, k, cols], xh[half][:, k, :], xl[half][:, k, :])
                                          for k in range(KC)]).then_inc(S["c_q"], 1)

            def accumulate(b, g, half, t):
                pe.wait_ge(S["c_kvlo"], g * GT + (t + 1))
                first, final = half == 0 and t == 0, half == 1 and t == GT - 1
                if first and not (isinstance(b, int) and b == 0):
                    pe.wait_ge(S["c_masked"], b * 3 - 1)
                for m in range(KC):
                    kc, vc = slice(m * P, (m + 1) * P), slice(D + m * P, D + (m + 1) * P)
                    dst = ps[:, O0, m * 2 * P:(m + 1) * 2 * P].rearrange("p (h c) -> p h c", h=2)
                    rhs = kvs[t % 2][:, :, vc]
                    pe.matmul(dst, kvl[t % 2][:, kc], rhs, start=first and m == 0, stop=False, skip_group_check=True)
                    last = pe.matmul(dst, kvh[t % 2][:, kc], rhs, start=False, stop=final and m == KC - 1,
                                     skip_group_check=True)
                if final:
                    last.then_inc(S["c_state"], 1)

            def attend(b, pair, bank=O1):
                pe.wait_ge(S["c_stlo"], b + 1)
                if isinstance(b, int) and b == B - 1:
                    pe.wait_ge(S["c_ocopied"], b * (ST // 2) + max(pair - 1, 0))
                elif not (isinstance(b, int) and b == 0 and pair == 0):
                    pe.wait_ge(S["c_ocopied"], b * (ST // 2) + pair)
                for t in (pair * 2, pair * 2 + 1):
                    for m in range(KC):
                        tk = slice(t * P, (t + 1) * P)
                        last = product(ps[:, bank, t % 2 * D + m * P:t % 2 * D + (m + 1) * P],
                                       [(qh[:, m, tk], ql[:, m, tk], stateh[:, m, :], statel[:, m, :])],
                                       group_check=False)
                last.then_inc(S["c_o"], 1)

            def output_turn(h, half, bank=T0):
                pe.wait_ge(S["c_gated"], h + 1)
                for k in range(KC):
                    for t in range(GT):
                        last = pe.transpose(ps[:, bank + k, t * P:(t + 1) * P],
                                            obuf[:, half * GT + t, k * P:(k + 1) * P], ident[:])
                last.then_inc(S["o_turned"], 1)

            def output_product(h, bank=T0):
                pe.wait_ge(S["o_hi"], h * 2 + 2)
                pe.wait_ge(S["o_lo"], CREDIT + h * 2 + 2)
                for t in range(GT):
                    tk = slice(t * P, (t + 1) * P)
                    last = product(token_major(bank)[:, t, :], [(oh[:, k, tk], ol[:, k, tk], woh[:, k, :], wol[:, k, :])
                                                                for k in range(KC)])
                last.then_inc(S["u_turned"], 1)

            def step(b, g, half, seq=None, h=None):
                first = isinstance(g, int) and g == 0
                front_ready(g + FRONT0["C"])
                kv_u(g, half, 0)
                if first:
                    result_turn("B", NG - 1, True)
                kv_u(g, half, 1)
                accumulate(b, g, half, 0)
                if seq is not None:
                    attend(seq, 0)
                kv_u(g, half, 2)
                if not first:
                    front(g + (FRONT0["C"] + 1), g + (UPDATE0["C"] - 3) if h is not None else UPDATE0["C"])
                accumulate(b, g, half, 1)
                if seq is not None:
                    attend(seq, 1)
                if h is not None:
                    pe.wait_ge(S["f_lo"], g * 2 + (FRONT0["C"] * 2 + 4))
                    output_turn(h, 1 - half)
                kv_u(g, half, 3)
                if first:
                    front(FRONT0["C"] + 1, UPDATE0["C"])
                accumulate(b, g, half, 2)
                if seq is not None:
                    attend(seq, 2)
                if h is not None:
                    output_product(h)
                if seq is not None:
                    attend(seq, 3)
                accumulate(b, g, half, 3)
                q_projection(g, half)

            pe.wait_ge(S["wc_hi"], 2)
            pe.wait_ge(S["wc_lo"], 2)
            step(0, 0, 0)
            step(0, 1, 1)
            step(1, 2, 0, seq=0)

            def phase_c(b):
                step(b, b * 2 + 1, 1, h=b * 2 - 2)
                step(b + 1, b * 2 + 2, 0, seq=b, h=b * 2 - 1)

            sequences(pe, 1, B - 2, phase_c)
            step(B - 1, NG - 1, 1, h=NG - 4)

            def router(F, half, bank=T0):
                front_ready(F)
                for t in range(GT):
                    tk = slice(t * P, (t + 1) * P)
                    for k in range(KC):
                        rhs = gws[:, k, :, :].rearrange("p h e -> p (h e)")
                        dst = ps[:, bank, t * 2 * E:(t + 1) * 2 * E]
                        pe.matmul(dst, xl[half][:, k, tk], rhs, start=k == 0, stop=False)
                        last = pe.matmul(dst, xh[half][:, k, tk], rhs, start=False, stop=k == KC - 1)
                last.then_inc(S["r_scores"], 1)

            def router_turn(g, bank=T1):
                pe.wait_ge(S["r_comb"], g + 1)
                for t in range(GT):
                    last = pe.transpose(ps[0:2 * E, bank, t * P:(t + 1) * P], comb[:, t, :].bitcast(F32), ident[:])
                last.then_inc(S["r_turned"], 1)

            attend(B - 1, 0)
            attend(B - 1, 1, O0)
            pe.wait_ge(S["c_ucopied"], NG * GT)
            pe.wait_ge(S["c_qlo"], NG * KC)
            attend(B - 1, 2)
            output_turn(NG - 3, 1, G0)
            attend(B - 1, 3, O0)
            pe.wait_ge(S["rt_hi"], 2)
            pe.wait_ge(S["rt_lo"], 2)
            pe.wait_ge(S["c_ocopied"], NT // 2)
            router(FRONT0["D"], 0, O0)
            output_product(NG - 3, G0)
            front(FRONT0["D"] + 1, UPDATE0["D"] - 3)
            output_turn(NG - 2, 0, G1)
            pe.wait_ge(S["f_lo"], FRONT0["D"] * 2 + 4)
            output_turn(NG - 1, 1)
            output_product(NG - 2, G1)
            router_turn(0, O1)
            output_product(NG - 1)

            def expert_pre(half, c, bank):
                cols = slice(c * P, (c + 1) * P)
                product(ps[:, bank, :], [(w1h[:, k, cols], w1l[:, k, cols], xh[half][:, k, :], xl[half][:, k, :])
                                         for k in range(KC)]).then_inc(S["pre_ready"], 1)
                pe.matmul(ps[:, bank + 1, :], selr[:, cols], combT[half][:], start=True, stop=True) \
                    .then_inc(S["up_ready"], 1)

            def expert_down(half, c, slot):
                for m in range(KC):
                    cols = slice(m * P, (m + 1) * P)
                    if c == 0:
                        pe.matmul(ps[:, O0 + m, :], b2l[:, cols], combT[half][:], start=True, stop=False)
                        pe.matmul(ps[:, O0 + m, :], b2h[:, cols], combT[half][:], start=False, stop=False)
                    last = product(ps[:, O0 + m, :], [(w2h[:, c, cols], w2l[:, c, cols], hh[slot][:], hl[slot][:])],
                                   start=False, stop=c == MC - 1)
                return last

            def expert_slot(g, half, c, left, prev):
                late = 1 if prev is None else 0
                if c == 1 + late and left > 0:
                    if prev is None:
                        pe.wait_ge(S["u_normed"], UPDATE0["D"])
                    router(g + (FRONT0["D"] + 1), 1 - half)
                if c == 4 and left > 0:
                    router_turn(g + 1)
                if c == 10 and left > 1:
                    front(g + (FRONT0["D"] + 2), g + UPDATE0["D"])
                if c == 5 and prev is not None:
                    if left > 0:
                        pe.wait_ge(S["r_copied"], g + 2)
                    result_turn("D", prev, left == 0)

            pe.wait_ge(S["u_normed"], UPDATE0["D"] - 2)
            pe.wait_ge(S["sel_hi"], 1)
            pe.wait_ge(S["w2_lo"], MC)
            pe.wait_ge(S["r_copied"], 1)
            run_groups(pe, LEAD["D"], MC, *hidden_layer("D", MC, expert_pre, expert_down, expert_slot))
            result_turn("D", NG - 1, True)

        @block.scalar
        def _(act):
            def front(F, half):
                act.wait_ge(S["f_turned"], F + 1)
                for k in range(KC):
                    act.activation(xh[half][:, k, :], ps[:, T0 + k, :], ACT.Copy).then_inc(S["f_hi"], 1)

            def update(n, bank=T0, dst=ry):
                act.wait_ge(S["u_rstd"], n + 1)
                act.wait_ge(S["u_nm"], n + 1)
                act.wait_ge(S["u_added"], n)
                for t in range(GT):
                    last = act.activation(dst[:, t, :], token_major(bank)[:, t, :], ACT.Identity,
                                          bias=unm[:, t:t + 1], scale=urstd[:, t:t + 1])
                last.then_inc(S["u_normed"], 1)

            act.sem_inc(S["k_done"], CREDIT)
            act.sem_inc(S["q_done"], CREDIT)
            act.preload_act_table(ACT.Copy)
            act.wait_ge(S["wa_raw"], 16)
            act.activation(wah[:], waraw[:], ACT.Copy).then_inc(S["wa_hi"], 1)
            act.wait_ge(S["consts"], 48)
            front(0, 0)

            def phase_a(b, last_b=False):
                for half in range(2):
                    g = b * 2 + half

                    def dequant_hi(s):
                        step = g * 2 + s
                        act.wait_ge(S["dq_w"], CREDIT + step + 1)
                        act.activation(wfh[:, bass.ds(step, 1)].rearrange("p o m n c -> p (o m n c)"),
                                       weight[:].rearrange("p m n c -> p (m n c)"), ACT.Copy) \
                            .then_inc(S["dq_hi"], 1)

                    for m, n in ((0, 1), (1, 3)):
                        act.wait_ge(S["proj"], g * 6 + n)
                        act.wait_ge(S["v_done"], CREDIT + g * 2 + m)
                        act.activation(ksb[:], ps[:, 2 * m, :], ACT.Identity, bias=bq[:, 2 + m:3 + m]) \
                            .then_inc(S["k_copied"], 1)
                        act.activation(ps[:, 2 * m, :], ps[:, 2 * m, :], ACT.Square, bias=bq[:, 2 + m:3 + m],
                                       accum_out=colsum[:, bass.ds(g, 1), m]).then_inc(S["k_done"], 1)
                    dequant_hi(0)
                    if last_b and half == 0:
                        update(0, dst=ry_first)
                    else:
                        front(g + 1, 1 - half)
                    for m in range(KC):
                        act.wait_ge(S["proj"], g * 6 + (5 + m))
                        act.activation(qT[:, m, bass.ds(g * GW, GW)], ps[:, 4 + m, :], ACT.Identity,
                                       bias=bq[:, m:m + 1])
                        act.activation(ps[:, 4 + m, :], ps[:, 4 + m, :], ACT.Square, bias=bq[:, m:m + 1],
                                       accum_out=colsum[:, bass.ds(g, 1), 2 + m]).then_inc(S["q_done"], 1)
                    if last_b and half == 0:
                        front(g + 1, 1)
                    dequant_hi(1)

            sequences(act, 0, B - 2, phase_a)
            phase_a(B - 1, last_b=True)

            def copy_acc(g, phase, n):
                scale = FP8_UNIT * FP8_UNIT if phase == "B" else 1.0
                act.wait_ge(S["down_done"], g * FC + FC if phase == "B" else g * MC + (NG * FC + MC))
                act.wait_ge(S["u_turned"], n)
                for m in range(KC):
                    act.activation(rT[:, m, :], ps[:, O0 + m, :], ACT.Copy, scale=scale).then_inc(S["acc_copied"], 1)

            def hidden_layer(phase, chunks, func, bias, scale, slot_work):
                n0 = 0 if phase == "B" else NG * FC

                def chunk(g, half, c, left):
                    n = g * chunks + (c + n0)
                    par = (half * chunks + c) % 2
                    act.wait_ge(S["pre_ready"], n + 1)
                    act.activation(hid[par][:], ps[:, par * 2, :], func, bias=bias(c), scale=scale).then_inc(S["act_done"], 1)
                    act.wait_ge(S["hid_ready"], n + 1)
                    if not (isinstance(n, int) and n < 2):
                        act.wait_ge(S["down_done"], n - 1)
                    act.activation(hh[par][:], hid[par][:], ACT.Copy).then_inc(S["hid_hi"], 1)

                return (lambda: None), chunk, slot_work

            def mlp_slot(g, half, c, left, prev):
                if c == 0 and prev is not None:
                    copy_acc(prev, "B", prev * 2 + 2)
                if c == 4 and prev is not None:
                    update(prev * 2 + 2)
                if c == 8 and left > 0:
                    update(in_attention_update(g + 1))
                if c == 12:
                    front(g + (FRONT0["B"] + 1), 1 - half)
                if c == 6 and left == 0:
                    act.wait_ge(S["wc_raw"], 32)
                    act.activation(wch[:], wcraw[:, :, 0:4 * D], ACT.Copy).then_inc(S["wc_hi"], 1)
                    act.activation(woh[:], wcraw[:, :, 4 * D:5 * D], ACT.Copy).then_inc(S["wc_hi"], 1)

            act.preload_act_table(ACT.Gelu_apprx_tanh)
            run_groups(act, LEAD["B"], FC, *hidden_layer("B", FC, ACT.Gelu_apprx_tanh, lambda c: 0.0, FP8_UNIT, mlp_slot))
            copy_acc(NG - 1, "B", 2 * NG - 1)

            act.preload_act_table(ACT.Silu)

            def kv_u(g, t):
                act.wait_ge(S["c_kv"], g * GT + (t + 1))
                act.activation(kvh[t % 2][:, 0:D], ps[:, 2 + t % 2, 0:D], ACT.Relu)
                act.activation(kvh[t % 2][:, D:2 * D], ps[:, 2 + t % 2, D:2 * D], ACT.Copy).then_inc(S["c_kvhi"], 1)
                act.wait_ge(S["c_u"], g * GT + (t + 1))
                act.activation(us[:, bass.ds(g * GT + t, 1), :].rearrange("p o c -> p (o c)"), ps[:, t % 2, 0:D],
                               ACT.Silu).then_inc(S["c_ucopied"], 1)

            def q_hi(g, half):
                for m in range(KC):
                    act.wait_ge(S["c_q"], g * KC + (m + 1))
                    act.activation(qh[:, m, half * GW:(half + 1) * GW], ps[:, m, :], ACT.Relu).then_inc(S["c_qhi"], 1)

            def output_hi(h, bank=T0):
                act.wait_ge(S["o_turned"], h + 1)
                for k in range(KC):
                    act.activation(oh[:, k, :], ps[:, bank + k, :], ACT.Copy).then_inc(S["o_hi"], 1)

            def attend(b, pair, bank=O1):
                act.wait_ge(S["c_o"], b * (ST // 2) + (pair + 1))
                o = ps[:, bank, :].rearrange("p (t c) -> p t c", t=2)
                act.activation(obuf[:, pair * 2:pair * 2 + 2, :], o, ACT.Copy)
                if pair >= 2:
                    act.wait_ge(S["c_hsum"], b * 2 + 1)
                elif not (isinstance(b, int) and b == 0):
                    act.wait_ge(S["c_hsum"], b * 2)
                act.activation(sq[:, pair % 2 * 2:pair % 2 * 2 + 2, :], o, ACT.Square).then_inc(S["c_ocopied"], 1)

            def step(g, half, seq=None, h=None):
                first = isinstance(g, int) and g == 0
                kv_u(g, 0)
                kv_u(g, 1)
                if seq is not None:
                    attend(seq, 0)
                if first:
                    update(2 * NG - 1)
                else:
                    front(g + (FRONT0["C"] + 1), 1 - half)
                kv_u(g, 2)
                if seq is not None:
                    attend(seq, 1)
                if h is not None:
                    output_hi(h)
                kv_u(g, 3)
                if first:
                    front(FRONT0["C"] + 1, 1)
                if seq is not None:
                    attend(seq, 2)
                    attend(seq, 3)
                q_hi(g, half)
                if h is not None:
                    update(h + UPDATE0["C"])

            step(0, 0)
            step(1, 1)
            step(2, 0, seq=0)

            def phase_c(b):
                step(b * 2 + 1, 1, h=b * 2 - 2)
                step(b * 2 + 2, 0, seq=b, h=b * 2 - 1)

            sequences(act, 1, B - 2, phase_c)
            step(NG - 1, 1, h=NG - 4)

            def gates(g, half, bank=T1):
                act.wait_ge(S["r_turned"], g + 1)
                act.activation(combT[half][:], ps[0:2 * E, bank, :], ACT.Copy).then_inc(S["r_copied"], 1)

            def expert_slot(g, half, c, left, prev):
                if c == 0 and prev is not None:
                    copy_acc(prev, "D", prev + UPDATE0["D"])
                if c == 1 and left > 0 and prev is not None:
                    front(g + (FRONT0["D"] + 1), 1 - half)
                if c == 6 and left > 0:
                    gates(g + 1, 1 - half)
                if c == 8 and prev is not None:
                    update(prev + UPDATE0["D"])
                if prev is None and isinstance(g, int) and g == 0:
                    split_next(c)

            def w1_hi(c):
                cols = slice(c * P, (c + 1) * P)
                act.activation(w1h[:, :, cols], w1raw[:, :, cols], ACT.Copy).then_inc(S["w1_hi"], 1)

            def w2_hi(c):
                act.activation(w2h[:, c, :], w2raw[:, c, :], ACT.Copy).then_inc(S["w2_hi"], 1)

            def split_next(c):
                if c + 3 < MC:
                    w1_hi(c + 3)
                if c == 1:
                    update(NG - 1 + UPDATE0["C"])

            act.wait_ge(S["wd_raw"], 112)
            for hi, raw in ((gwh, gw), (b2h[:], b2s)):
                act.activation(hi, raw[:], ACT.Copy).then_inc(S["rt_hi"], 1)
            attend(B - 1, 0)
            attend(B - 1, 1, O0)
            act.wait_ge(S["o_turned"], NG - 2)
            attend(B - 1, 2)
            attend(B - 1, 3, O0)
            output_hi(NG - 3, G0)
            for c in range(3):
                w1_hi(c)
            act.wait_ge(S["c_gated"], NG - 2)
            front(FRONT0["D"] + 1, 1)
            for c in range(MC):
                w2_hi(c)
            output_hi(NG - 2, G1)
            update(NG - 3 + UPDATE0["C"], G0)
            act.wait_ge(S["sel_raw"], 16)
            act.activation(selr[:], sel[:], ACT.Copy).then_inc(S["sel_hi"], 1)
            act.wait_ge(S["u_turned"], UPDATE0["D"] - 1)
            output_hi(NG - 1)
            gates(0, 0, O1)
            update(NG - 2 + UPDATE0["C"], G1)
            run_groups(act, LEAD["D"], MC, *hidden_layer("D", MC, ACT.Silu, lambda c: b1s[:, c:c + 1], 1.0, expert_slot))
            copy_acc(NG - 1, "D", NG - 1 + UPDATE0["D"])
            n = NG - 1 + UPDATE0["D"]
            act.wait_ge(S["u_rstd"], n + 1)
            act.wait_ge(S["u_nm"], n + 1)
            act.wait_ge(S["u_added"], n)
            for t in range(GT):
                act.activation(ry[:, t, :], tok_banks[:, t, :], ACT.Identity,
                               bias=unm[:, t:t + 1], scale=urstd[:, t:t + 1]).then_inc(S["end_normed"], 1)

        @block.vector
        def _(dve):
            dve.memset(neghalf[:], -0.5).then_inc(S["half_ready"], 1)
            dve.sem_inc(S["v_done"], CREDIT)
            dve.sem_inc(S["o_lo"], CREDIT)

            def front_stats(F, g, updates):
                dve.wait_ge(S["u_added"], updates)
                apart(dve)
                for t in range(GT):
                    last = dve.bn_stats(fstats[:, t, :], x[:, bass.ds(g * GT + t, 1), :].rearrange("p o c -> p (o c)"))
                last.then_inc(S["f_stats"], 1)
                dve.wait_ge(S["f_stats"], F + 1)
                apart(dve)
                for t in range(GT):
                    last = dve.bn_aggr(fmv[:, t, :], fstats[:, t, :])
                last.then_inc(S["f_mv"], 1)

            def front_norm(F, g, between=lambda t: None):
                dve.wait_ge(S["f_rstd"], F + 1)
                dve.wait_ge(S["f_turned"], F)
                for t in range(GT):
                    last = dve.tensor_scalar(xn[:, t, :], x[:, bass.ds(g * GT + t, 1), :].rearrange("p o c -> p (o c)"),
                                             fmv[:, t, 0:1], frstd[:, t:t + 1], ALU.subtract, ALU.mult)
                    between(t)
                last.then_inc(S["f_xn"], 1)

            def front_lo(F, half):
                for k in range(KC):
                    dve.wait_ge(S["f_hi"], F * 2 + (k + 1))
                    dve.tensor_tensor(xl[half][:, k, :], ps[:, T0 + k, :], xh[half][:, k, :].bitcast(F32),
                                      ALU.subtract).then_inc(S["f_lo"], 1)

            def update_stats(n, bank=T0):
                dve.wait_ge(S["u_turned"], n + 1)
                apart(dve)
                for t in range(GT):
                    last = dve.bn_stats(ustats[:, t, :], token_major(bank)[:, t, :])
                last.then_inc(S["u_stats"], 1)
                dve.wait_ge(S["u_stats"], n + 1)
                if not (isinstance(n, int) and n == 0):
                    dve.wait_ge(S["u_nm"], n)
                apart(dve)
                for t in range(GT):
                    last = dve.bn_aggr(umv[:, t, :], ustats[:, t, :])
                last.then_inc(S["u_mv"], 1)

            def scale(g, n, dst=rT):
                dve.wait_ge(S["u_turned"], n)
                for m in range(KC):
                    last = dve.tensor_scalar(dst[:, m, :], qT[:, m, bass.ds(g * GW, GW)],
                                             colc[:, bass.ds(g, 1), m], None, ALU.mult)
                last.then_inc(S["u_scaled"], 1)

            def column_totals(b0, b1):
                dve.wait_ge(S["k_done"], CREDIT + 4 * b1)
                dve.wait_ge(S["q_done"], CREDIT + 4 * b1)
                dve.wait_ge(S["v_done"], CREDIT + 4 * b1)
                sums = colsum[:].rearrange("p (b h) s -> p b h s", h=2)[:, b0:b1]
                dve.tensor_tensor(coltot[:, b0:b1], sums[:, :, 0, :], sums[:, :, 1, :], ALU.add).then_inc(S["col_tot"], 1)

            def column_factors(b0, b1, done):
                dve.wait_ge(S["col_tot"], done)
                dve.wait_ge(S["col_rn"], done)
                dve.tensor_tensor(colkv[:, b0:b1], coltot[:, b0:b1, 4:6], colrn[:, b0:b1, 0:2], ALU.mult) \
                    .then_inc(S["col_c0"], 1)
                dve.wait_ge(S["col_c0"], done)
                factor = colc[:].rearrange("p (b h) c -> p b h c", h=2)[:, b0:b1]
                for half in range(2):
                    dve.tensor_tensor(factor[:, :, half, :], colkv[:, b0:b1], colrn[:, b0:b1, 2:4], ALU.mult) \
                        .then_inc(S["col_c"], 1)
                dve.wait_ge(S["col_c"], done * 2)

            dve.wait_ge(S["x_even"], 16)
            front_stats(0, 0, 0)
            front_norm(0, 0)
            dve.wait_ge(S["wa_hi"], 1)
            dve.tensor_tensor(wal[:], waraw[:], wah[:].bitcast(F32), ALU.subtract).then_inc(S["wa_lo"], 1)
            dve.wait_ge(S["consts"], 48)
            front_lo(0, 0)
            dve.wait_ge(S["x_odd"], 16)
            front_stats(1, 1, 0)

            def phase_a(b, last_b=False):
                for half in range(2):
                    g = b * 2 + half

                    def codes(s):
                        step = g * 2 + s
                        f0 = step * 4
                        dve.wait_ge(pk_loaded[s], g * 16 + 16)
                        if last_b:
                            dve.wait_ge(S["dq_code"], step)
                        dve.tensor_scalar(field[:], pk[s][:], 0xF0, 4, ALU.bitwise_and, ALU.logical_shift_left) \
                            .then_inc(S["dq_f"], 1)
                        dve.wait_ge(S["dq_f"], f0 + 1)
                        dve.wait_ge(S["dq_w"], CREDIT + step)
                        dve.scalar_tensor_tensor(code[:], pk[s][:], 0x0F, field[:], ALU.bitwise_and, ALU.bitwise_or) \
                            .then_inc(S["dq_f"], 1)
                        dve.wait_ge(S["dq_f"], f0 + 2)
                        dve.tensor_scalar(field[:], code[:], 0x707, 2, ALU.bitwise_and, ALU.logical_shift_left) \
                            .then_inc(S["dq_f"], 1)
                        dve.tensor_scalar(code[:], code[:], 0x808, 4, ALU.bitwise_and, ALU.logical_shift_left) \
                            .then_inc(S["dq_f"], 1)
                        dve.wait_ge(S["dq_f"], f0 + 4)
                        dve.tensor_tensor(code[:], code[:], field[:], ALU.bitwise_or).then_inc(S["dq_code"], 1)

                    def v_sum(m):
                        dve.wait_ge(S["proj"], g * 6 + (2 + 2 * m))
                        dve.wait_ge(S["k_copied"], g * 2 + (1 + m))
                        dve.scalar_tensor_tensor(ps[:, 1 + 2 * m, :], ps[:, 1 + 2 * m, :], bq[:, 4 + m:5 + m], ksb[:],
                                                 ALU.add, ALU.mult, accum_out=colsum[:, bass.ds(g, 1), 4 + m]) \
                            .then_inc(S["v_done"], 1)

                    codes(0)
                    if last_b and half == 0:
                        column_totals(0, 1)
                        column_factors(0, 1, 1)
                        scale(0, 0, rT_first)
                    v_sum(0)
                    if last_b and half == 1:
                        codes(1)
                    front_norm(g + 1, 0 if last_b and half == 1 else g + 1)
                    v_sum(1)
                    if last_b and half == 0:
                        update_stats(0)
                    if not (last_b and half == 1):
                        codes(1)
                    front_lo(g + 1, 1 - half)
                    if not last_b:
                        dve.wait_ge(x_loaded[half], b * 16 + 32)
                        front_stats(g + 2, g + 2, 0)
                    elif half == 0:
                        front_stats(g + 2, 0, 1)

            sequences(dve, 0, B - 2, phase_a)
            phase_a(B - 1, last_b=True)
            column_totals(1, B)
            def hidden_layer(phase, chunks, slot_work):
                n0 = 0 if phase == "B" else NG * FC

                def chunk(g, half, c, left):
                    n = g * chunks + (c + n0)
                    par = (half * chunks + c) % 2
                    dve.wait_ge(S["act_done"], n + 1)
                    dve.wait_ge(S["up_ready"], n + 1)
                    dve.tensor_tensor(hid[par][:], hid[par][:], ps[:, par * 2 + 1, :], ALU.mult) \
                        .then_inc(S["hid_ready"], 1)
                    dve.wait_ge(S["hid_hi"], n + 1)
                    dve.tensor_tensor(hl[par][:], hid[par][:], hh[par][:].bitcast(F32), ALU.subtract) \
                        .then_inc(S["hid_lo"], 1)

                return (lambda: None), chunk, slot_work

            def mlp_slot(g, half, c, left, prev):
                if c == 2 and prev is None:
                    column_factors(1, B, 2)
                if c == 3 and prev is not None:
                    update_stats(prev * 2 + 2)
                if left > 0:
                    n = g * 2 + 1
                    if c == 5:
                        scale(g + 1, n)
                    if c == 7:
                        update_stats(n)
                if c == 9:
                    if left > 0:
                        front_stats(g + (FRONT0["B"] + 1), g + 1, g * 2 + 2)
                    else:
                        front_stats(FRONT0["C"], 0, 2 * NG - 1)
                if c == 10:
                    front_norm(g + (FRONT0["B"] + 1), g + 1 if left > 0 else 0)
                if c == 12:
                    front_lo(g + (FRONT0["B"] + 1), 1 - half)
                if c == 13 and left == 0:
                    front_stats(FRONT0["C"] + 1, 1, 2 * NG - 1)
                if c == 14 and left == 0:
                    front_norm(FRONT0["C"] + 1, 1)
                if c == 7 and left == 0:
                    dve.wait_ge(S["wc_hi"], 2)
                    dve.tensor_tensor(wcl[:], wcraw[:, :, 0:4 * D], wch[:].bitcast(F32), ALU.subtract) \
                        .then_inc(S["wc_lo"], 1)
                    dve.tensor_tensor(wol[:], wcraw[:, :, 4 * D:5 * D], woh[:].bitcast(F32), ALU.subtract) \
                        .then_inc(S["wc_lo"], 1)

            run_groups(dve, LEAD["B"], FC, *hidden_layer("B", FC, mlp_slot))

            def kv_lo(g, t):
                dve.wait_ge(S["c_kvhi"], g * GT + (t + 1))
                dve.scalar_tensor_tensor(kvl[t % 2][:, 0:D], ps[:, 2 + t % 2, 0:D], 0.0,
                                         kvh[t % 2][:, 0:D].bitcast(F32), ALU.max, ALU.subtract)
                dve.tensor_tensor(kvl[t % 2][:, D:2 * D], ps[:, 2 + t % 2, D:2 * D],
                                  kvh[t % 2][:, D:2 * D].bitcast(F32), ALU.subtract).then_inc(S["c_kvlo"], 1)

            def q_lo(g, half):
                for m in range(KC):
                    dve.wait_ge(S["c_qhi"], g * KC + (m + 1))
                    dve.scalar_tensor_tensor(ql[:, m, half * GW:(half + 1) * GW], ps[:, m, :], 0.0,
                                             qh[:, m, half * GW:(half + 1) * GW].bitcast(F32), ALU.max, ALU.subtract) \
                        .then_inc(S["c_qlo"], 1)

            def gate(h, half):
                if half == 0:
                    dve.wait_ge(S["c_hrstd"], h * (HEAD_OPS // 2) + HEAD_OPS)
                heads = obuf[:, half * GT:(half + 1) * GT, :].rearrange("p t (h d) -> p (t h) d", d=HD)
                rstd = hrstd[:, half * GT * NH:(half + 1) * GT * NH].unsqueeze(2).to_broadcast([P, GT * NH, HD])
                dve.tensor_tensor(heads, heads, rstd, ALU.mult).then_inc(S["c_scaled"], 1)

            def output_lo(h, bank=T0):
                for k in range(KC):
                    dve.wait_ge(S["o_hi"], h * 2 + (k + 1))
                    dve.tensor_tensor(ol[:, k, :], ps[:, bank + k, :], oh[:, k, :].bitcast(F32), ALU.subtract) \
                        .then_inc(S["o_lo"], 1)

            def mask_state(b):
                dve.wait_ge(S["c_state"], b + 1)
                for m in range(KC):
                    last = dve.scalar_tensor_tensor(state[:, m, :], ps[:, O0, m * 2 * P:(m * 2 + 1) * P], 1.0 / HD,
                                                    mask[:], ALU.mult, ALU.mult)
                last.then_inc(S["c_masked"], 1)
                for m in range(KC):
                    last = dve.scalar_tensor_tensor(state_lo[:, m, :], ps[:, O0, (m * 2 + 1) * P:(m * 2 + 2) * P],
                                                    1.0 / HD, mask[:], ALU.mult, ALU.mult)
                last.then_inc(S["c_masked"], 1)

            def split_state(b):
                dve.wait_ge(S["c_masked"], b * 3 + 2)
                dve.tensor_tensor(state[:], state[:], state_lo[:], ALU.add).then_inc(S["c_masked"], 1)
                dve.wait_ge(S["c_masked"], b * 3 + 3)
                dve.tensor_copy(stateh[:], state[:]).then_inc(S["c_sthi"], 1)
                dve.wait_ge(S["c_sthi"], b + 1)
                dve.tensor_tensor(statel[:], state[:], stateh[:].bitcast(F32), ALU.subtract).then_inc(S["c_stlo"], 1)

            def head_sums(b, half):
                dve.wait_ge(S["c_ocopied"], b * (ST // 2) + (half * 2 + 2))
                dve.tensor_reduce(hsum[:, half * GT * NH:(half + 1) * GT * NH],
                                  sq[:].rearrange("p t (h d) -> p (t h) d", d=HD),
                                  AX_X, ALU.add).then_inc(S["c_hsum"], 1)

            def head_rstd(b, ops):
                guess = hrstd[:].bitcast(I32)
                for k in ops:
                    if k == 0:
                        dve.wait_ge(S["c_hsum"], b * 2 + 2)
                        ins = dve.tensor_scalar(hsum[:], hsum[:], 1.0 / HD, 1e-24, ALU.mult, ALU.max)
                    else:
                        dve.wait_ge(S["c_hrstd"], b * HEAD_OPS + k)
                        if k == 1:
                            ins = dve.tensor_scalar(guess, hsum[:].bitcast(I32), 1, None, ALU.logical_shift_right)
                        elif k == 2:
                            ins = dve.tensor_scalar(guess, guess, -1.0, float(0x5F3759DF), ALU.mult, ALU.add)
                        elif k % 3 == 0:
                            ins = dve.tensor_tensor(hwork[:], hrstd[:], hrstd[:], ALU.mult)
                        elif k % 3 == 1:
                            ins = dve.scalar_tensor_tensor(hwork[:], hwork[:], -0.5, hsum[:], ALU.mult, ALU.mult)
                        else:
                            ins = dve.scalar_tensor_tensor(hrstd[:], hwork[:], 1.5, hrstd[:], ALU.add, ALU.mult)
                    ins.then_inc(S["c_hrstd"], 1)

            def step(b, g, half, seq=None, h=None):
                first = isinstance(g, int) and g == 0
                F = g + (FRONT0["C"] + 1)
                gx = 0 if isinstance(g, int) and g == NG - 1 else g + 1
                if not first:
                    front_stats(F, gx, UPDATE0["C"] + 1 if isinstance(g, int) and g == NG - 1 else UPDATE0["C"])
                rstd = seq is not None and half == 1
                if rstd:
                    head_rstd(seq, range(5, 7))
                kv_lo(g, 0)
                if seq is not None and half == 0:
                    split_state(seq)
                if first:
                    update_stats(2 * NG - 1)
                if rstd:
                    head_rstd(seq, range(7, 8))
                if not first:
                    front_norm(F, gx, between=lambda t: head_rstd(seq, range(8 + t, 9 + t)) if rstd else None)
                if h is not None:
                    gate(h, 1 - half)
                kv_lo(g, 1)
                if not first:
                    front_lo(F, 1 - half)
                kv_lo(g, 2)
                if h is not None:
                    output_lo(h)
                kv_lo(g, 3)
                if first:
                    front_lo(F, 1)
                if seq is not None and half == 0:
                    head_sums(seq, 0)
                if h is not None:
                    update_stats(h + UPDATE0["C"])
                if half == 1:
                    mask_state(b)
                if seq is not None and half == 0:
                    head_sums(seq, 1)
                    head_rstd(seq, range(0, 5))
                if isinstance(g, int) and g == NG - 1:
                    split_state(B - 1)
                q_lo(g, half)

            dve.wait_ge(S["consts"], 64)
            step(0, 0, 0)
            step(0, 1, 1)
            step(1, 2, 0, seq=0)

            def phase_c(b):
                step(b, b * 2 + 1, 1, seq=b - 1, h=b * 2 - 2)
                step(b + 1, b * 2 + 2, 0, seq=b, h=b * 2 - 1)

            sequences(dve, 1, B - 2, phase_c)
            step(B - 1, NG - 1, 1, seq=B - 2, h=NG - 4)

            RC = 9

            def linker(g, k):
                def link(ins):
                    k[0] += 1
                    ins.then_inc(S["r_chain"], 1)
                    dve.wait_ge(S["r_chain"], g * RC + k[0])
                return link

            def pick(g, bank=T0):
                link = linker(g, [0])
                dve.wait_ge(S["r_scores"], g + 1)
                parts = ps[:, bank, 0:GT * 2 * E].rearrange("p (t h e) -> p t h e", h=2, e=E)
                dve.tensor_tensor(score[:], parts[:, :, 0, :], gbs[:].unsqueeze(1).to_broadcast([P, GT, E]), ALU.add) \
                    .then_inc(S["r_scored"], 1)
                dve.wait_ge(S["r_scored"], g * 2 + 1)
                dve.tensor_tensor(score[:], score[:], parts[:, :, 1, :], ALU.add).then_inc(S["r_scored"], 1)
                dve.wait_ge(S["r_scored"], g * 2 + 2)
                apart(dve)
                for t in range(GT):
                    last = dve.max(best[:, t, :], score[:, t, :])
                last.then_inc(S["r_best"], 1)
                dve.wait_ge(S["r_best"], g + 1)
                apart(dve)
                for t in range(GT):
                    last = dve.max_index(besti[:, t, :], best[:, t, :], score[:, t, :])
                last.then_inc(S["r_found"], 1)
                dve.tensor_tensor(gap[:], best[:, :, 1], best[:, :, 0], ALU.subtract).then_inc(S["r_gap"], 1)
                dve.wait_ge(S["r_found"], g + 1)
                link(dve.tensor_copy(bestf[:], besti[:]))
                rows = iota[:].unsqueeze(1).to_broadcast([P, GT, E])
                link(dve.tensor_tensor(pick1[:], rows, bestf[:, :, 0:1].to_broadcast([P, GT, E]), ALU.is_equal))
                link(dve.tensor_tensor(pick2[:], rows, bestf[:, :, 1:2].to_broadcast([P, GT, E]), ALU.is_equal))

            def combine(g):
                k = [3]
                link = linker(g, k)
                dve.wait_ge(S["r_second"], g + 1)
                link(dve.tensor_scalar(denom[:], second[:], 1.0, None, ALU.add))
                link(dve.reciprocal(gate1[:], denom[:]))
                link(dve.tensor_tensor(gate2[:], gate1[:], second[:], ALU.mult))
                link(dve.tensor_tensor(pick1[:], pick1[:], gate1[:].unsqueeze(2).to_broadcast([P, GT, E]), ALU.mult))
                link(dve.tensor_tensor(pick2[:], pick2[:], gate2[:].unsqueeze(2).to_broadcast([P, GT, E]), ALU.mult))
                link(dve.tensor_tensor(pick1[:], pick1[:], pick2[:], ALU.add))
                assert k[0] == RC
                dve.tensor_copy(comb[:, :, 0:E], pick1[:]).then_inc(S["r_comb_hi"], 1)
                dve.wait_ge(S["r_comb_hi"], g + 1)
                dve.tensor_tensor(comb[:, :, E:2 * E], pick1[:], comb[:, :, 0:E].bitcast(F32), ALU.subtract) \
                    .then_inc(S["r_comb"], 1)

            def w1_lo(c):
                dve.wait_ge(S["w1_hi"], c + 1)
                cols = slice(c * P, (c + 1) * P)
                dve.tensor_tensor(w1l[:, :, cols], w1raw[:, :, cols], w1h[:, :, cols].bitcast(F32), ALU.subtract) \
                    .then_inc(S["w1_lo"], 1)

            def w2_lo(c):
                dve.wait_ge(S["w2_hi"], c + 1)
                dve.tensor_tensor(w2l[:, c, :], w2raw[:, c, :], w2h[:, c, :].bitcast(F32), ALU.subtract) \
                    .then_inc(S["w2_lo"], 1)

            dve.wait_ge(S["rt_hi"], 2)
            for lo, raw, hi in ((gwl, gw, gwh), (b2l[:], b2s, b2h[:])):
                dve.tensor_tensor(lo, raw[:], hi.bitcast(F32), ALU.subtract).then_inc(S["rt_lo"], 1)
            dve.tensor_tensor(gbs[:], gb[:, 0, :], gb[:, 1, :], ALU.add).then_inc(S["r_bias"], 1)
            gate(NG - 3, 1)
            head_sums(B - 1, 0)
            front_stats(FRONT0["D"] + 1, 1, UPDATE0["C"] + 2)
            head_sums(B - 1, 1)
            output_lo(NG - 3, G0)
            head_rstd(B - 1, range(0, 3))
            front_norm(FRONT0["D"] + 1, 1, between=lambda t: head_rstd(B - 1, range(3 + t, 4 + t)))
            head_rstd(B - 1, range(3 + GT, HEAD_OPS))
            gate(NG - 2, 0)
            gate(NG - 1, 1)
            update_stats(NG - 3 + UPDATE0["C"], G0)
            front_lo(FRONT0["D"] + 1, 1)
            dve.wait_ge(S["r_bias"], 1)
            dve.wait_ge(S["r_consts"], E + 1)
            pick(0, O0)
            output_lo(NG - 2, G1)
            for c in range(3):
                w1_lo(c)
            combine(0)
            output_lo(NG - 1)
            update_stats(NG - 2 + UPDATE0["C"], G1)
            for c in range(MC):
                w2_lo(c)

            def expert_slot(g, half, c, left, prev):
                late = 1 if prev is None else 0
                if c == 1 and left > 0 and prev is not None:
                    front_lo(g + (FRONT0["D"] + 1), 1 - half)
                if c == 3 + late and left > 0:
                    pick(g + 1)
                if c == 4 + late and left > 0:
                    combine(g + 1)
                if c == 7 and prev is not None:
                    update_stats(prev + UPDATE0["D"])
                if c == 9 and left > 1:
                    front_stats(g + (FRONT0["D"] + 2), g + 2, g + (UPDATE0["C"] + 3))
                if c == 10 and left > 1:
                    front_norm(g + (FRONT0["D"] + 2), g + 2)
                if prev is None and isinstance(g, int) and g == 0 and c + 3 < MC:
                    w1_lo(c + 3)
                if prev is None and isinstance(g, int) and g == 0 and c == 0:
                    update_stats(NG - 1 + UPDATE0["C"])

            run_groups(dve, LEAD["D"], MC, *hidden_layer("D", MC, expert_slot))
            update_stats(NG - 1 + UPDATE0["D"])
            for t in range(GT):
                dve.wait_ge(S["end_normed"], t + 1)
                xt = x[:, NT - GT + t, :]
                dve.tensor_tensor(xt, xt, ry[:, t, :], ALU.add).then_inc(S["end_added"], 1)

        @block.gpsimd
        def _(pool):
            pool.sem_inc(S["dq_w"], CREDIT)
            pool.sem_inc(S["dq_lo"], CREDIT)
            pool.wait_ge(S["half_ready"], 1)

            def front(F):
                pool.wait_ge(S["f_mv"], F + 1)
                pool.wait_ge(S["f_xn"], F)
                apart(pool)
                pool.tensor_scalar(fvar[:], fmv[:, :, 1], EPS, None, ALU.add).then_inc(S["f_var"], 1)
                pool.wait_ge(S["f_var"], F + 1)
                pool.tensor_tensor(frstd[:], fvar[:], neghalf[:, 0:GT], ALU.pow).then_inc(S["f_rstd"], 1)

            def update_rstd(n):
                pool.wait_ge(S["u_mv"], n + 1)
                apart(pool)
                pool.tensor_scalar(uvar[:], umv[:, :, 1], EPS, None, ALU.add).then_inc(S["u_var"], 1)
                pool.tensor_scalar(unm[:], umv[:, :, 0], -1.0, None, ALU.mult).then_inc(S["u_neg"], 1)
                pool.wait_ge(S["u_var"], n + 1)
                pool.tensor_tensor(urstd[:], uvar[:], neghalf[:, 0:GT], ALU.pow).then_inc(S["u_rstd"], 1)
                pool.wait_ge(S["u_neg"], n + 1)
                pool.wait_ge(S["u_rstd"], n + 1)
                pool.tensor_tensor(unm[:], unm[:], urstd[:], ALU.mult).then_inc(S["u_nm"], 1)

            def update_add(n, g, result=ry):
                pool.wait_ge(S["u_normed"], n + 1)
                apart(pool)
                xg = x[:, bass.ds(g * GT, GT), :]
                pool.tensor_tensor(xg, xg, result[:], ALU.add).then_inc(S["u_added"], 1)

            def update(n, g):
                update_rstd(n)
                update_add(n, g)

            def column_rn(b0, b1, done):
                pool.wait_ge(S["col_tot"], done)
                pool.tensor_tensor(colrn[:, b0:b1], coltot[:, b0:b1, 0:4],
                                   neghalf[:, 0:4 * (b1 - b0)].rearrange("p (b s) -> p b s", s=4),
                                   ALU.pow).then_inc(S["col_rn"], 1)

            front(0)
            front(1)

            def phase_a(b, last_b=False):
                for half in range(2):
                    g = b * 2 + half

                    def dequant(s):
                        step = g * 2 + s
                        pool.wait_ge(S["dq_code"], step + 1)
                        pool.wait_ge(sc_loaded[s], g * 16 + 16)
                        pool.wait_ge(S["dq_lo"], CREDIT + step)
                        apart(pool)
                        low = code[:].bitcast(FP8).rearrange("p m (c e) -> p m e c", e=4)
                        for nib in range(2):
                            last = pool.tensor_tensor(weight[:, :, nib, :], low[:, :, nib, :], sc[s][:], ALU.mult)
                        last.then_inc(S["dq_w"], 1)

                    def dequant_lo(s):
                        step = g * 2 + s
                        pool.wait_ge(S["dq_hi"], step + 1)
                        pool.tensor_tensor(wfl[:, bass.ds(step, 1)].rearrange("p o m n c -> p (o m n c)"),
                                           weight[:].rearrange("p m n c -> p (m n c)"),
                                           wfh[:, bass.ds(step, 1)].bitcast(F32).rearrange("p o m n c -> p (o m n c)"),
                                           ALU.subtract).then_inc(S["dq_lo"], 1)

                    dequant(0)
                    if last_b and half == 0:
                        column_rn(0, 1, 1)
                    dequant_lo(0)
                    if last_b and half == 0:
                        update_rstd(0)
                    dequant(1)
                    if last_b and half == 0:
                        update_add(0, 0, ry_first)
                    if not (last_b and half == 1):
                        front(g + 2)
                    dequant_lo(1)

            sequences(pool, 0, B - 2, phase_a)
            phase_a(B - 1, last_b=True)
            column_rn(1, B, 2)

            def phase_b(b, last_b=False):
                for half in range(2):
                    g = b * 2 + half
                    last_g = last_b and half == 1
                    if not last_g:
                        update(g * 2 + 1, g + 1)
                    front(g + (FRONT0["B"] + 1))
                    if last_g:
                        front(FRONT0["C"] + 1)
                    update(2 * NG - 1 if last_g else g * 2 + 2, g)

            sequences(pool, 0, B - 2, phase_b)
            phase_b(B - 1, last_b=True)

            pool.wait_ge(S["wc_lo"], 2)
            for e in range(E):
                pool.memset(iota[:, e:e + 1], float(e)).then_inc(S["r_consts"], 1)
            pool.memset(ebase[:], E_BASE).then_inc(S["r_consts"], 1)

            def gate(h, half):
                o = obuf[:, half * GT:(half + 1) * GT, :]
                pool.wait_ge(S["c_scaled"], h + 1)
                apart(pool)
                pool.tensor_tensor(o, o, us[:, bass.ds(h * GT, GT), :], ALU.mult).then_inc(S["c_gated"], 1)

            def step(g, h, half):
                front(g + (FRONT0["C"] + 1))
                if not (isinstance(h, int) and h == 0):
                    update_add(h + (UPDATE0["C"] - 1), h - 1)
                gate(h, half)
                update_rstd(h + UPDATE0["C"])

            front(FRONT0["C"] + 2)
            front(FRONT0["C"] + 3)

            step(3, 0, 0)

            def phase_c(b):
                step(b * 2 + 2, b * 2 - 1, 1)
                step(b * 2 + 3, b * 2, 0)

            sequences(pool, 1, B - 2, phase_c)

            def second_gate(g):
                pool.wait_ge(S["r_gap"], g + 1)
                pool.tensor_tensor(second[:], ebase[:], gap[:], ALU.pow).then_inc(S["r_second"], 1)

            pool.wait_ge(S["r_consts"], E + 1)
            update_add(UPDATE0["C"] + NG - 4, NG - 4)
            gate(NG - 3, 1)
            front(FRONT0["D"] + 1)
            gate(NG - 2, 0)
            gate(NG - 1, 1)
            update_rstd(UPDATE0["C"] + NG - 3)
            second_gate(0)
            update_add(UPDATE0["C"] + NG - 3, NG - 3)
            update(UPDATE0["C"] + NG - 2, NG - 2)
            update(UPDATE0["C"] + NG - 1, NG - 1)
            second_gate(1)

            def phase_d(b, last_b=False):
                for half in range(2):
                    g = b * 2 + half
                    if not last_b:
                        front(g + (FRONT0["D"] + 2))
                        second_gate(g + 2)
                    if last_b and half == 1:
                        update_rstd(g + UPDATE0["D"])
                    else:
                        update(g + UPDATE0["D"], g)

            sequences(pool, 0, B - 2, phase_d)
            phase_d(B - 1, last_b=True)


def kernel(L0_attn_x, L0_attn_W, L0_attn_b, L0_ffn_gate_W_packed, L0_ffn_gate_scales, L0_ffn_up_W_packed,
           L0_ffn_up_scales, L0_ffn_down_W_packed, L0_ffn_down_scales, L1_attn_Wq, L1_attn_Wk, L1_attn_Wv, L1_attn_Wu,
           L1_attn_Wo, L1_ffn_gate_w, L1_ffn_gate_b, L1_ffn_bias, L1_ffn_w1, L1_ffn_b1, L1_ffn_w2, L1_ffn_b2):
    import numpy as np
    import concourse.bacc as bacc
    from concourse.bass_utils import run_bass_kernel_spmd

    a = np.asarray

    def in_rows(w):
        return a(w).reshape(P, KC, -1)

    def pack_in(w, t):
        return a(w).reshape(FC // 2, P, 2, t).transpose(0, 2, 3, 1).reshape(FC, t, P)

    def pack_down(w, t):
        return a(w).reshape(P, KC, FC // 2, t).transpose(2, 1, 3, 0).reshape(FC, t, P)

    packed = np.stack([pack_in(L0_ffn_gate_W_packed, P), pack_in(L0_ffn_up_W_packed, P),
                       pack_down(L0_ffn_down_W_packed, P)], axis=2).reshape(FC, P, 3 * P)
    scales = np.stack([pack_in(L0_ffn_gate_scales, 8), pack_in(L0_ffn_up_scales, 8),
                       pack_down(L0_ffn_down_scales, 8)], axis=2).reshape(FC * 8, 3 * P)
    arrays = {
        "x_in": a(L0_attn_x).reshape(NT, P, P, KC).transpose(0, 1, 3, 2).reshape(NT, P, D),
        "wqkv": a(L0_attn_W).reshape(P, KC, 3, P, KC).transpose(0, 1, 2, 4, 3).reshape(P, KC, 3 * D),
        "bqkv": a(L0_attn_b).reshape(3, P, KC).transpose(1, 0, 2).reshape(P, 6),
        "packed": packed,
        "scales": scales,
        "wl1": np.concatenate([in_rows(w) for w in (L1_attn_Wq, L1_attn_Wk, L1_attn_Wv, L1_attn_Wu)], axis=2),
        "wo": a(L1_attn_Wo).reshape(KC, P, P, KC).transpose(1, 0, 3, 2).reshape(P, KC, D),
        "w1": a(L1_ffn_w1).reshape(MH, P, KC).transpose(1, 2, 0),
        "b1": a(L1_ffn_b1).reshape(MC, P).T,
        "w2": a(L1_ffn_w2).transpose(0, 2, 1).reshape(MC, P, P, KC).transpose(1, 0, 3, 2).reshape(P, MC, D),
        "b2": a(L1_ffn_b2).reshape(E, P, KC).transpose(0, 2, 1).reshape(E, D),
        "gate_w": a(L1_ffn_gate_w).reshape(E, P, KC).transpose(1, 2, 0),
        "gate_b": a(L1_ffn_gate_b),
        "gate_bias": a(L1_ffn_bias),
        "ident_in": np.eye(P, dtype=np.float32),
        "mask_in": np.kron(np.eye(P // HD), np.ones((HD, HD))).astype(np.float32),
        "sel_in": np.tile(np.repeat(np.eye(E), EH, axis=1), (2, 1)).astype(np.float32),
    }
    nc = bacc.Bacc("TRN2", target_bir_lowering=False, num_devices=1)
    arrays = {n: np.ascontiguousarray(v) for n, v in arrays.items()}
    args = [nc.dram_tensor(n, v.shape, mybir.dt.from_np(v.dtype), kind="ExternalInput").ap() for n, v in arrays.items()]
    out = nc.dram_tensor("out", (NT, P, D), F32, kind="ExternalOutput").ap()
    build_program(nc, *args, out)
    r = run_bass_kernel_spmd(nc, [arrays], core_ids=[0])
    got = r.results[0]["out"]
    return got.reshape(B, TOK // B, KC, P).transpose(0, 1, 3, 2).reshape(B, TOK // B, D)
```
